# Optimizing a Trainium2 kernel written in Bass

```python
import numpy as np
import jax
import jax.numpy as jnp

def _softmax(x, axis=-1):
    return jax.nn.softmax(x, axis=axis)

def _gelu(x):
    return jax.nn.gelu(x, approximate=True)

def _silu(x):
    return jax.nn.silu(x)

def _sigmoid(x):
    return jax.nn.sigmoid(x)

def _layernorm(x, axis=-1, eps=1e-05):
    m = jnp.mean(x, axis=axis, keepdims=True)
    v = jnp.var(x, axis=axis, keepdims=True)
    return (x - m) / jnp.sqrt(v + eps)

def _scatter_add(tgt, idx, src, axis=0):
    return tgt.at[idx].add(src)

def _segment_sum(src, seg, n):
    return jax.ops.segment_sum(src, seg, n)
kernel_name = 'mk_sandwich_d1_jaxref_r8_bf4b7a'

def setup_inputs(seed: int=0):
    np.random.seed(seed)
    _w = jnp.asarray

    def _L0_attn_setup():
        import jax, jax.numpy as jnp
        import numpy as np
        DIM = 256
        N_HEADS = 16
        KV_RANK = 64
        NOPE = 128
        ROPE = 64
        VDIM = 128
        QK_HEAD = NOPE + ROPE
        THETA = 10000.0
        EPS = 1e-06
        SCALE = QK_HEAD ** (-0.5)
        NEG_INF = -1e+30

        def precompute_freqs(seq_len, head_dim, theta=THETA):
            freqs = 1.0 / theta ** (np.arange(0, head_dim, 2, dtype=np.float32) / head_dim)
            ang = np.outer(np.arange(seq_len, dtype=np.float32), freqs)
            return (jnp.asarray(np.cos(ang)), jnp.asarray(np.sin(ang)))

        def apply_rope(x, cos, sin):
            x2 = x.reshape(*x.shape[:-1], -1, 2)
            x0, x1 = (x2[..., 0], x2[..., 1])
            c = cos[None, :, None, :]
            s = sin[None, :, None, :]
            r0 = x0 * c - x1 * s
            r1 = x0 * s + x1 * c
            return jnp.stack([r0, r1], axis=-1).reshape(x.shape)

        def rmsnorm(x, w, eps=EPS):
            rms = jnp.sqrt(jnp.mean(x * x, axis=-1, keepdims=True) + eps)
            return x / rms * w
        key = jax.random.key(seed)
        ks = jax.random.split(key, 5)
        B, S = (2, 256)
        sc = lambda n: 1.0 / np.sqrt(n)
        return {'x': jax.random.normal(ks[0], (B, S, DIM), jnp.float32), 'wq': jax.random.normal(ks[1], (N_HEADS * QK_HEAD, DIM), jnp.float32) * sc(DIM), 'wkv_a': jax.random.normal(ks[2], (KV_RANK + ROPE, DIM), jnp.float32) * sc(DIM), 'wkv_b': jax.random.normal(ks[3], (N_HEADS * (NOPE + VDIM), KV_RANK), jnp.float32) * sc(KV_RANK), 'wo': jax.random.normal(ks[4], (DIM, N_HEADS * VDIM), jnp.float32) * sc(N_HEADS * VDIM), 'kv_norm_w': jnp.ones((KV_RANK,), jnp.float32)}
    _L0_attn_in = _L0_attn_setup()

    def _L0_ffn_setup():
        import jax, jax.numpy as jnp
        import numpy as np
        DIM = 256
        HID = 704
        ZERO_POINT = 128.0

        def _qlinear(x, wq, scale):
            W = (wq.astype(jnp.float32) - ZERO_POINT) * scale[:, None]
            return jnp.einsum('bsd,hd->bsh', x, W)
        key = jax.random.key(seed)
        ks = jax.random.split(key, 7)
        B, S = (4, 256)
        sg = jax.random.uniform(ks[1], (HID,)) * (0.02 / np.sqrt(DIM)) + 0.0001
        su = jax.random.uniform(ks[3], (HID,)) * (0.02 / np.sqrt(DIM)) + 0.0001
        sd = jax.random.uniform(ks[5], (DIM,)) * (0.02 / np.sqrt(HID)) + 0.0001
        return {'x': jax.random.normal(ks[0], (B, S, DIM), dtype=jnp.float32), 'wq_gate': jax.random.randint(ks[2], (HID, DIM), 0, 32, dtype=jnp.int32), 's_gate': sg, 'wq_up': jax.random.randint(ks[4], (HID, DIM), 0, 32, dtype=jnp.int32), 's_up': su, 'wq_down': jax.random.randint(ks[6], (DIM, HID), 0, 32, dtype=jnp.int32), 's_down': sd}
    _L0_ffn_in = _L0_ffn_setup()
    _d = {'L0_attn_x': _L0_attn_in['x'], 'L0_attn_wq': _L0_attn_in['wq'], 'L0_attn_wkv_a': _L0_attn_in['wkv_a'], 'L0_attn_wkv_b': _L0_attn_in['wkv_b'], 'L0_attn_wo': _L0_attn_in['wo'], 'L0_attn_kv_norm_w': _L0_attn_in['kv_norm_w'], 'L0_ffn_wq_gate': _L0_ffn_in['wq_gate'], 'L0_ffn_s_gate': _L0_ffn_in['s_gate'], 'L0_ffn_wq_up': _L0_ffn_in['wq_up'], 'L0_ffn_s_up': _L0_ffn_in['s_up'], 'L0_ffn_wq_down': _L0_ffn_in['wq_down'], 'L0_ffn_s_down': _L0_ffn_in['s_down']}
    _x0 = _d['L0_attn_x']
    _d['L0_attn_x'] = jax.random.normal(jax.random.fold_in(jax.random.key(seed), 1), (1, 2048, 256), dtype=_x0.dtype)
    del _x0
    return _d

def reference(L0_attn_x, L0_attn_wq, L0_attn_wkv_a, L0_attn_wkv_b, L0_attn_wo, L0_attn_kv_norm_w, L0_ffn_wq_gate, L0_ffn_s_gate, L0_ffn_wq_up, L0_ffn_s_up, L0_ffn_wq_down, L0_ffn_s_down):

    def _L0_attn_ref(x, wq, wkv_a, wkv_b, wo, kv_norm_w):
        import jax, jax.numpy as jnp
        import numpy as np
        DIM = 256
        N_HEADS = 16
        KV_RANK = 64
        NOPE = 128
        ROPE = 64
        VDIM = 128
        QK_HEAD = NOPE + ROPE
        THETA = 10000.0
        EPS = 1e-06
        SCALE = QK_HEAD ** (-0.5)
        NEG_INF = -1e+30

        def precompute_freqs(seq_len, head_dim, theta=THETA):
            freqs = 1.0 / theta ** (np.arange(0, head_dim, 2, dtype=np.float32) / head_dim)
            ang = np.outer(np.arange(seq_len, dtype=np.float32), freqs)
            return (jnp.asarray(np.cos(ang)), jnp.asarray(np.sin(ang)))

        def apply_rope(x, cos, sin):
            x2 = x.reshape(*x.shape[:-1], -1, 2)
            x0, x1 = (x2[..., 0], x2[..., 1])
            c = cos[None, :, None, :]
            s = sin[None, :, None, :]
            r0 = x0 * c - x1 * s
            r1 = x0 * s + x1 * c
            return jnp.stack([r0, r1], axis=-1).reshape(x.shape)

        def rmsnorm(x, w, eps=EPS):
            rms = jnp.sqrt(jnp.mean(x * x, axis=-1, keepdims=True) + eps)
            return x / rms * w
        B, S, _ = x.shape
        cos, sin = precompute_freqs(S, ROPE)
        q = (x @ wq.T).reshape(B, S, N_HEADS, QK_HEAD)
        q_nope, q_pe = (q[..., :NOPE], q[..., NOPE:])
        q_pe = apply_rope(q_pe, cos, sin)
        kv = x @ wkv_a.T
        kv_lat, k_pe = (kv[..., :KV_RANK], kv[..., KV_RANK:])
        k_pe = apply_rope(k_pe[:, :, None, :], cos, sin)[:, :, 0, :]
        wkv_b_h = wkv_b.reshape(N_HEADS, NOPE + VDIM, KV_RANK)
        q_lat = jnp.einsum('bshd,hdc->bshc', q_nope, wkv_b_h[:, :NOPE])
        kv_cache = rmsnorm(kv_lat, kv_norm_w)
        scores = (jnp.einsum('bshc,btc->bsht', q_lat, kv_cache) + jnp.einsum('bshr,btr->bsht', q_pe, k_pe)) * SCALE
        causal = jnp.tril(jnp.ones((S, S), bool))
        scores = jnp.where(causal[None, :, None, :], scores, NEG_INF)
        attn = jax.nn.softmax(scores, axis=-1)
        out_lat = jnp.einsum('bsht,btc->bshc', attn, kv_cache)
        out = jnp.einsum('bshc,hdc->bshd', out_lat, wkv_b_h[:, NOPE:])
        return out.reshape(B, S, N_HEADS * VDIM) @ wo.T

    def _L0_ffn_ref(x, wq_gate, s_gate, wq_up, s_up, wq_down, s_down):
        import jax, jax.numpy as jnp
        import numpy as np
        DIM = 256
        HID = 704
        ZERO_POINT = 128.0

        def _qlinear(x, wq, scale):
            W = (wq.astype(jnp.float32) - ZERO_POINT) * scale[:, None]
            return jnp.einsum('bsd,hd->bsh', x, W)
        gate = _qlinear(x, wq_gate, s_gate)
        gate = jax.nn.silu(gate)
        up = _qlinear(x, wq_up, s_up)
        return _qlinear(gate * up, wq_down, s_down)
    x = L0_attn_x
    x = x + _layernorm(_L0_attn_ref(_layernorm(x, axis=-1), L0_attn_wq, L0_attn_wkv_a, L0_attn_wkv_b, L0_attn_wo, L0_attn_kv_norm_w), axis=-1)
    x = x + _layernorm(_L0_ffn_ref(_layernorm(x, axis=-1), L0_ffn_wq_gate, L0_ffn_s_gate, L0_ffn_wq_up, L0_ffn_s_up, L0_ffn_wq_down, L0_ffn_s_down), axis=-1)
    return x

_drawn_inputs = setup_inputs


def setup_inputs(seed=0):
    import zlib

    import numpy as np

    out = dict(_drawn_inputs(seed))
    spreads = {'L0_attn_kv_norm_w': (1.0, 0.2)}
    factors = {}
    for name, (base, spread) in spreads.items():
        noise = np.random.default_rng([zlib.crc32(name.encode()), seed]).standard_normal(out[name].shape)
        drawn = base * np.exp(spread * noise) if base else spread * noise
        out[name] = jnp.asarray(drawn.astype(out[name].dtype))
    for name, factor in factors.items():
        out[name] = (out[name] * factor).astype(out[name].dtype)
    return out
```

```python
from contextlib import ExitStack

import numpy as np

import concourse.bass as bass
from concourse import mybir


P = 128
F32 = mybir.dt.float32
F32R = mybir.dt.float32r
F16 = mybir.dt.float16
BF16 = mybir.dt.bfloat16
I32 = mybir.dt.int32
ALU = mybir.AluOpType
ACT = mybir.ActivationFunctionType
AX = mybir.AxisListType

S = 2048
D = 256
KT = D // P
H = 16
NOPE, ROPE, VD, C = 128, 64, 128, 64
QK = NOPE + ROPE
NT = S // P
PAIRS = H // 2
HID = 704
HT = -(-HID // P)
HTAIL = HID - (HT - 1) * P
SCALE = float(QK) ** -0.5
EPS_LN = 1e-5
EPS_RMS = 1e-6
MASKED = -1e30
ZERO_POINT = 128.0
THETA = 10000.0


def plan_attention():
    steps, groups = [], 0
    for i in range(NT):
        n = i + 1
        chunks = [(0, n)] if n <= 8 else [(0, -(-n // 2)), (-(-n // 2), n)]
        for head in range(2):
            for c, (b0, b1) in enumerate(chunks):
                g = []
                for b in range(b0, b1, 4):
                    g.append((groups, b, min(4, b1 - b)))
                    groups += 1
                steps.append(dict(tile=i, head=head, chunk=c, chunks=len(chunks), b0=b0, nb=b1 - b0,
                                  groups=g, diagonal=b1 == n))
    first, last = {}, {}
    for k, s in enumerate(steps):
        first.setdefault(s["tile"], k)
        last[s["tile"]] = k
    n = len(steps)
    side = [[] for _ in steps]
    for j in range(NT // 2):
        side[first[2 * j]].append(("project", j + 2))
        side[first[2 * j] + 3].append(("turn_query", j + 2))
    f5 = first[10]
    side[f5 + 2].append(("absorb", 0))
    side[f5 + 6].append(("turn_wo", 0))
    side[f5 + 9].append(("value_map", 0))
    for i in range(NT):
        side[min(last[i] + 3, n - 1)].append(("turn_out", i))
    finish = [[] for _ in steps]
    for i in range(NT):
        for lag, what in ((0, "least"), (1, "weigh"), (2, "scale")):
            finish[min(last[i] + lag, n - 1)].append((what, i))
    return steps, groups, first, last, side, finish


def build(nc, x, wq, wkv_a, wkv_b, wo, kv_norm_w, wq_gate, s_gate, wq_up, s_up, wq_down, s_down,
          cos_table, sin_table, out):
    steps, GROUPS, first, last, side, finish = plan_attention()
    STEPS = len(steps)
    QG = NT // 2

    ctx = ExitStack()
    with ctx:
        def sem(name):
            return ctx.enter_context(nc.semaphore(name))

        def psum(name, shape):
            return ctx.enter_context(nc.psum_tensor(name, shape, F32))

        def kept(name, shape, dt):
            return ctx.enter_context(nc.sbuf_tensor(name, shape, dt))

        scores = psum("scores", [P, 2, 1024])
        turned = psum("turned", [P, 2, 512])
        latent = psum("latent", [P, 512])
        shared = psum("shared", [P, 512])

        ident = kept("ident", [P, P], F32)
        half = kept("half", [P, 1], F32)
        one = kept("one", [P, 1], F32)
        pause = kept("pause", [P, 1], F32)
        out_T = kept("out_T", [P, PAIRS, S], F32)
        gmap_hi = kept("gmap_hi", [P, PAIRS, D], F32R)
        gmap_lo = kept("gmap_lo", [P, PAIRS, D], F32R)

        early = ExitStack()

        def sb(name, shape, dt):
            return early.enter_context(nc.sbuf_tensor(name, shape, dt))

        ident16 = sb("ident16", [P, P], BF16)
        mask = sb("mask", [P, P], BF16)
        cos_sb = sb("cos_sb", [P, NT, ROPE // 2], F32)
        sin_sb = sb("sin_sb", [P, NT, ROPE // 2], F32)
        wscale = sb("wscale", [P, P], F32)
        wcol = sb("wcol", [P, 1], F32)
        xT_hi = sb("xT_hi", [P, KT, S], F32R)
        xT_lo = sb("xT_lo", [P, KT, S], F32R)
        kT_hi = sb("kT_hi", [P, S], F32R)
        kT_lo = sb("kT_lo", [P, S], F32R)
        v_hi = sb("v_hi", [P, NT, C], F16)
        v_lo = sb("v_lo", [P, NT, C], F16)
        wqn = sb("wqn", [P, 2, D], F32)
        wqr = sb("wqr", [P, D], F32)
        wkb = sb("wkb", [P, 2, C], F32)
        wvb = sb("wvb", [P, 2, P], F32)
        wo_sb = sb("wo_sb", [P, KT, 2, VD], F32)
        wo_T = sb("wo_T", [P, 2, D], F32)
        w_f = sb("w_f", [P, KT, 2, P], F32)
        w_hi = sb("w_hi", [P, KT, 2 * P], F32R)
        w_lo = sb("w_lo", [P, KT, 2 * P], F32R)
        g_f = sb("g_f", [P, D], F32)
        qn = sb("qn", [P, 2, 2, 2, P], F32)
        q_hi = sb("q_hi", [P, 4, 512], F32R)
        q_lo = sb("q_lo", [P, 4, 512], F32R)
        rope_t = sb("rope_t", [P, 4, 2, 2, ROPE // 2], F32)
        prob = sb("prob", [P, 2, 1024], F32)
        probT_hi = sb("probT_hi", [P, 2, 512], F16)
        probT_lo = sb("probT_lo", [P, 2, 512], F16)
        negmax = sb("negmax", [P, 4, 2, 2], F32)
        rowsum = sb("rowsum", [P, 4, 2, 2], F32)
        negall = sb("negall", [P, 4, 2], F32)
        below = sb("below", [P, 4, 2, 2], F32)
        weight = sb("weight", [P, 4, 2, 2], F32)
        wsum = sb("wsum", [P, 4, 2, 2], F32)
        total = sb("total", [P, 4, 2], F32)
        inverse = sb("inverse", [P, 4, 2], F32)
        factor = sb("factor", [P, 4, 2, 2], F32)
        raw_out = sb("raw_out", [P, 4, 4, C], F32)
        part_out = sb("part_out", [P, 4, 4, C], F32)
        norm_out = sb("norm_out", [P, 4, 2, C], F32)
        stats = sb("stats", [P, 4, 6], F32)
        meanvar = sb("meanvar", [P, 4, 2], F32)
        vareps = sb("vareps", [P, 4], F32)
        rstd = sb("rstd", [P, 4], F32)
        wkva_f = sb("wkva_f", [P, D], F32)
        wkva_hi = sb("wkva_hi", [P, KT, P], F32R)
        wkva_lo = sb("wkva_lo", [P, KT, P], F32R)
        x_in = out_T[:, PAIRS - 1, :].rearrange("p (a t d) -> p a t d", a=2, t=4)
        xn = prob[:, :, :].rearrange("p a (t d) -> p (a t) d", d=D)[:, 0:4, :]
        kvT = prob[:, 1, 0:512]
        kv_f = qn[:, 0].rearrange("p a b c -> p (a b) c")
        keys = qn[:, 1].rearrange("p a b c -> p (a b) c")
        square = raw_out[:, 0]
        early.close()

        late = ExitStack()

        def sl(name, shape, dt):
            return late.enter_context(nc.sbuf_tensor(name, shape, dt))

        wg_hi = sl("wg_hi", [P, KT, HID], F32R)
        wg_lo = sl("wg_lo", [P, KT, HID], F32R)
        wu_hi = sl("wu_hi", [P, KT, HID], F32R)
        wu_lo = sl("wu_lo", [P, KT, HID], F32R)
        wd_hi = sl("wd_hi", [P, HT, D], F32R)
        wd_lo = sl("wd_lo", [P, HT, D], F32R)
        w_int = sl("w_int", [P, 2, HID], I32)
        w_flt = sl("w_flt", [P, 2, HID], F32)
        sgate_half = sl("sgate_half", [P, HT], F32)
        sgate = sl("sgate", [P, HT], F32)
        sup_half = sl("sup_half", [P, HT], F32)
        sup = sl("sup", [P, HT], F32)
        sgu = sl("sgu", [P, HT], F32)
        sdown = sl("sdown", [P, D], F32)
        o_hi = sl("o_hi", [P, 4, 512], F32R)
        o_lo = sl("o_lo", [P, 4, 512], F32R)
        x_res = sl("x_res", [P, 4, D], F32)
        att_T = sl("att_T", [P, KT, 512], F32)
        y1 = sl("y1", [P, 4, D], F32)
        z = sl("z", [P, 4, D], F32)
        zT_hi = sl("zT_hi", [P, KT, 512], F32R)
        zT_lo = sl("zT_lo", [P, KT, 512], F32R)
        tanh_g = sl("tanh_g", [P, 2, 512], F32)
        gated = sl("gated", [P, 2, 512], F32)
        h_f = sl("h_f", [P, 2, 512], F32)
        h_hi = sl("h_hi", [P, HT, 512], F32R)
        h_lo = sl("h_lo", [P, HT, 512], F32R)
        result = sl("result", [P, 4, D], F32)
        lstats = sl("lstats", [P, 4, 6], F32)
        lmv = sl("lmv", [P, 4, 2], F32)
        lvar = sl("lvar", [P, 4], F32)
        lrstd = sl("lrstd", [P, 4], F32)
        late.close()

        x_v = x.rearrange("b (g t p) d -> (b g) p t d", t=4, p=P)
        out_v = out.rearrange("b (g t p) d -> (b g) p t d", t=4, p=P)
        wq_v = wq.rearrange("(g t e) d -> g e t d", t=2, e=QK)
        wkvb_v = wkv_b.rearrange("(g t e) c -> g e t c", t=2, e=NOPE + VD)
        wo_v = wo.rearrange("(a p) (g t v) -> g p a t v", p=P, t=2, v=VD)

        names = """const_in table_in x_in_s ident_ok ones_ok pad_ok
            var_ready rstd_ready xn_ready xT_psum xT_hi_ok xT_lo_ok kvT_psum kvT_sb kv_psum kv_sb
            ms_ready rms_ready keys_ok k_psum k_hi_ok k_lo_ok values_ok wkva_psum wkva_hi_ok wkva_lo_ok wscale_ok
            dve_setup pool_setup
            head_w head_v absorbed absorbed_sb w_split wo_turned wo_T_ok gmapped gmap_sb gmap_ok
            projected qn_ok roped q_turned q_hi_ok q_lo_ok
            scored maxed exped turned_p probT_hi_ok probT_lo_ok summed raw_ok
            least_ok below_ok weight_ok total_ok inverse_ok norm_ok out_turned out_T_ok pool_chain
            wint_in0 wint_in1 wflt_ok fw_psum fw_hi_ok fw_lo_ok scales_in scales_ok scales_chain
            xres_in o_hi_ok o_lo_ok o_used att_sb att_back ln_var ln_rstd dve_late z_ready z_psum zT_hi_ok
            zT_lo_ok y1_ok gate_psum tanh_ok gated_ok h_ok h_hi_ok h_lo_ok down_psum ffn_ok result_ok stored result_free""".split()
        s = {n: sem(n) for n in names}
        block = ctx.enter_context(nc.Block())

        @block.sync
        def _(sp):
            sp.dma_start(wkva_f[:, :], wkv_a).then_inc(s["const_in"], 16)
            sp.dma_start(x_in[:, 0], x_v[0]).then_inc(s["x_in_s"], 16)

            def load_key_weights(p):
                sp.dma_start(wqn[:, :, :], wq_v[p, 0:NOPE]).then_inc(s["head_w"], 16)
                sp.dma_start(wqr[0:ROPE, :], wq_v[p, NOPE:QK, 0]).then_inc(s["head_w"], 16)
                sp.dma_start(wqr[ROPE:P, :], wq_v[p, NOPE:QK, 1]).then_inc(s["head_w"], 16)
                sp.dma_start(wkb[:, :, :], wkvb_v[p, 0:NOPE]).then_inc(s["head_w"], 16)

            def load_value_weights(p):
                sp.dma_start(wvb[:, 0, 0:C], wkvb_v[p, NOPE:NOPE + VD, 0]).then_inc(s["head_v"], 16)
                sp.dma_start(wvb[:, 1, C:P], wkvb_v[p, NOPE:NOPE + VD, 1]).then_inc(s["head_v"], 16)
                for a in range(KT):
                    sp.dma_start(wo_sb[:, a], wo_v[p, :, a]).then_inc(s["head_v"], 16)

            load_key_weights(0)
            sp.dma_start(wscale[:, 0:C], kv_norm_w.partition_broadcast(P)).then_inc(s["const_in"], 16)
            for half_ in range(2):
                sp.dma_start(wcol[half_ * C:(half_ + 1) * C, :],
                             kv_norm_w.rearrange("(p a) -> p a", a=1)).then_inc(s["const_in"], 16)
            sp.dma_start(cos_sb[:, :, :], cos_table.rearrange("(t p) f -> p t f", p=P)).then_inc(s["table_in"], 16)
            sp.dma_start(sin_sb[:, :, :], sin_table.rearrange("(t p) f -> p t f", p=P)).then_inc(s["table_in"], 16)
            for g in range(1, 4):
                sp.wait_ge(s["x_in_s"], 16 * g)
                if g >= 2:
                    sp.wait_ge(s["xn_ready"], g - 1)
                sp.dma_start(x_in[:, g % 2], x_v[g]).then_inc(s["x_in_s"], 16)

            sp.wait_ge(s["pad_ok"], 1)
            with sp.Fori(0, PAIRS - 1) as p:
                sp.wait_ge(s["gmapped"], p + 1)
                load_value_weights(p)
                sp.wait_ge(s["absorbed"], p + 1)
                load_key_weights(p + 1)
            sp.wait_ge(s["gmapped"], PAIRS)
            load_value_weights(PAIRS - 1)
            sp.wait_ge(s["absorbed"], PAIRS)
            load_key_weights(PAIRS - 1)

            sp.wait_ge(s["out_T_ok"], PAIRS * NT + 1)
            sp.wait_ge(s["exped"], PAIRS * STEPS + 1)
            sp.wait_ge(s["maxed"], PAIRS * STEPS + 2)
            sp.wait_ge(s["q_lo_ok"], PAIRS * QG + 2)
            sp.wait_ge(s["gmap_ok"], PAIRS)
            sp.wait_ge(s["w_split"], PAIRS + 1)
            for scale, tile in ((s_gate, sgate), (s_up, sup)):
                with nc.allow_non_contiguous_dma(reason="704 scales, once"):
                    sp.dma_start(tile[:, 0:HT - 1], scale[0:(HT - 1) * P].rearrange("(t p) -> p t", p=P))\
                        .then_inc(s["scales_in"], 16)
                sp.dma_start(tile[0:HTAIL, HT - 1:HT], scale[(HT - 1) * P:HID].rearrange("(p a) -> p a", a=1))\
                    .then_inc(s["scales_in"], 16)
            sp.dma_start(sdown[:, :], s_down.partition_broadcast(P)).then_inc(s["scales_in"], 16)
            n = 0
            for w in (wq_gate, wq_up):
                for t0 in (0, 2, 4):
                    for t in (t0, t0 + 1):
                        rows = min(P, HID - t * P)
                        if n >= 4:
                            sp.wait_ge(s["wflt_ok"], n // 2 - 1)
                        sp.dma_start(w_int[0:rows, (n // 2) % 2, (t - t0) * D:(t - t0 + 1) * D],
                                     w[t * P:t * P + rows, :]).then_inc(s[f"wint_in{n // 2 % 2}"], 16)
                        n += 1
            for a in range(KT):
                sp.wait_ge(s["wflt_ok"], n // 2 - 1 + a)
                sp.dma_start(w_int[:, (n // 2 + a) % 2, 0:HID], wq_down[a * P:(a + 1) * P, :])\
                    .then_inc(s[f"wint_in{(n // 2 + a) % 2}"], 16)
            with sp.Fori(0, 4) as c:
                sp.wait_ge(s["y1_ok"], c + 1)
                sp.dma_start(x_res[:, :, :], x_v[c]).then_inc(s["xres_in"], 16)
                sp.wait_ge(s["result_ok"], c + 1)
                sp.dma_start(out_v[c], result[:, :, :]).then_inc(s["stored"], 16)
                sp.wait_ge(s["stored"], 16 * c + 16)
                sp.sem_inc(s["result_free"], 1)

        @block.gpsimd
        def _(pool):
            pool.memset(half[:, :], -0.5).then_inc(s["ones_ok"], 1)
            pool.memset(one[:, :], 1.0).then_inc(s["ones_ok"], 1)
            pool.memset(wscale[:, C:P], 1.0).then_inc(s["ones_ok"], 1)
            pool.memset(wvb[:, :, :], 0.0).then_inc(s["pad_ok"], 1)
            pool.memset(ident[:, :], 0.0).then_inc(s["ident_ok"], 1)
            pool.memset(ident16[:, :], 0.0).then_inc(s["ident_ok"], 1)
            pool.memset(mask[:, :], 0.0).then_inc(s["ident_ok"], 1)
            pool.wait_ge(s["ident_ok"], 3)
            for m in (ident, ident16):
                pool.affine_select(out=m[:, :], in_=m[:, :], compare_op=ALU.not_equal, fill=1.0, base=0,
                                   pattern=[[-1, P]], channel_multiplier=1).then_inc(s["ident_ok"], 1)
            pool.affine_select(out=mask[:, :], in_=mask[:, :], compare_op=ALU.is_ge, fill=MASKED, base=0,
                               pattern=[[-1, P]], channel_multiplier=1).then_inc(s["ident_ok"], 1)

            def power(dst, src):
                return pool.tensor_tensor(dst, src, half[:, 0:1].to_broadcast([P, 4]), ALU.pow)

            def rope(src, cos, sin, shape, link):
                even, odd = src[..., 0:ROPE:2], src[..., 1:ROPE:2]
                t = [rope_t[:, n] if len(shape) == 4 else rope_t[:, n].rearrange("p a b f -> p (a b) f")
                     for n in range(4)]
                pool.tensor_tensor(t[0], even, cos, ALU.mult)
                pool.tensor_tensor(t[1], odd, sin, ALU.mult)
                pool.tensor_tensor(t[2], even, sin, ALU.mult)
                link(pool.tensor_tensor(t[3], odd, cos, ALU.mult))
                pool.tensor_tensor(even, t[0], t[1], ALU.subtract)
                return pool.tensor_tensor(odd, t[2], t[3], ALU.add)

            pool.wait_ge(s["ones_ok"], 3)
            pool.wait_ge(s["table_in"], 32)
            with pool.Fori(0, 4) as g:
                count = [0]

                def link(ins):
                    count[0] += 1
                    ins.then_inc(s["pool_setup"], 1)
                    pool.wait_ge(s["pool_setup"], g * 1 + count[0])

                pool.wait_ge(s["var_ready"], g + 1)
                power(rstd[:, :], vareps[:, :]).then_inc(s["rstd_ready"], 1)
                pool.wait_ge(s["ms_ready"], g + 1)
                power(rstd[:, :], vareps[:, :]).then_inc(s["rms_ready"], 1)
                pool.wait_ge(s["keys_ok"], 2 * g + 1)
                rope(keys[:, :, C:P], cos_sb[:, bass.ds(g * 4, 4), :], sin_sb[:, bass.ds(g * 4, 4), :],
                     [P, 4, 32], link).then_inc(s["keys_ok"], 1)
                assert count[0] == 1

            def split_w(n):
                pool.wait_ge(s["absorbed_sb"], n)
                flat = w_f[:, :, :, :].rearrange("p k t c -> p k (t c)")
                pool.tensor_tensor(w_hi[:, :, :], flat, one[:, 0:1, None].to_broadcast([P, KT, 2 * P]), ALU.mult)\
                    .then_inc(s["pool_chain"], 1)

            def split_w_low():
                flat = w_f[:, :, :, :].rearrange("p k t c -> p k (t c)")
                pool.tensor_tensor(w_lo[:, :, :], flat, w_hi[:, :, :].bitcast(F32), ALU.subtract)\
                    .then_inc(s["w_split"], 1)

            def rope_group(slot, tile0, n, link):
                pool.wait_ge(s["qn_ok"], n)
                cos = cos_sb[:, tile0:tile0 + 2, None, :].to_broadcast([P, 2, 2, ROPE // 2])
                sin = sin_sb[:, tile0:tile0 + 2, None, :].to_broadcast([P, 2, 2, ROPE // 2])
                rope(qn[:, slot, :, :, C:P], cos, sin, [P, 2, 2, 32], link).then_inc(s["roped"], 1)

            LEAD = 1 + 2
            count = [0]

            def first_link(ins):
                count[0] += 1
                if ins is not None:
                    ins.then_inc(s["pool_chain"], 1)
                pool.wait_ge(s["pool_chain"], count[0])

            split_w(1)
            first_link(None)
            split_w_low()
            for j in range(2):
                rope_group(j % 2, 2 * j, j + 1, first_link)
            assert count[0] == LEAD

            with pool.Fori(0, PAIRS) as p:
                PER = 8 + 1 + 1 + 8 + 8 * 4
                count = [0]

                def link(ins):
                    count[0] += 1
                    if ins is not None:
                        ins.then_inc(s["pool_chain"], 1)
                    pool.wait_ge(s["pool_chain"], p * PER + LEAD + count[0])

                for k in range(STEPS):
                    for what, i in side[k]:
                        if what == "project":
                            rope_group(i % 2, 2 * (i % QG), p * QG + i + 1, link)
                        elif what == "absorb":
                            split_w(p + 2)
                            link(None)
                            split_w_low()
                        elif what == "value_map":
                            pool.wait_ge(s["gmap_sb"], p + 1)
                            link(pool.tensor_tensor(gmap_hi[:, p, :], g_f[:, :], one[:, 0:1].to_broadcast([P, D]), ALU.mult))
                            pool.tensor_tensor(gmap_lo[:, p, :], g_f[:, :], gmap_hi[:, p, :].bitcast(F32),
                                               ALU.subtract).then_inc(s["gmap_ok"], 1)
                    for what, i in finish[k]:
                        r = i % 4
                        two = i >= 8
                        if what == "least" and two:
                            pool.wait_ge(s["least_ok"], p * 8 + i - 7)
                            pool.tensor_tensor(below[:, r], negall[:, r, :, None].to_broadcast([P, 2, 2]),
                                               negmax[:, r], ALU.subtract).then_inc(s["below_ok"], 1)
                        elif what == "weigh" and two:
                            pool.wait_ge(s["weight_ok"], p * 8 + i - 7)
                            link(pool.tensor_tensor(wsum[:, r], weight[:, r], rowsum[:, r], ALU.mult))
                            pool.tensor_tensor(total[:, r], wsum[:, r, :, 0], wsum[:, r, :, 1], ALU.add)\
                                .then_inc(s["total_ok"], 1)
                        elif what == "scale":
                            pool.wait_ge(s["inverse_ok"], p * NT + i + 1)
                            pool.wait_ge(s["raw_ok"], p * NT + i + 2)
                            if two:
                                link(pool.tensor_tensor(factor[:, r], weight[:, r],
                                                        inverse[:, r, :, None].to_broadcast([P, 2, 2]), ALU.mult))
                                link(pool.tensor_tensor(
                                    part_out[:, r], raw_out[:, r],
                                    factor[:, r].rearrange("p a b -> p (a b)")[:, :, None].to_broadcast([P, 4, C]),
                                    ALU.mult))
                                pair = part_out[:, r].rearrange("p (a b) c -> p a b c", b=2)
                                link(pool.tensor_tensor(norm_out[:, r], pair[:, :, 0], pair[:, :, 1], ALU.add))
                            else:
                                link(pool.tensor_tensor(norm_out[:, r], raw_out[:, r, 0:2],
                                                        inverse[:, r, :, None].to_broadcast([P, 2, C]), ALU.mult))
                            pool.sem_inc(s["norm_ok"], 1)
                assert count[0] == PER, count

            with pool.Fori(0, 4) as c:
                for n in range(3):
                    pool.wait_ge(s["ln_var"], c * 3 + n + 1)
                    power(lrstd[:, :], lvar[:, :]).then_inc(s["ln_rstd"], 1)

        @block.tensor
        def _(pe):
            def three(dst, w_h, w_l, x_h, x_l, start, stop):
                pe.matmul(dst, w_h, x_h, start=start, stop=False)
                pe.matmul(dst, w_h, x_l, start=False, stop=False)
                return pe.matmul(dst, w_l, x_h, start=False, stop=stop)

            pe.sem_inc(s["gmapped"], 1)
            pe.sem_inc(s["o_used"], 1)
            pe.wait_ge(s["ident_ok"], 6)
            pe.wait_ge(s["const_in"], 64)
            for k in range(KT):
                m = pe.transpose(shared[:, k * P:(k + 1) * P], wkva_f[:, k * P:(k + 1) * P], ident[:, :])
            m.then_inc(s["wkva_psum"], 1)
            pe.wait_ge(s["wkva_lo_ok"], 1)
            xT_ps = scores[:, 0]
            with pe.Fori(0, 4) as g:
                pe.wait_ge(s["xn_ready"], g + 1)
                for k in range(KT):
                    for t in range(4):
                        m = pe.transpose(xT_ps[:, k * 512 + t * P:k * 512 + (t + 1) * P],
                                         xn[:, t, k * P:(k + 1) * P], ident[:, :])
                m.then_inc(s["xT_psum"], 1)
                pe.wait_ge(s["xT_lo_ok"], g + 1)
                for k in range(KT):
                    m = three(shared[:, :], wkva_hi[:, k], wkva_lo[:, k], xT_hi[:, k, bass.ds(g * 512, 512)],
                              xT_lo[:, k, bass.ds(g * 512, 512)], k == 0, k == KT - 1)
                m.then_inc(s["kvT_psum"], 1)
                pe.wait_ge(s["kvT_sb"], g + 1)
                for t in range(4):
                    m = pe.transpose(latent[:, t * P:(t + 1) * P], kvT[:, t * P:(t + 1) * P], ident[:, :])
                m.then_inc(s["kv_psum"], 1)
                pe.wait_ge(s["values_ok"], g + 1)
                pe.wait_ge(s["keys_ok"], 2 * g + 2)
                for t in range(4):
                    m = pe.transpose(turned[:, 0, t * P:(t + 1) * P], keys[:, t, :], ident[:, :])
                m.then_inc(s["k_psum"], 1)
            pe.wait_ge(s["k_lo_ok"], 4)

            def absorb():
                for k in range(KT):
                    for t in range(2):
                        pe.matmul(shared[:, (2 * k + t) * P:(2 * k + t) * P + C], wqn[:, t, k * P:(k + 1) * P],
                                  wkb[:, t, :], start=True, stop=True)
                    rot = shared[:, k * 2 * P:(k + 1) * 2 * P].rearrange("p (t c) -> p t c", t=2)[:, :, C:P]
                    m = pe.transpose(rot, wqr[:, k * P:(k + 1) * P], ident[:, :])
                m.then_inc(s["absorbed"], 1)

            def project(tile0):
                for t in range(2):
                    for k in range(KT):
                        cols = slice((tile0 + t) * P, (tile0 + t + 1) * P)
                        m = three(shared[:, t * 256:(t + 1) * 256], xT_hi[:, k, cols], xT_lo[:, k, cols],
                                  w_hi[:, k], w_lo[:, k], k == 0, k == KT - 1)
                m.then_inc(s["projected"], 1)

            def turn_query(slot):
                for t in range(2):
                    for h in range(2):
                        m = pe.transpose(shared[:, (2 * t + h) * P:(2 * t + h + 1) * P], qn[:, slot, t, h, :],
                                         ident[:, :])
                m.then_inc(s["q_turned"], 1)

            def score(k):
                st = steps[k]
                i = st["tile"]
                q0 = ((i % 2) * 2 + st["head"]) * P
                qh = q_hi[:, (i // 2) % 4, q0:q0 + P]
                ql = q_lo[:, (i // 2) % 4, q0:q0 + P]
                for half_ in range(0, st["nb"], 4):
                    nb = min(4, st["nb"] - half_)
                    wide = max(nb, 2)
                    c0 = (st["b0"] + half_) * P
                    dst = scores[:, k % 2, half_ * P:(half_ + wide) * P]
                    kh, kl = kT_hi[:, c0:c0 + wide * P], kT_lo[:, c0:c0 + wide * P]
                    pe.matmul(dst, qh, kh, start=True, stop=False)
                    if st["diagonal"] and half_ + nb == st["nb"]:
                        d0 = (half_ + nb - 1) * P
                        pe.matmul(scores[:, k % 2, d0:d0 + P], ident16[:, :], mask[:, :], start=False, stop=False)
                    pe.matmul(dst, qh, kl, start=False, stop=False)
                    m = pe.matmul(dst, ql, kh, start=False, stop=True)
                m.then_inc(s["scored"], 1)

            pe.wait_ge(s["head_w"], 64)
            absorb()
            for j in range(2):
                pe.wait_ge(s["absorbed_sb"], 1)
                if j:
                    pe.wait_ge(s["q_lo_ok"], j)
                else:
                    pe.wait_ge(s["w_split"], 1)
                project(2 * j)
                pe.wait_ge(s["roped"], j + 1)
                turn_query(j)
            for k in range(2):
                if k == 0:
                    pe.wait_ge(s["q_lo_ok"], 1)
                score(k)

            with pe.Fori(0, PAIRS) as p:
                reader = [("q_lo_ok", p * QG + 2), ("out_T_ok", p * NT + 1)]

                for k, st in enumerate(steps):
                    pe.wait_ge(s["exped"], p * STEPS + k + 1)
                    for g, b, nb in st["groups"]:
                        for n in range(nb):
                            m = pe.transpose(turned[:, g % 2, n * P:(n + 1) * P],
                                             prob[:, k % 2, (b - st["b0"] + n) * P:(b - st["b0"] + n + 1) * P],
                                             ident[:, :])
                        m.then_inc(s["turned_p"], 1)
                    nk = k + 2
                    if nk % STEPS == first[steps[nk % STEPS]["tile"]] and steps[nk % STEPS]["tile"] % 2 == 0:
                        pe.wait_ge(s["q_lo_ok"], p * QG + steps[nk % STEPS]["tile"] // 2 + 1 + QG * (nk // STEPS))
                    score(nk % STEPS)
                    i = st["tile"]
                    o0 = (st["head"] * st["chunks"] + st["chunk"]) * C
                    if k == first[i]:
                        pe.wait_ge(s["raw_ok"], p * NT + i + 1)
                    for g, b, nb in st["groups"]:
                        pe.wait_ge(s["probT_lo_ok"], p * GROUPS + g + 1)
                        for n in range(nb):
                            f, l = b + n == st["b0"], b + n == st["b0"] + st["nb"] - 1
                            cols = slice(n * P, (n + 1) * P)
                            m = three(latent[:, o0:o0 + C], probT_hi[:, g % 2, cols], probT_lo[:, g % 2, cols],
                                      v_hi[:, b + n, :], v_lo[:, b + n, :], f, l)
                    if k == last[i]:
                        m.then_inc(s["summed"], 1)
                    for what, j in side[k]:
                        for name, value in reader:
                            pe.wait_ge(s[name], value)
                        if what == "project":
                            if j == QG:
                                pe.wait_ge(s["w_split"], p + 2)
                            project(2 * (j % QG))
                            reader = [("qn_ok", p * QG + j + 1)]
                        elif what == "turn_query":
                            pe.wait_ge(s["roped"], p * QG + j + 1)
                            turn_query(j % 2)
                            reader = [("q_lo_ok", p * QG + j + 1)]
                        elif what == "absorb":
                            pe.wait_ge(s["head_w"], p * 64 + 128)
                            absorb()
                            reader = [("absorbed_sb", p + 2)]
                        elif what == "turn_wo":
                            pe.wait_ge(s["head_v"], p * 64 + 64)
                            for h in range(2):
                                for a in range(KT):
                                    m = pe.transpose(shared[:, h * D + a * P:h * D + (a + 1) * P],
                                                     wo_sb[:, a, h, :], ident[:, :])
                            m.then_inc(s["wo_turned"], 1)
                            reader = [("wo_T_ok", p + 1)]
                        elif what == "value_map":
                            for h in range(2):
                                m = pe.matmul(shared[:, 0:D], wvb[:, h, :], wo_T[:, h, :], start=h == 0, stop=h == 1)
                            m.then_inc(s["gmapped"], 1)
                            reader = [("gmap_sb", p + 1)]
                        elif what == "turn_out":
                            pe.wait_ge(s["norm_ok"], p * NT + j + 1)
                            pe.transpose(shared[:, 0:P], norm_out[:, j % 4].rearrange("p a c -> p (a c)"),
                                         ident[:, :]).then_inc(s["out_turned"], 1)
                            reader = [("out_T_ok", p * NT + j + 2)]
                assert reader[0][0] == "out_T_ok"

            pe.wait_ge(s["exped"], PAIRS * STEPS + 1)
            pe.wait_ge(s["maxed"], PAIRS * STEPS + 2)
            n = 0
            for w in range(2):
                for t0 in (0, 2, 4):
                    pe.wait_ge(s["wflt_ok"], w * 3 + t0 // 2 + 1)
                    if n >= 2:
                        pe.wait_ge(s["fw_lo_ok"], n - 1)
                    for t in range(2):
                        rows = min(P, HID - (t0 + t) * P)
                        for k in range(KT):
                            m = pe.transpose(turned[:, n % 2, k * 256 + t * P:k * 256 + t * P + rows],
                                             w_flt[0:rows, n % 2, t * D + k * P:t * D + (k + 1) * P],
                                             ident[0:rows, 0:rows])
                    m.then_inc(s["fw_psum"], 1)
                    n += 1
            pe.wait_ge(s["wflt_ok"], 8)
            for t0 in (0, 2, 4):
                pe.wait_ge(s["fw_lo_ok"], n - 1)
                for t in range(2):
                    cols = min(P, HID - (t0 + t) * P)
                    for a in range(KT):
                        m = pe.transpose(turned[0:cols, n % 2, t * D + a * P:t * D + (a + 1) * P],
                                         w_flt[:, a, (t0 + t) * P:(t0 + t) * P + cols], ident[:, :])
                m.then_inc(s["fw_psum"], 1)
                n += 1
            pe.wait_ge(s["fw_lo_ok"], 9)

            wide0, wide1 = scores[:, 0], scores[:, 1]
            gate_bank = [turned[:, 0], latent[:, :]]
            up_bank = [turned[:, 1], shared[:, :]]
            with pe.Fori(0, 4) as c:
                pe.wait_ge(s["zT_lo_ok"], c + 1)
                for q in range(PAIRS):
                    pe.wait_ge(s["o_lo_ok"], c * PAIRS + q + 1)
                    for a in range(KT):
                        m = three(wide0[:, a * 512:(a + 1) * 512], gmap_hi[:, q, a * P:(a + 1) * P],
                                  gmap_lo[:, q, a * P:(a + 1) * P], o_hi[:, q % 4], o_lo[:, q % 4],
                                  q == 0, q == PAIRS - 1)
                    m.then_inc(s["o_used"], 1)
                pe.wait_ge(s["ffn_ok"], c + 1)
                pe.wait_ge(s["att_sb"], c + 1)
                for t in range(4):
                    for a in range(KT):
                        m = pe.transpose(wide1[:, t * D + a * P:t * D + (a + 1) * P],
                                         att_T[:, a, t * P:(t + 1) * P], ident[:, :])
                m.then_inc(s["att_back"], 1)
                pe.wait_ge(s["z_ready"], c + 1)
                for k in range(KT):
                    for t in range(4):
                        m = pe.transpose(wide0[:, k * 512 + t * P:k * 512 + (t + 1) * P],
                                         z[:, t, k * P:(k + 1) * P], ident[:, :])
                m.then_inc(s["z_psum"], 1)
                pe.wait_ge(s["zT_lo_ok"], c + 2)
                for t in range(HT):
                    rows = min(P, HID - t * P)
                    pe.wait_ge(s["h_ok"], c * HT + max(t, 1))
                    for bank, whi, wlo in ((gate_bank, wg_hi, wg_lo), (up_bank, wu_hi, wu_lo)):
                        for k in range(KT):
                            m = three(bank[t % 2][0:rows, :], whi[:, k, t * P:t * P + rows],
                                      wlo[:, k, t * P:t * P + rows], zT_hi[:, k], zT_lo[:, k],
                                      k == 0, k == KT - 1)
                    m.then_inc(s["gate_psum"], 1)
                pe.wait_ge(s["h_lo_ok"], c * HT + HT)
                for t in range(4):
                    for u in range(HT):
                        rows = min(P, HID - u * P)
                        cols = slice(t * P, (t + 1) * P)
                        m = three(wide1[:, t * D:(t + 1) * D], h_hi[0:rows, u, cols], h_lo[0:rows, u, cols],
                                  wd_hi[0:rows, u], wd_lo[0:rows, u], u == 0, u == HT - 1)
                m.then_inc(s["down_psum"], 1)

        @block.scalar
        def _(act):
            def copy(dst, src, **kw):
                return act.activation(dst, src, ACT.Copy, **kw)

            act.sem_inc(s["raw_ok"], 1)
            act.sem_inc(s["out_T_ok"], 1)
            act.wait_ge(s["wkva_psum"], 1)
            copy(wkva_hi[:, :, :].rearrange("p k c -> p (k c)"), shared[:, 0:2 * P]).then_inc(s["wkva_hi_ok"], 1)
            with act.Fori(0, 4) as g:
                act.wait_ge(s["xT_psum"], g + 1)
                copy(xT_hi[:, :, bass.ds(g * 512, 512)], scores[:, 0].rearrange("p (k s) -> p k s", k=KT))\
                    .then_inc(s["xT_hi_ok"], 1)
                act.wait_ge(s["kvT_psum"], g + 1)
                copy(kvT, shared[:, :]).then_inc(s["kvT_sb"], 1)
                act.wait_ge(s["kv_psum"], g + 1)
                copy(kv_f, latent[:, :].rearrange("p (t c) -> p t c", t=4)).then_inc(s["kv_sb"], 1)
                act.wait_ge(s["k_psum"], g + 1)
                copy(kT_hi[:, bass.ds(g * 512, 512)], turned[:, 0]).then_inc(s["k_hi_ok"], 1)

            def take_queries(slot, n):
                act.wait_ge(s["projected"], n)
                copy(qn[:, slot].rearrange("p a b c -> p (a b c)"), shared[:, :]).then_inc(s["qn_ok"], 1)

            def high_queries(slot, n):
                act.wait_ge(s["q_turned"], n)
                copy(q_hi[:, slot], shared[:, :]).then_inc(s["q_hi_ok"], 1)

            def exponentials(k, n):
                st = steps[k]
                r = st["tile"] % 4
                w = st["nb"] * P
                act.wait_ge(s["maxed"], n)
                act.activation(prob[:, k % 2, 0:w], scores[:, k % 2, 0:w], ACT.Exp,
                               bias=negmax[:, r, st["head"], st["chunk"]:st["chunk"] + 1],
                               accum_out=rowsum[:, r, st["head"], st["chunk"]:st["chunk"] + 1])\
                    .then_inc(s["exped"], 1)

            for j in range(2):
                take_queries(j, j + 1)
                high_queries(j, j + 1)
            exponentials(0, 1)

            with act.Fori(0, PAIRS) as p:
                def take_sums(j):
                    n = 2 if j < 8 else 4
                    act.wait_ge(s["summed"], p * NT + j + 1)
                    copy(raw_out[:, j % 4, 0:n], latent[:, 0:n * C].rearrange("p (a c) -> p a c", c=C))\
                        .then_inc(s["raw_ok"], 1)

                for k, st in enumerate(steps):
                    for g, b, nb in st["groups"]:
                        if k and k == first[st["tile"]] and g == st["groups"][-1][0]:
                            take_sums(st["tile"] - 1)
                        act.wait_ge(s["turned_p"], p * GROUPS + g + 1)
                        copy(probT_hi[:, g % 2, 0:nb * P], turned[:, g % 2, 0:nb * P])\
                            .then_inc(s["probT_hi_ok"], 1)
                    exponentials((k + 1) % STEPS, p * STEPS + k + 2)
                    for what, j in finish[k]:
                        if what != "weigh":
                            continue
                        r = j % 4
                        if j == NT - 1:
                            take_sums(j)
                        if j >= 8:
                            act.wait_ge(s["below_ok"], p * 8 + j - 7)
                            act.activation(weight[:, r].rearrange("p a b -> p (a b)"),
                                           below[:, r].rearrange("p a b -> p (a b)"), ACT.Exp)\
                                .then_inc(s["weight_ok"], 1)
                    for what, j in side[k]:
                        if what == "project":
                            take_queries(j % 2, p * QG + j + 1)
                        elif what == "turn_query":
                            high_queries(j % 4, p * QG + j + 1)
                        elif what == "turn_wo":
                            act.wait_ge(s["wo_turned"], p + 1)
                            copy(wo_T[:, :, :].rearrange("p h n -> p (h n)"), shared[:, :]).then_inc(s["wo_T_ok"], 1)
                        elif what == "value_map":
                            act.wait_ge(s["gmapped"], p + 2)
                            copy(g_f[:, :], shared[:, 0:D], scale=wcol[:, 0:1]).then_inc(s["gmap_sb"], 1)
                        elif what == "turn_out":
                            act.wait_ge(s["out_turned"], p * NT + j + 1)
                            copy(out_T[:, p, j * P:(j + 1) * P], shared[:, 0:P]).then_inc(s["out_T_ok"], 1)

            n = 0
            for hi in (wg_hi, wu_hi):
                for t0 in (0, 2, 4):
                    w = min(2 * P, HID - t0 * P)
                    act.wait_ge(s["fw_psum"], n + 1)
                    copy(hi[:, :, t0 * P:t0 * P + w],
                         turned[:, n % 2].rearrange("p (k c) -> p k c", k=KT)[:, :, 0:w]).then_inc(s["fw_hi_ok"], 1)
                    n += 1
            for t0 in (0, 2, 4):
                act.wait_ge(s["fw_psum"], n + 1)
                for t, rows in ((t0, P), (t0 + 1, min(P, HID - (t0 + 1) * P))):
                    m = copy(wd_hi[0:rows, t], turned[0:rows, n % 2, (t - t0) * D:(t - t0 + 1) * D])
                m.then_inc(s["fw_hi_ok"], 1)
                n += 1
            with act.Fori(0, 4) as c:
                for q in range(PAIRS):
                    act.wait_ge(s["o_used"], c * PAIRS + max(q - 2, 1))
                    copy(o_hi[:, q % 4], out_T[:, q, bass.ds(c * 512, 512)]).then_inc(s["o_hi_ok"], 1)
                act.wait_ge(s["o_used"], (c + 1) * PAIRS + 1)
                copy(att_T[:, :, :].rearrange("p a s -> p (a s)"), scores[:, 0]).then_inc(s["att_sb"], 1)
                act.wait_ge(s["z_psum"], c + 1)
                copy(zT_hi[:, :, :].rearrange("p a s -> p (a s)"), scores[:, 0]).then_inc(s["zT_hi_ok"], 1)
                for t in range(HT):
                    rows = min(P, HID - t * P)
                    bank = [turned[:, 0], latent[:, :]][t % 2]
                    act.wait_ge(s["gate_psum"], c * HT + t + 1)
                    act.activation(tanh_g[0:rows, t % 2], bank[0:rows, :], ACT.Tanh,
                                   scale=sgate_half[0:rows, t:t + 1]).then_inc(s["tanh_ok"], 1)
                    act.wait_ge(s["h_ok"], c * HT + t + 2)
                    copy(h_hi[0:rows, t], h_f[0:rows, t % 2]).then_inc(s["h_hi_ok"], 1)

        @block.vector
        def _(dve):
            for name in ("zT_lo_ok", "ffn_ok", "h_ok", "y1_ok", "result_free"):
                dve.sem_inc(s[name], 1)
            dve.wait_ge(s["wkva_hi_ok"], 1)
            dve.tensor_tensor(wkva_lo[:, :, :].rearrange("p k c -> p (k c)"), shared[:, 0:2 * P],
                              wkva_hi[:, :, :].rearrange("p k c -> p (k c)").bitcast(F32), ALU.subtract)\
                .then_inc(s["wkva_lo_ok"], 1)
            dve.wait_ge(s["const_in"], 64)
            dve.wait_ge(s["ones_ok"], 3)
            dve.tensor_scalar(wscale[:, :], wscale[:, :], SCALE, None, ALU.mult).then_inc(s["wscale_ok"], 1)

            with dve.Fori(0, 4) as g:
                PER = 6
                count = [0]

                def link(ins):
                    count[0] += 1
                    ins.then_inc(s["dve_setup"], 1)
                    dve.wait_ge(s["dve_setup"], g * PER + count[0])

                dve.wait_ge(s["x_in_s"], g * 16 + 16)
                xs = out_T[:, PAIRS - 1, :].rearrange("p (t d) -> p t d", d=D)[:, bass.ds((g % 2) * 4, 4), :]
                for t in range(4):
                    m = dve.bn_stats(stats[:, t, :], xs[:, t, :])
                link(m)
                dve.memset(pause[:, :], 0.0)
                for t in range(4):
                    m = dve.bn_aggr(meanvar[:, t, :], stats[:, t, :])
                link(m)
                dve.tensor_scalar(vareps[:, :], meanvar[:, :, 1], EPS_LN, None, ALU.add).then_inc(s["var_ready"], 1)
                dve.wait_ge(s["rstd_ready"], g + 1)
                for t in range(4):
                    m = dve.tensor_scalar(xn[:, t, :], xs[:, t, :], meanvar[:, t, 0:1], rstd[:, t:t + 1],
                                          ALU.subtract, ALU.mult)
                m.then_inc(s["xn_ready"], 1)
                dve.wait_ge(s["xT_hi_ok"], g + 1)
                dve.tensor_tensor(xT_lo[:, :, bass.ds(g * 512, 512)],
                                  scores[:, 0].rearrange("p (k s) -> p k s", k=KT),
                                  xT_hi[:, :, bass.ds(g * 512, 512)].bitcast(F32), ALU.subtract)\
                    .then_inc(s["xT_lo_ok"], 1)
                dve.wait_ge(s["kv_sb"], g + 1)
                link(dve.tensor_tensor(square[:, :, :], kv_f[:, :, 0:C], kv_f[:, :, 0:C], ALU.mult))
                link(dve.tensor_reduce(vareps[:, :], square[:, :, :], AX.X, ALU.add))
                dve.tensor_scalar(vareps[:, :], vareps[:, :], 1.0 / C, EPS_RMS, ALU.mult, ALU.add)\
                    .then_inc(s["ms_ready"], 1)
                dve.tensor_copy(keys[:, :, C:P], kv_f[:, :, C:P]).then_inc(s["keys_ok"], 1)
                dve.wait_ge(s["rms_ready"], g + 1)
                link(dve.tensor_tensor(keys[:, :, 0:C], kv_f[:, :, 0:C],
                                       rstd[:, :, None].to_broadcast([P, 4, C]), ALU.mult))
                link(dve.tensor_copy(v_hi[:, bass.ds(g * 4, 4), :], keys[:, :, 0:C]))
                dve.tensor_tensor(v_lo[:, bass.ds(g * 4, 4), :], keys[:, :, 0:C],
                                  v_hi[:, bass.ds(g * 4, 4), :], ALU.subtract).then_inc(s["values_ok"], 1)
                dve.wait_ge(s["k_hi_ok"], g + 1)
                dve.tensor_tensor(kT_lo[:, bass.ds(g * 512, 512)], turned[:, 0],
                                  kT_hi[:, bass.ds(g * 512, 512)].bitcast(F32), ALU.subtract)\
                    .then_inc(s["k_lo_ok"], 1)
                assert count[0] == PER

            def take_absorbed(n):
                dve.wait_ge(s["absorbed"], n)
                dve.tensor_tensor(w_f[:, :, :, :].rearrange("p k t c -> p (k t) c"),
                                  shared[:, :].rearrange("p (a c) -> p a c", c=P),
                                  wscale[:, None, :].to_broadcast([P, 2 * KT, P]), ALU.mult)\
                    .then_inc(s["absorbed_sb"], 1)

            def low_queries(slot, n):
                dve.wait_ge(s["q_hi_ok"], n)
                dve.tensor_tensor(q_lo[:, slot], shared[:, :], q_hi[:, slot].bitcast(F32), ALU.subtract)\
                    .then_inc(s["q_lo_ok"], 1)

            def maxima(k, n):
                st = steps[k]
                dve.wait_ge(s["scored"], n)
                dve.tensor_reduce(negmax[:, st["tile"] % 4, st["head"], st["chunk"]:st["chunk"] + 1],
                                  scores[:, k % 2, 0:st["nb"] * P], AX.X, ALU.max, negate=True)\
                    .then_inc(s["maxed"], 1)

            dve.wait_ge(s["wscale_ok"], 1)
            take_absorbed(1)
            for j in range(2):
                low_queries(j, j + 1)
            for k in range(2):
                maxima(k, k + 1)

            with dve.Fori(0, PAIRS) as p:
                for k, st in enumerate(steps):
                    for g, b, nb in st["groups"]:
                        dve.wait_ge(s["probT_hi_ok"], p * GROUPS + g + 1)
                        dve.tensor_tensor(probT_lo[:, g % 2, 0:nb * P], turned[:, g % 2, 0:nb * P],
                                          probT_hi[:, g % 2, 0:nb * P], ALU.subtract).then_inc(s["probT_lo_ok"], 1)
                    maxima((k + 2) % STEPS, p * STEPS + k + 3)
                    for what, j in finish[k]:
                        r = j % 4
                        if what == "least" and j >= 8:
                            dve.wait_ge(s["maxed"], p * STEPS + last[j] + 1)
                            dve.tensor_tensor(negall[:, r], negmax[:, r, :, 0], negmax[:, r, :, 1], ALU.min)\
                                .then_inc(s["least_ok"], 1)
                        elif what == "scale":
                            if j >= 8:
                                dve.wait_ge(s["total_ok"], p * 8 + j - 7)
                                src = total[:, r]
                            else:
                                dve.wait_ge(s["exped"], p * STEPS + last[j] + 1)
                                src = rowsum[:, r, :, 0]
                            dve.reciprocal(inverse[:, r], src).then_inc(s["inverse_ok"], 1)
                    for what, j in side[k]:
                        if what == "turn_query":
                            low_queries(j % 4, p * QG + j + 1)
                        elif what == "absorb":
                            take_absorbed(p + 2)

            dve.wait_ge(s["w_split"], PAIRS + 1)
            dve.wait_ge(s["scales_in"], 80)
            for half_, full in ((sgate_half, sgate), (sup_half, sup)):
                dve.tensor_scalar(half_[:, 0:HT - 1], full[:, 0:HT - 1], 0.5, None, ALU.mult)
                m = dve.tensor_scalar(half_[0:HTAIL, HT - 1:HT], full[0:HTAIL, HT - 1:HT], 0.5, None, ALU.mult)
            m.then_inc(s["scales_chain"], 1)
            dve.wait_ge(s["scales_chain"], 1)
            dve.tensor_tensor(sgu[:, 0:HT - 1], sgate[:, 0:HT - 1], sup_half[:, 0:HT - 1], ALU.mult)
            dve.tensor_tensor(sgu[0:HTAIL, HT - 1:HT], sgate[0:HTAIL, HT - 1:HT], sup_half[0:HTAIL, HT - 1:HT],
                              ALU.mult).then_inc(s["scales_chain"], 1)
            dve.wait_ge(s["scales_chain"], 2)

            def to_float(n, loads, parts):
                dve.wait_ge(s[f"wint_in{n % 2}"], 16 * loads)
                if n >= 2:
                    dve.wait_ge(s["fw_psum"], n - 1)
                for rows, c0, c1 in parts:
                    m = dve.tensor_scalar(w_flt[0:rows, n % 2, c0:c1], w_int[0:rows, n % 2, c0:c1],
                                          -ZERO_POINT, None, ALU.add)
                m.then_inc(s["wflt_ok"], 1)

            def low_up_gate(n):
                w = min(2 * P, HID - (n % 3) * 2 * P)
                lo, hi = ((wg_lo, wg_hi), (wu_lo, wu_hi))[n // 3]
                c0 = (n % 3) * 2 * P
                dve.wait_ge(s["fw_hi_ok"], n + 1)
                dve.tensor_tensor(lo[:, :, c0:c0 + w],
                                  turned[:, n % 2].rearrange("p (k c) -> p k c", k=KT)[:, :, 0:w],
                                  hi[:, :, c0:c0 + w].bitcast(F32), ALU.subtract).then_inc(s["fw_lo_ok"], 1)

            for n in range(6):
                tail = n % 3 == 2
                to_float(n, 2 * (n // 2 + 1), [(P, 0, 2 * D)] if not tail else [(P, 0, D), (HTAIL, D, 2 * D)])
                if n >= 1:
                    low_up_gate(n - 1)
            low_up_gate(5)
            for a in range(KT):
                to_float(6 + a, 7, [(P, 0, HID)])
            for n in range(6, 9):
                t0 = (n - 6) * 2
                dve.wait_ge(s["fw_hi_ok"], n + 1)
                for t in (t0, t0 + 1):
                    rows = min(P, HID - t * P)
                    m = dve.tensor_tensor(wd_lo[0:rows, t], turned[0:rows, n % 2, (t - t0) * D:(t - t0 + 1) * D],
                                          wd_hi[0:rows, t].bitcast(F32), ALU.subtract)
                m.then_inc(s["fw_lo_ok"], 1)

            with dve.Fori(0, 4) as c:
                PER = 3 * 2 + 1 + 1 + 1
                count = [0]

                def chain(ins):
                    count[0] += 1
                    ins.then_inc(s["dve_late"], 1)
                    dve.wait_ge(s["dve_late"], c * PER + count[0])

                def norm(src, dst, which):
                    for t in range(4):
                        m = dve.bn_stats(lstats[:, t, :], src[:, t, :])
                    chain(m)
                    dve.memset(pause[:, :], 0.0)
                    for t in range(4):
                        m = dve.bn_aggr(lmv[:, t, :], lstats[:, t, :])
                    chain(m)
                    dve.tensor_scalar(lvar[:, :], lmv[:, :, 1], EPS_LN, None, ALU.add).then_inc(s["ln_var"], 1)
                    dve.wait_ge(s["ln_rstd"], c * 3 + which + 1)
                    for t in range(4):
                        m = dve.tensor_scalar(dst[:, t, :], src[:, t, :], lmv[:, t, 0:1], lrstd[:, t:t + 1],
                                              ALU.subtract, ALU.mult)
                    return m

                for q in range(PAIRS):
                    dve.wait_ge(s["o_hi_ok"], c * PAIRS + q + 1)
                    dve.tensor_tensor(o_lo[:, q % 4], out_T[:, q, bass.ds(c * 512, 512)],
                                      o_hi[:, q % 4].bitcast(F32), ALU.subtract).then_inc(s["o_lo_ok"], 1)
                dve.wait_ge(s["att_back"], c + 1)
                att = scores[:, 1].rearrange("p (t d) -> p t d", d=D)
                chain(norm(att, z, 0))
                dve.wait_ge(s["xres_in"], 16 * c + 16)
                m = dve.tensor_tensor(y1[:, :, :], z[:, :, :], x_res[:, :, :], ALU.add)
                chain(m)
                dve.sem_inc(s["y1_ok"], 1)
                norm(y1, z, 1).then_inc(s["z_ready"], 1)
                dve.wait_ge(s["zT_hi_ok"], c + 1)
                dve.tensor_tensor(zT_lo[:, :, :].rearrange("p a s -> p (a s)"), scores[:, 0],
                                  zT_hi[:, :, :].rearrange("p a s -> p (a s)").bitcast(F32), ALU.subtract)\
                    .then_inc(s["zT_lo_ok"], 1)

                def low_hidden(t):
                    rows = min(P, HID - t * P)
                    dve.wait_ge(s["h_hi_ok"], c * HT + t + 1)
                    dve.tensor_tensor(h_lo[0:rows, t], h_f[0:rows, t % 2], h_hi[0:rows, t].bitcast(F32),
                                      ALU.subtract).then_inc(s["h_lo_ok"], 1)

                for t in range(HT):
                    rows = min(P, HID - t * P)
                    gate = [turned[:, 0], latent[:, :]][t % 2]
                    up = [turned[:, 1], shared[:, :]][t % 2]
                    dve.wait_ge(s["tanh_ok"], c * HT + t + 1)
                    dve.scalar_tensor_tensor(gated[0:rows, t % 2], tanh_g[0:rows, t % 2], 1.0, gate[0:rows, :],
                                             ALU.add, ALU.mult).then_inc(s["gated_ok"], 1)
                    dve.wait_ge(s["gated_ok"], c * HT + t + 1)
                    dve.scalar_tensor_tensor(h_f[0:rows, t % 2], up[0:rows, :], sgu[0:rows, t:t + 1],
                                             gated[0:rows, t % 2], ALU.mult, ALU.mult).then_inc(s["h_ok"], 1)
                    if t:
                        low_hidden(t - 1)
                low_hidden(HT - 1)
                dve.wait_ge(s["down_psum"], c + 1)
                m = dve.tensor_tensor(z[:, :, :], scores[:, 1].rearrange("p (t d) -> p t d", d=D),
                                      sdown[:, None, :].to_broadcast([P, 4, D]), ALU.mult)
                chain(m)
                dve.sem_inc(s["ffn_ok"], 1)
                norm(z, z, 2).then_inc(s["scales_ok"], 1)
                dve.wait_ge(s["scales_ok"], c + 1)
                dve.wait_ge(s["result_free"], c + 1)
                dve.tensor_tensor(result[:, :, :], z[:, :, :], y1[:, :, :], ALU.add).then_inc(s["result_ok"], 1)
                assert count[0] == PER, count


_INS = ["L0_attn_x", "L0_attn_wq", "L0_attn_wkv_a", "L0_attn_wkv_b", "L0_attn_wo", "L0_attn_kv_norm_w",
        "L0_ffn_wq_gate", "L0_ffn_s_gate", "L0_ffn_wq_up", "L0_ffn_s_up", "L0_ffn_wq_down", "L0_ffn_s_down"]


def kernel(**inputs):
    import concourse.bacc as bacc
    from concourse.bass_utils import run_bass_kernel_spmd

    nc = bacc.Bacc("TRN2", target_bir_lowering=False, num_devices=1)
    arrays = {name: np.ascontiguousarray(inputs[name]) for name in _INS}
    freqs = 1.0 / THETA ** (np.arange(0, ROPE, 2, dtype=np.float32) / ROPE)
    angles = np.outer(np.arange(S, dtype=np.float32), freqs)
    arrays["cos_table"] = np.cos(angles).astype(np.float32)
    arrays["sin_table"] = np.sin(angles).astype(np.float32)
    args = [nc.dram_tensor(name, a.shape, mybir.dt.from_np(a.dtype), kind="ExternalInput").ap()
            for name, a in arrays.items()]
    out = nc.dram_tensor("out", (1, S, D), F32, kind="ExternalOutput").ap()
    build(nc, *args, out)
    r = run_bass_kernel_spmd(nc, [arrays], core_ids=[0])
    return r.results[0]["out"]
```

```python
from contextlib import ExitStack

import numpy as np

import concourse.bass as bass
from concourse import mybir


P = 128
F32 = mybir.dt.float32
F32R = mybir.dt.float32r
F16 = mybir.dt.float16
BF16 = mybir.dt.bfloat16
I32 = mybir.dt.int32
ALU = mybir.AluOpType
ACT = mybir.ActivationFunctionType
AX = mybir.AxisListType

S = 2048
D = 256
KT = D // P
H = 16
NOPE, ROPE, VD, C = 128, 64, 128, 64
QK = NOPE + ROPE
NT = S // P
PAIRS = H // 2
HID = 704
HT = -(-HID // P)
HTAIL = HID - (HT - 1) * P
SCALE = float(QK) ** -0.5
EPS_LN = 1e-5
EPS_RMS = 1e-6
MASKED = -1e30
ZERO_POINT = 128.0
THETA = 10000.0


UNITS = NT // 2


def plan_attention():
    steps, groups = [], 0
    for j in range(UNITS):
        small, big = j, NT - 1 - j
        n = big + 1
        for head in range(2):
            for part, tile, b0, b1 in ((2 * head, big, 0, -(-n // 2)), (4 + head, small, 0, small + 1),
                                       (2 * head + 1, big, -(-n // 2), n)):
                g = []
                for b in range(b0, b1, 4):
                    g.append((groups, b, min(4, b1 - b)))
                    groups += 1
                steps.append(dict(unit=j, head=head, tile=tile, part=part, b0=b0, nb=b1 - b0, groups=g,
                                  diagonal=b1 == tile + 1))
    side = [[] for _ in steps]
    for j in range(UNITS):
        side[6 * j].append(("project", j + 2))
        side[6 * j + 3].append(("turn_out", j - 1))
        side[6 * j + 4].append(("turn_query", j + 2))
    side[6 * 5 + 2].append(("absorb", 0))
    side[6 * 5 + 5].append(("turn_wo", 0))
    side[6 * 6 + 2].append(("value_map", 0))
    finish = [[] for _ in steps]
    for j in range(UNITS):
        for lag, what in ((0, "least"), (1, "weigh"), (2, "scale")):
            finish[min(6 * j + 5 + lag, len(steps) - 1)].append((what, j))
    return steps, groups, side, finish


def build(nc, x, wq, wkv_a, wkv_b, wo, kv_norm_w, wq_gate, s_gate, wq_up, s_up, wq_down, s_down,
          cos_table, sin_table, out):
    steps, GROUPS, side, finish = plan_attention()
    STEPS = len(steps)

    ctx = ExitStack()
    with ctx:
        def sem(name):
            return ctx.enter_context(nc.semaphore(name))

        def psum(name, shape):
            return ctx.enter_context(nc.psum_tensor(name, shape, F32))

        def kept(name, shape, dt):
            return ctx.enter_context(nc.sbuf_tensor(name, shape, dt))

        scores = psum("scores", [P, 2, 1024])
        turned = psum("turned", [P, 2, 512])
        latent = psum("latent", [P, 512])
        shared = psum("shared", [P, 512])

        ident = kept("ident", [P, P], F32)
        half = kept("half", [P, 1], F32)
        one = kept("one", [P, 1], F32)
        pause = kept("pause", [P, 1], F32)
        out_T = kept("out_T", [P, PAIRS, S], F32)
        gmap_hi = kept("gmap_hi", [P, PAIRS, D], F32R)
        gmap_lo = kept("gmap_lo", [P, PAIRS, D], F32R)

        early = ExitStack()

        def sb(name, shape, dt):
            return early.enter_context(nc.sbuf_tensor(name, shape, dt))

        ident16 = sb("ident16", [P, P], BF16)
        mask = sb("mask", [P, P], BF16)
        cos_sb = sb("cos_sb", [P, NT, ROPE // 2], F32)
        sin_sb = sb("sin_sb", [P, NT, ROPE // 2], F32)
        wscale = sb("wscale", [P, P], F32)
        wcol = sb("wcol", [P, 1], F32)
        xT_hi = sb("xT_hi", [P, KT, S], F32R)
        xT_lo = sb("xT_lo", [P, KT, S], F32R)
        kT_hi = sb("kT_hi", [P, S], F32R)
        kT_lo = sb("kT_lo", [P, S], F32R)
        v_hi = sb("v_hi", [P, NT, C], F16)
        v_lo = sb("v_lo", [P, NT, C], F16)
        wqn = sb("wqn", [P, 2, D], F32)
        wqr = sb("wqr", [P, D], F32)
        wkb = sb("wkb", [P, 2, C], F32)
        wvb = sb("wvb", [P, 2, P], F32)
        wo_sb = sb("wo_sb", [P, KT, 2, VD], F32)
        wo_T = sb("wo_T", [P, 2, D], F32)
        w_f = sb("w_f", [P, KT, 2, P], F32)
        w_hi = sb("w_hi", [P, KT, 2 * P], F32R)
        w_lo = sb("w_lo", [P, KT, 2 * P], F32R)
        g_f = sb("g_f", [P, D], F32)
        qn = sb("qn", [P, 2, 2, 2, P], F32)
        q_hi = sb("q_hi", [P, 4, 512], F32R)
        q_lo = sb("q_lo", [P, 4, 512], F32R)
        rope_t = sb("rope_t", [P, 4, 2, 2, ROPE // 2], F32)
        prob = sb("prob", [P, 2, 1024], F32)
        probT_hi = sb("probT_hi", [P, 2, 512], F16)
        probT_lo = sb("probT_lo", [P, 2, 512], F16)
        negmax = sb("negmax", [P, 2, 6], F32)
        rowsum = sb("rowsum", [P, 2, 6], F32)
        negall = sb("negall", [P, 2, 2], F32)
        below = sb("below", [P, 2, 2, 2], F32)
        weight = sb("weight", [P, 2, 2, 2], F32)
        wsum = sb("wsum", [P, 2, 2, 2], F32)
        total = sb("total", [P, 2, 2], F32)
        inverse = sb("inverse", [P, 2, 4], F32)
        factor = sb("factor", [P, 2, 2, 2], F32)
        raw_out = sb("raw_out", [P, 2, 6, C], F32)
        part_out = sb("part_out", [P, 4, C], F32)
        norm_out = sb("norm_out", [P, 2, 2, 2, C], F32)
        stats = sb("stats", [P, 4, 6], F32)
        meanvar = sb("meanvar", [P, 4, 2], F32)
        vareps = sb("vareps", [P, 4], F32)
        rstd = sb("rstd", [P, 4], F32)
        wkva_f = sb("wkva_f", [P, D], F32)
        wkva_hi = sb("wkva_hi", [P, KT, P], F32R)
        wkva_lo = sb("wkva_lo", [P, KT, P], F32R)
        x_in = out_T[:, PAIRS - 1, :].rearrange("p (a t d) -> p a t d", a=2, t=4)
        xn = prob[:, :, :].rearrange("p a (t d) -> p (a t) d", d=D)[:, 0:4, :]
        kvT = prob[:, 1, 0:512]
        kv_f = qn[:, 0].rearrange("p a b c -> p (a b) c")
        keys = qn[:, 1].rearrange("p a b c -> p (a b) c")
        square = raw_out[:, 0, 0:4]
        early.close()

        late = ExitStack()

        def sl(name, shape, dt):
            return late.enter_context(nc.sbuf_tensor(name, shape, dt))

        sdown = sl("sdown", [P, D], F32)
        sgate_half = sl("sgate_half", [P, HT], F32)
        sgate = sl("sgate", [P, HT], F32)
        sup_half = sl("sup_half", [P, HT], F32)
        sup = sl("sup", [P, HT], F32)
        sgu = sl("sgu", [P, HT], F32)
        lstats = sl("lstats", [P, 4, 6], F32)
        lmv = sl("lmv", [P, 4, 2], F32)
        lvar = sl("lvar", [P, 4], F32)
        lrstd = sl("lrstd", [P, 4], F32)
        fstats = sl("fstats", [P, 4, 6], F32)
        fmv = sl("fmv", [P, 4, 2], F32)
        fvar = sl("fvar", [P, 4], F32)
        frstd = sl("frstd", [P, 4], F32)
        o_hi = sl("o_hi", [P, 4, 512], F32R)
        o_lo = sl("o_lo", [P, 4, 512], F32R)
        x_res = sl("x_res", [P, 4, D], F32)
        att_T = sl("att_T", [P, KT, 512], F32)
        y1 = sl("y1", [P, 2 * 4, D], F32)
        z = sl("z", [P, 4, D], F32)
        wg_hi = sl("wg_hi", [P, KT, HID], F32R)
        wg_lo = sl("wg_lo", [P, KT, HID], F32R)
        wu_hi = sl("wu_hi", [P, KT, HID], F32R)
        wu_lo = sl("wu_lo", [P, KT, HID], F32R)
        wd_hi = sl("wd_hi", [P, HT, D], F32R)
        wd_lo = sl("wd_lo", [P, HT, D], F32R)
        zT_hi = sl("zT_hi", [P, KT, 512], F32R)
        zT_lo = sl("zT_lo", [P, KT, 512], F32R)
        with ExitStack() as passing:
            w_int = passing.enter_context(nc.sbuf_tensor("w_int", [P, 2, HID], I32))
            w_flt = passing.enter_context(nc.sbuf_tensor("w_flt", [P, 2, HID], F32))
        h_hi = sl("h_hi", [P, HT, 512], F32R)
        tanh_g = sl("tanh_g", [P, 2, 512], F32)
        gated = sl("gated", [P, 2, 512], F32)
        h_f = sl("h_f", [P, 2, 512], F32)
        h_lo = sl("h_lo", [P, HT, 512], F32R)
        result = sl("result", [P, 4, D], F32)
        out_flat = out_T[:, :, :].rearrange("p q s -> p (q s)")
        late.close()

        x_v = x.rearrange("b (g t p) d -> (b g) p t d", t=4, p=P)
        out_v = out.rearrange("b (g t p) d -> (b g) p t d", t=4, p=P)
        wq_v = wq.rearrange("(g t e) d -> g e t d", t=2, e=QK)
        wkvb_v = wkv_b.rearrange("(g t e) c -> g e t c", t=2, e=NOPE + VD)
        wo_v = wo.rearrange("(a p) (g t v) -> g p a t v", p=P, t=2, v=VD)

        names = """const_in table_in x_in_s ident_ok ones_ok pad_ok
            var_ready rstd_ready xn_ready xT_psum xT_hi_ok xT_lo_ok kvT_psum kvT_sb kv_psum kv_sb
            ms_ready rms_ready keys_ok k_psum k_hi_ok k_lo_ok values_ok wkva_psum wkva_hi_ok wkva_lo_ok wscale_ok
            dve_setup pool_setup
            head_w head_v absorbed absorbed_sb w_split wo_turned wo_T_ok gmapped gmap_sb gmap_ok
            projected qn_ok roped q_turned q_hi_ok q_lo_ok
            scored maxed exped turned_p probT_hi_ok probT_lo_ok summed raw_ok
            least_ok below_ok weight_ok total_ok inverse_ok norm_ok out_turned out_T_ok pool_chain
            wint_in0 wint_in1 wflt_ok fw_psum fw_hi_ok fw_lo_ok scales_in scales_ok scales_chain
            xres_in o_hi_ok o_lo_front o_lo_back o_used att_sb att_back ln_var ln_rstd z1_ok dve_late z_ready z_psum
            zT_hi_ok zT_lo_ok y1_ok gate_psum tanh_ok gated_ok h_ok h_hi_ok h_lo_ok down_psum ffn_ok ffn_var ffn_rstd
            f_done result_ok stored result_free""".split()
        s = {n: sem(n) for n in names}
        block = ctx.enter_context(nc.Block())

        @block.sync
        def _(sp):
            sp.dma_start(wkva_f[:, :], wkv_a).then_inc(s["const_in"], 16)
            sp.dma_start(x_in[:, 0], x_v[0]).then_inc(s["x_in_s"], 16)

            def load_key_weights(p):
                sp.dma_start(wqn[:, :, :], wq_v[p, 0:NOPE]).then_inc(s["head_w"], 16)
                sp.dma_start(wqr[0:ROPE, :], wq_v[p, NOPE:QK, 0]).then_inc(s["head_w"], 16)
                sp.dma_start(wqr[ROPE:P, :], wq_v[p, NOPE:QK, 1]).then_inc(s["head_w"], 16)
                sp.dma_start(wkb[:, :, :], wkvb_v[p, 0:NOPE]).then_inc(s["head_w"], 16)

            def load_value_weights(p):
                sp.dma_start(wvb[:, 0, 0:C], wkvb_v[p, NOPE:NOPE + VD, 0]).then_inc(s["head_v"], 16)
                sp.dma_start(wvb[:, 1, C:P], wkvb_v[p, NOPE:NOPE + VD, 1]).then_inc(s["head_v"], 16)
                for a in range(KT):
                    sp.dma_start(wo_sb[:, a], wo_v[p, :, a]).then_inc(s["head_v"], 16)

            load_key_weights(0)
            sp.dma_start(wscale[:, 0:C], kv_norm_w.partition_broadcast(P)).then_inc(s["const_in"], 16)
            for half_ in range(2):
                sp.dma_start(wcol[half_ * C:(half_ + 1) * C, :],
                             kv_norm_w.rearrange("(p a) -> p a", a=1)).then_inc(s["const_in"], 16)
            sp.dma_start(cos_sb[:, :, :], cos_table.rearrange("(t p) f -> p t f", p=P)).then_inc(s["table_in"], 16)
            sp.dma_start(sin_sb[:, :, :], sin_table.rearrange("(t p) f -> p t f", p=P)).then_inc(s["table_in"], 16)
            for g in range(1, 4):
                sp.wait_ge(s["x_in_s"], 16 * g)
                if g >= 2:
                    sp.wait_ge(s["xn_ready"], g - 1)
                sp.dma_start(x_in[:, g % 2], x_v[g]).then_inc(s["x_in_s"], 16)

            sp.wait_ge(s["pad_ok"], 1)
            with sp.Fori(0, PAIRS - 1) as p:
                sp.wait_ge(s["gmapped"], p + 1)
                load_value_weights(p)
                sp.wait_ge(s["absorbed"], p + 1)
                load_key_weights(p + 1)
            sp.wait_ge(s["gmapped"], PAIRS)
            load_value_weights(PAIRS - 1)
            sp.wait_ge(s["absorbed"], PAIRS)
            load_key_weights(PAIRS - 1)

            sp.wait_ge(s["exped"], PAIRS * STEPS + 1)
            sp.wait_ge(s["maxed"], PAIRS * STEPS + 2)
            sp.wait_ge(s["q_lo_ok"], PAIRS * UNITS + 2)
            sp.wait_ge(s["gmap_ok"], PAIRS)
            sp.wait_ge(s["w_split"], PAIRS + 1)
            sp.dma_start(x_res[:, :, :], x_v[0]).then_inc(s["xres_in"], 16)
            for scale, tile in ((s_gate, sgate), (s_up, sup)):
                with nc.allow_non_contiguous_dma(reason="704 scales, once"):
                    sp.dma_start(tile[:, 0:HT - 1], scale[0:(HT - 1) * P].rearrange("(t p) -> p t", p=P))\
                        .then_inc(s["scales_in"], 16)
                sp.dma_start(tile[0:HTAIL, HT - 1:HT], scale[(HT - 1) * P:HID].rearrange("(p a) -> p a", a=1))\
                    .then_inc(s["scales_in"], 16)
            sp.dma_start(sdown[:, :], s_down.partition_broadcast(P)).then_inc(s["scales_in"], 16)
            n = 0
            for w in (wq_gate, wq_up):
                for t0 in (0, 2, 4):
                    for t in (t0, t0 + 1):
                        rows = min(P, HID - t * P)
                        if n >= 4:
                            sp.wait_ge(s["wflt_ok"], n // 2 - 1)
                        sp.dma_start(w_int[0:rows, (n // 2) % 2, (t - t0) * D:(t - t0 + 1) * D],
                                     w[t * P:t * P + rows, :]).then_inc(s[f"wint_in{n // 2 % 2}"], 16)
                        n += 1
            for a in range(KT):
                sp.wait_ge(s["wflt_ok"], n // 2 - 1 + a)
                sp.dma_start(w_int[:, (n // 2 + a) % 2, 0:HID], wq_down[a * P:(a + 1) * P, :])\
                    .then_inc(s[f"wint_in{(n // 2 + a) % 2}"], 16)

            def store(c):
                for half_ in range(2):
                    sp.wait_ge(s["result_ok"], c * 2 + half_ + 1)
                    sp.dma_start(out_v[c][:, 2 * half_:2 * half_ + 2], result[:, 2 * half_:2 * half_ + 2, :])\
                        .then_inc(s["stored"], 16)
                sp.wait_ge(s["stored"], c * 32 + 32)
                sp.sem_inc(s["result_free"], 1)

            with sp.Fori(0, 3) as c:
                sp.wait_ge(s["y1_ok"], c + 1)
                sp.dma_start(x_res[:, :, :], x_v[c + 1]).then_inc(s["xres_in"], 16)
                store(c)
            store(3)

        @block.gpsimd
        def _(pool):
            pool.memset(half[:, :], -0.5).then_inc(s["ones_ok"], 1)
            pool.memset(one[:, :], 1.0).then_inc(s["ones_ok"], 1)
            pool.memset(wscale[:, C:P], 1.0).then_inc(s["ones_ok"], 1)
            pool.memset(wvb[:, :, :], 0.0).then_inc(s["pad_ok"], 1)
            pool.memset(norm_out[:, :, :, :, :], 0.0).then_inc(s["norm_ok"], 1)
            pool.memset(ident[:, :], 0.0).then_inc(s["ident_ok"], 1)
            pool.memset(ident16[:, :], 0.0).then_inc(s["ident_ok"], 1)
            pool.memset(mask[:, :], 0.0).then_inc(s["ident_ok"], 1)
            pool.wait_ge(s["ident_ok"], 3)
            for m in (ident, ident16):
                pool.affine_select(out=m[:, :], in_=m[:, :], compare_op=ALU.not_equal, fill=1.0, base=0,
                                   pattern=[[-1, P]], channel_multiplier=1).then_inc(s["ident_ok"], 1)
            pool.affine_select(out=mask[:, :], in_=mask[:, :], compare_op=ALU.is_ge, fill=MASKED, base=0,
                               pattern=[[-1, P]], channel_multiplier=1).then_inc(s["ident_ok"], 1)

            def power(dst, src):
                return pool.tensor_tensor(dst, src, half[:, 0:1].to_broadcast([P, 4]), ALU.pow)

            def rope(src, cos, sin, shape, link):
                even, odd = src[..., 0:ROPE:2], src[..., 1:ROPE:2]
                t = [rope_t[:, n] if len(shape) == 4 else rope_t[:, n].rearrange("p a b f -> p (a b) f")
                     for n in range(4)]
                pool.tensor_tensor(t[0], even, cos, ALU.mult)
                pool.tensor_tensor(t[1], odd, sin, ALU.mult)
                pool.tensor_tensor(t[2], even, sin, ALU.mult)
                link(pool.tensor_tensor(t[3], odd, cos, ALU.mult))
                pool.tensor_tensor(even, t[0], t[1], ALU.subtract)
                return pool.tensor_tensor(odd, t[2], t[3], ALU.add)

            pool.wait_ge(s["ones_ok"], 3)
            pool.wait_ge(s["table_in"], 32)
            with pool.Fori(0, 4) as g:
                count = [0]

                def link(ins):
                    count[0] += 1
                    ins.then_inc(s["pool_setup"], 1)
                    pool.wait_ge(s["pool_setup"], g * 1 + count[0])

                pool.wait_ge(s["var_ready"], g + 1)
                power(rstd[:, :], vareps[:, :]).then_inc(s["rstd_ready"], 1)
                pool.wait_ge(s["ms_ready"], g + 1)
                power(rstd[:, :], vareps[:, :]).then_inc(s["rms_ready"], 1)
                pool.wait_ge(s["keys_ok"], 2 * g + 1)
                rope(keys[:, :, C:P], cos_sb[:, bass.ds(g * 4, 4), :], sin_sb[:, bass.ds(g * 4, 4), :],
                     [P, 4, 32], link).then_inc(s["keys_ok"], 1)
                assert count[0] == 1

            def split_w(n):
                pool.wait_ge(s["absorbed_sb"], n)
                flat = w_f[:, :, :, :].rearrange("p k t c -> p k (t c)")
                pool.tensor_tensor(w_hi[:, :, :], flat, one[:, 0:1, None].to_broadcast([P, KT, 2 * P]), ALU.mult)\
                    .then_inc(s["pool_chain"], 1)

            def split_w_low():
                flat = w_f[:, :, :, :].rearrange("p k t c -> p k (t c)")
                pool.tensor_tensor(w_lo[:, :, :], flat, w_hi[:, :, :].bitcast(F32), ALU.subtract)\
                    .then_inc(s["w_split"], 1)

            def rope_group(slot, j, n, link):
                pool.wait_ge(s["qn_ok"], n)
                two = slice(j, NT - j, NT - 1 - 2 * j)
                cos = cos_sb[:, two, None, :].to_broadcast([P, 2, 2, ROPE // 2])
                sin = sin_sb[:, two, None, :].to_broadcast([P, 2, 2, ROPE // 2])
                rope(qn[:, slot, :, :, C:P], cos, sin, [P, 2, 2, 32], link).then_inc(s["roped"], 1)

            LEAD = 1 + 2
            count = [0]

            def first_link(ins):
                count[0] += 1
                if ins is not None:
                    ins.then_inc(s["pool_chain"], 1)
                pool.wait_ge(s["pool_chain"], count[0])

            split_w(1)
            first_link(None)
            split_w_low()
            for j in range(2):
                rope_group(j % 2, j, j + 1, first_link)
            assert count[0] == LEAD

            with pool.Fori(0, PAIRS) as p:
                PER = 8 + 1 + 1 + 8 * 4
                count = [0]

                def link(ins):
                    count[0] += 1
                    if ins is not None:
                        ins.then_inc(s["pool_chain"], 1)
                    pool.wait_ge(s["pool_chain"], p * PER + LEAD + count[0])

                for k in range(STEPS):
                    for what, i in side[k]:
                        if what == "project":
                            rope_group(i % 2, i % UNITS, p * UNITS + i + 1, link)
                        elif what == "absorb":
                            split_w(p + 2)
                            link(None)
                            split_w_low()
                        elif what == "value_map":
                            pool.wait_ge(s["gmap_sb"], p + 1)
                            link(pool.tensor_tensor(gmap_hi[:, p, :], g_f[:, :], one[:, 0:1].to_broadcast([P, D]), ALU.mult))
                            pool.tensor_tensor(gmap_lo[:, p, :], g_f[:, :], gmap_hi[:, p, :].bitcast(F32),
                                               ALU.subtract).then_inc(s["gmap_ok"], 1)
                    for what, j in finish[k]:
                        r = j % 2
                        four = lambda a: a[:, r].rearrange("p a b -> p (a b)")
                        if what == "least":
                            pool.wait_ge(s["least_ok"], p * UNITS + j + 1)
                            pool.tensor_tensor(below[:, r], negall[:, r, :, None].to_broadcast([P, 2, 2]),
                                               negmax[:, r, 0:4].rearrange("p (a b) -> p a b", b=2),
                                               ALU.subtract).then_inc(s["below_ok"], 1)
                        elif what == "weigh":
                            pool.wait_ge(s["weight_ok"], p * UNITS + j + 1)
                            link(pool.tensor_tensor(four(wsum), four(weight), rowsum[:, r, 0:4], ALU.mult))
                            pool.tensor_tensor(total[:, r], wsum[:, r, :, 0], wsum[:, r, :, 1], ALU.add)\
                                .then_inc(s["total_ok"], 1)
                        elif what == "scale":
                            pool.wait_ge(s["inverse_ok"], p * UNITS + j + 1)
                            pool.wait_ge(s["raw_ok"], p * UNITS + j + 2)
                            pool.tensor_tensor(norm_out[:, r, 0], raw_out[:, r, 4:6],
                                               inverse[:, r, 2:4, None].to_broadcast([P, 2, C]), ALU.mult)
                            link(pool.tensor_tensor(factor[:, r], weight[:, r],
                                                    inverse[:, r, 0:2, None].to_broadcast([P, 2, 2]), ALU.mult))
                            link(pool.tensor_tensor(part_out[:, :, :], raw_out[:, r, 0:4],
                                                    four(factor)[:, :, None].to_broadcast([P, 4, C]), ALU.mult))
                            pair = part_out[:, :, :].rearrange("p (a b) c -> p a b c", b=2)
                            link(pool.tensor_tensor(norm_out[:, r, 1], pair[:, :, 0], pair[:, :, 1], ALU.add))
                            pool.sem_inc(s["norm_ok"], 1)
                assert count[0] == PER, count

            def power_of(dst, src, n):
                return pool.tensor_tensor(dst, src, half[:, 0:1].to_broadcast([P, n]), ALU.pow)

            def to_float(n, loads):
                pool.wait_ge(s[f"wint_in{n % 2}"], 16 * loads)
                if n >= 2:
                    pool.wait_ge(s["fw_psum"], n - 1)
                down = n >= 6
                parts = [(P, 0, HID)] if down else [(P, 0, D), (HTAIL, D, 2 * D)] if n % 3 == 2 else [(P, 0, 2 * D)]
                for rows, c0, c1 in parts:
                    m = pool.tensor_scalar(w_flt[0:rows, n % 2, c0:c1], w_int[0:rows, n % 2, c0:c1],
                                           -ZERO_POINT, None, ALU.add)
                m.then_inc(s["wflt_ok"], 1)

            def loads(n):
                return 2 * (n // 2 + 1) if n < 6 else 7

            def norm_root(n):
                pool.wait_ge(s["ln_var"], n + 1)
                power_of(lrstd[:, :], lvar[:, :], 4).then_inc(s["ln_rstd"], 1)

            def add_tokens(c):
                pool.wait_ge(s["z1_ok"], c + 1)
                pool.wait_ge(s["xres_in"], c * 16 + 16)
                slot = c % 2
                pool.tensor_tensor(y1[:, bass.ds(slot * 4, 4), :] if not isinstance(c, int) else
                                   y1[:, slot * 4:slot * 4 + 4, :], z[:, :, :], x_res[:, :, :], ALU.add)\
                    .then_inc(s["y1_ok"], 1)

            def low_hidden(c, t):
                rows = min(P, HID - t * P)
                pool.wait_ge(s["h_hi_ok"], c * HT + t + 1)
                pool.tensor_tensor(h_lo[0:rows, t], h_f[0:rows, t % 2], h_hi[0:rows, t].bitcast(F32),
                                   ALU.subtract).then_inc(s["h_lo_ok"], 1)

            def ffn_roots(c):
                for half_ in range(2):
                    pool.wait_ge(s["ffn_var"], c * 2 + half_ + 1)
                    two = slice(2 * half_, 2 * half_ + 2)
                    power_of(frstd[:, two], fvar[:, two], 2).then_inc(s["ffn_rstd"], 1)

            for n in range(2):
                to_float(n, loads(n))
            norm_root(0)
            to_float(2, loads(2))
            add_tokens(0)
            to_float(3, loads(3))
            norm_root(1)
            for n in range(4, 8):
                to_float(n, loads(n))
            with pool.Fori(0, 3) as c:
                for q in range(4, PAIRS):
                    pool.wait_ge(s["o_hi_ok"], c * PAIRS + PAIRS + q + 1)
                    pool.tensor_tensor(o_lo[:, q % 4], out_T[:, q, bass.ds(c * 512 + 512, 512)],
                                       o_hi[:, q % 4].bitcast(F32), ALU.subtract).then_inc(s["o_lo_back"], 1)
                norm_root(c * 2 + 2)
                low_hidden(c, 0)
                add_tokens(c + 1)
                low_hidden(c, 1)
                low_hidden(c, 2)
                norm_root(c * 2 + 3)
                for t in range(3, HT):
                    low_hidden(c, t)
                ffn_roots(c)
            for t in range(HT):
                low_hidden(3, t)
            ffn_roots(3)

        @block.tensor
        def _(pe):
            def three(dst, w_h, w_l, x_h, x_l, start, stop):
                pe.matmul(dst, w_h, x_h, start=start, stop=False)
                pe.matmul(dst, w_h, x_l, start=False, stop=False)
                return pe.matmul(dst, w_l, x_h, start=False, stop=stop)

            pe.sem_inc(s["gmapped"], 1)
            pe.sem_inc(s["o_used"], 1)
            pe.wait_ge(s["ident_ok"], 6)
            pe.wait_ge(s["const_in"], 64)
            for k in range(KT):
                m = pe.transpose(shared[:, k * P:(k + 1) * P], wkva_f[:, k * P:(k + 1) * P], ident[:, :])
            m.then_inc(s["wkva_psum"], 1)
            pe.wait_ge(s["wkva_lo_ok"], 1)
            xT_ps = scores[:, 0]
            with pe.Fori(0, 4) as g:
                pe.wait_ge(s["xn_ready"], g + 1)
                for k in range(KT):
                    for t in range(4):
                        m = pe.transpose(xT_ps[:, k * 512 + t * P:k * 512 + (t + 1) * P],
                                         xn[:, t, k * P:(k + 1) * P], ident[:, :])
                m.then_inc(s["xT_psum"], 1)
                pe.wait_ge(s["xT_lo_ok"], g + 1)
                for k in range(KT):
                    m = three(shared[:, :], wkva_hi[:, k], wkva_lo[:, k], xT_hi[:, k, bass.ds(g * 512, 512)],
                              xT_lo[:, k, bass.ds(g * 512, 512)], k == 0, k == KT - 1)
                m.then_inc(s["kvT_psum"], 1)
                pe.wait_ge(s["kvT_sb"], g + 1)
                for t in range(4):
                    m = pe.transpose(latent[:, t * P:(t + 1) * P], kvT[:, t * P:(t + 1) * P], ident[:, :])
                m.then_inc(s["kv_psum"], 1)
                pe.wait_ge(s["values_ok"], g + 1)
                pe.wait_ge(s["keys_ok"], 2 * g + 2)
                for t in range(4):
                    m = pe.transpose(turned[:, 0, t * P:(t + 1) * P], keys[:, t, :], ident[:, :])
                m.then_inc(s["k_psum"], 1)
            pe.wait_ge(s["k_lo_ok"], 4)

            def absorb():
                for k in range(KT):
                    for t in range(2):
                        pe.matmul(shared[:, (2 * k + t) * P:(2 * k + t) * P + C], wqn[:, t, k * P:(k + 1) * P],
                                  wkb[:, t, :], start=True, stop=True)
                    rot = shared[:, k * 2 * P:(k + 1) * 2 * P].rearrange("p (t c) -> p t c", t=2)[:, :, C:P]
                    m = pe.transpose(rot, wqr[:, k * P:(k + 1) * P], ident[:, :])
                m.then_inc(s["absorbed"], 1)

            def project(j):
                for t, tile in enumerate((j, NT - 1 - j)):
                    for k in range(KT):
                        cols = slice(tile * P, (tile + 1) * P)
                        m = three(shared[:, t * 256:(t + 1) * 256], xT_hi[:, k, cols], xT_lo[:, k, cols],
                                  w_hi[:, k], w_lo[:, k], k == 0, k == KT - 1)
                m.then_inc(s["projected"], 1)

            def turn_query(slot):
                for t in range(2):
                    for h in range(2):
                        m = pe.transpose(shared[:, (2 * t + h) * P:(2 * t + h + 1) * P], qn[:, slot, t, h, :],
                                         ident[:, :])
                m.then_inc(s["q_turned"], 1)

            def score(k, half_, done):
                st = steps[k]
                q0 = ((0 if st["part"] >= 4 else 2) + st["head"]) * P
                qh = q_hi[:, st["unit"] % 4, q0:q0 + P]
                ql = q_lo[:, st["unit"] % 4, q0:q0 + P]
                nb = min(4, st["nb"] - half_)
                wide = max(nb, 2)
                c0 = (st["b0"] + half_) * P
                dst = scores[:, k % 2, half_ * P:(half_ + wide) * P]
                kh, kl = kT_hi[:, c0:c0 + wide * P], kT_lo[:, c0:c0 + wide * P]
                pe.matmul(dst, qh, kh, start=True, stop=False)
                if st["diagonal"] and half_ + nb == st["nb"]:
                    d0 = (half_ + nb - 1) * P
                    pe.matmul(scores[:, k % 2, d0:d0 + P], ident16[:, :], mask[:, :], start=False, stop=False)
                pe.matmul(dst, qh, kl, start=False, stop=False)
                m = pe.matmul(dst, ql, kh, start=False, stop=True)
                if done:
                    m.then_inc(s["scored"], 1)

            def turn_out(j, n):
                pe.wait_ge(s["norm_ok"], n)
                for t in range(2):
                    m = pe.transpose(shared[:, t * P:(t + 1) * P],
                                     norm_out[:, j % 2, t].rearrange("p a c -> p (a c)"), ident[:, :])
                m.then_inc(s["out_turned"], 1)

            pe.wait_ge(s["head_w"], 64)
            absorb()
            for j in range(2):
                pe.wait_ge(s["absorbed_sb"], 1)
                if j:
                    pe.wait_ge(s["q_lo_ok"], j)
                else:
                    pe.wait_ge(s["w_split"], 1)
                project(j)
                pe.wait_ge(s["roped"], j + 1)
                turn_query(j)
            for k in range(2):
                if k == 0:
                    pe.wait_ge(s["q_lo_ok"], 1)
                for half_ in range(0, steps[k]["nb"], 4):
                    score(k, half_, half_ + 4 >= steps[k]["nb"])

            with pe.Fori(0, PAIRS) as p:
                reader = [("q_lo_ok", p * UNITS + 2)]

                def turn(k, group):
                    g, b, nb = group
                    b -= steps[k]["b0"]
                    for n in range(nb):
                        m = pe.transpose(turned[:, g % 2, n * P:(n + 1) * P], prob[:, k % 2, (b + n) * P:(b + n + 1) * P],
                                         ident[:, :])
                    m.then_inc(s["turned_p"], 1)

                def add_values(k, group):
                    st = steps[k]
                    g, b, nb = group
                    if k % 6 == 0 and group is st["groups"][0]:
                        pe.wait_ge(s["raw_ok"], p * UNITS + st["unit"] + 1)
                    pe.wait_ge(s["probT_lo_ok"], p * GROUPS + g + 1)
                    dst = latent[:, st["part"] * C:(st["part"] + 1) * C]
                    for n in range(nb):
                        cols = slice(n * P, (n + 1) * P)
                        m = three(dst, probT_hi[:, g % 2, cols], probT_lo[:, g % 2, cols], v_hi[:, b + n, :],
                                  v_lo[:, b + n, :], b + n == st["b0"], b + n == st["b0"] + st["nb"] - 1)
                    if k % 6 == 5 and group is st["groups"][-1]:
                        m.then_inc(s["summed"], 1)

                waiting = None
                for k, st in enumerate(steps):
                    pe.wait_ge(s["exped"], p * STEPS + k + 1)
                    nk = (k + 2) % STEPS
                    if nk % 6 == 0:
                        ahead = k + 2 == STEPS
                        new_unit = p * UNITS + steps[nk]["unit"] + 1 + UNITS * ahead
                    halves = list(range(0, steps[nk]["nb"], 4))
                    for n, group in enumerate(st["groups"]):
                        turn(k, group)
                        last_group = n == len(st["groups"]) - 1
                        now = halves if last_group else halves[:-1][:1]
                        halves = halves[len(now):]
                        for half_ in now:
                            if nk % 6 == 0 and half_ == 0:
                                pe.wait_ge(s["q_lo_ok"], new_unit)
                            score(nk, half_, half_ + 4 >= steps[nk]["nb"])
                        if waiting:
                            add_values(*waiting)
                        waiting = (k, group)
                    if k == STEPS - 1:
                        add_values(*waiting)
                    for what, j in side[k]:
                        for name, value in reader:
                            pe.wait_ge(s[name], value)
                        if what == "project":
                            if j == UNITS:
                                pe.wait_ge(s["w_split"], p + 2)
                            project(j % UNITS)
                            reader = [("qn_ok", p * UNITS + j + 1)]
                        elif what == "turn_query":
                            pe.wait_ge(s["roped"], p * UNITS + j + 1)
                            turn_query(j % 2)
                            reader = [("q_lo_ok", p * UNITS + j + 1)]
                        elif what == "absorb":
                            pe.wait_ge(s["head_w"], p * 64 + 128)
                            absorb()
                            reader = [("absorbed_sb", p + 2)]
                        elif what == "turn_wo":
                            pe.wait_ge(s["head_v"], p * 64 + 64)
                            for h in range(2):
                                for a in range(KT):
                                    m = pe.transpose(shared[:, h * D + a * P:h * D + (a + 1) * P],
                                                     wo_sb[:, a, h, :], ident[:, :])
                            m.then_inc(s["wo_turned"], 1)
                            reader = [("wo_T_ok", p + 1)]
                        elif what == "value_map":
                            for h in range(2):
                                m = pe.matmul(shared[:, 0:D], wvb[:, h, :], wo_T[:, h, :], start=h == 0, stop=h == 1)
                            m.then_inc(s["gmapped"], 1)
                            reader = [("gmap_sb", p + 1)]
                        elif what == "turn_out":
                            turn_out(j, p * UNITS + j + 2)
                            reader = [("out_T_ok", p * UNITS + j + 2)]
                assert reader[0][0] == "q_lo_ok"
            pe.wait_ge(s["q_lo_ok"], PAIRS * UNITS + 2)

            wide0, wide1 = scores[:, 0], scores[:, 1]
            gate_bank = [turned[:, 0], latent[:, :]]
            up_bank = [turned[:, 1], shared[:, :]]

            def attend(c):
                for q in range(PAIRS):
                    pe.wait_ge(s["o_lo_front" if q < 4 else "o_lo_back"], c * 4 + q % 4 + 1)
                    for a in range(KT):
                        m = three(wide0[:, a * 512:(a + 1) * 512], gmap_hi[:, q, a * P:(a + 1) * P],
                                  gmap_lo[:, q, a * P:(a + 1) * P], o_hi[:, q % 4], o_lo[:, q % 4],
                                  q == 0, q == PAIRS - 1)
                    m.then_inc(s["o_used"], 1)

            def turn_attended(c):
                pe.wait_ge(s["att_sb"], c + 1)
                for t in range(4):
                    for a in range(KT):
                        m = pe.transpose(wide1[:, t * D + a * P:t * D + (a + 1) * P],
                                         att_T[:, a, t * P:(t + 1) * P], ident[:, :])
                m.then_inc(s["att_back"], 1)

            def turn_tokens(c):
                pe.wait_ge(s["z_ready"], c + 1)
                for k in range(KT):
                    for t in range(4):
                        m = pe.transpose(wide0[:, k * 512 + t * P:k * 512 + (t + 1) * P],
                                         z[:, t, k * P:(k + 1) * P], ident[:, :])
                m.then_inc(s["z_psum"], 1)

            def gates(c):
                for t in range(HT):
                    rows = min(P, HID - t * P)
                    pe.wait_ge(s["h_ok"], c * HT + max(t, 1))
                    for bank, whi, wlo in ((gate_bank, wg_hi, wg_lo), (up_bank, wu_hi, wu_lo)):
                        for k in range(KT):
                            m = three(bank[t % 2][0:rows, :], whi[:, k, t * P:t * P + rows],
                                      wlo[:, k, t * P:t * P + rows], zT_hi[:, k], zT_lo[:, k],
                                      k == 0, k == KT - 1)
                    m.then_inc(s["gate_psum"], 1)

            def down(c):
                pe.wait_ge(s["h_lo_ok"], c * HT + HT)
                for t in range(4):
                    for u in range(HT):
                        rows = min(P, HID - u * P)
                        cols = slice(t * P, (t + 1) * P)
                        m = three(wide1[:, t * D:(t + 1) * D], h_hi[0:rows, u, cols], h_lo[0:rows, u, cols],
                                  wd_hi[0:rows, u], wd_lo[0:rows, u], u == 0, u == HT - 1)
                    if t % 2:
                        m.then_inc(s["down_psum"], 1)

            pe.wait_ge(s["exped"], PAIRS * STEPS + 1)
            pe.wait_ge(s["maxed"], PAIRS * STEPS + 2)
            attend(0)
            turn_out(UNITS - 1, PAIRS * UNITS + 1)
            turn_attended(0)
            n = 0
            for w in range(2):
                for t0 in (0, 2, 4):
                    pe.wait_ge(s["wflt_ok"], w * 3 + t0 // 2 + 1)
                    if n >= 2:
                        pe.wait_ge(s["fw_lo_ok"], n - 1)
                    for t in range(2):
                        rows = min(P, HID - (t0 + t) * P)
                        for k in range(KT):
                            m = pe.transpose(turned[:, n % 2, k * 256 + t * P:k * 256 + t * P + rows],
                                             w_flt[0:rows, n % 2, t * D + k * P:t * D + (k + 1) * P],
                                             ident[0:rows, 0:rows])
                    m.then_inc(s["fw_psum"], 1)
                    n += 1
            turn_tokens(0)
            pe.wait_ge(s["wflt_ok"], 8)
            for t0 in (0, 2, 4):
                pe.wait_ge(s["fw_lo_ok"], n - 1)
                for t in range(2):
                    cols = min(P, HID - (t0 + t) * P)
                    for a in range(KT):
                        m = pe.transpose(turned[0:cols, n % 2, t * D + a * P:t * D + (a + 1) * P],
                                         w_flt[:, a, (t0 + t) * P:(t0 + t) * P + cols], ident[:, :])
                m.then_inc(s["fw_psum"], 1)
                n += 1
            pe.wait_ge(s["fw_lo_ok"], 9)
            pe.wait_ge(s["zT_lo_ok"], 1)
            pe.wait_ge(s["out_T_ok"], PAIRS * UNITS + 1)
            with pe.Fori(0, 3) as c:
                attend(c + 1)
                pe.wait_ge(s["ffn_ok"], c + 1)
                turn_attended(c + 1)
                gates(c)
                turn_tokens(c + 1)
                down(c)
                pe.wait_ge(s["zT_lo_ok"], c + 2)
            gates(3)
            pe.wait_ge(s["ffn_ok"], 4)
            down(3)

        @block.scalar
        def _(act):
            def copy(dst, src, **kw):
                return act.activation(dst, src, ACT.Copy, **kw)

            act.sem_inc(s["raw_ok"], 1)
            act.wait_ge(s["wkva_psum"], 1)
            copy(wkva_hi[:, :, :].rearrange("p k c -> p (k c)"), shared[:, 0:2 * P]).then_inc(s["wkva_hi_ok"], 1)
            with act.Fori(0, 4) as g:
                act.wait_ge(s["xT_psum"], g + 1)
                copy(xT_hi[:, :, bass.ds(g * 512, 512)], scores[:, 0].rearrange("p (k s) -> p k s", k=KT))\
                    .then_inc(s["xT_hi_ok"], 1)
                act.wait_ge(s["kvT_psum"], g + 1)
                copy(kvT, shared[:, :]).then_inc(s["kvT_sb"], 1)
                act.wait_ge(s["kv_psum"], g + 1)
                copy(kv_f, latent[:, :].rearrange("p (t c) -> p t c", t=4)).then_inc(s["kv_sb"], 1)
                act.wait_ge(s["k_psum"], g + 1)
                copy(kT_hi[:, bass.ds(g * 512, 512)], turned[:, 0]).then_inc(s["k_hi_ok"], 1)

            def take_queries(slot, n):
                act.wait_ge(s["projected"], n)
                copy(qn[:, slot].rearrange("p a b c -> p (a b c)"), shared[:, :]).then_inc(s["qn_ok"], 1)

            def high_queries(slot, n):
                act.wait_ge(s["q_turned"], n)
                copy(q_hi[:, slot], shared[:, :]).then_inc(s["q_hi_ok"], 1)

            def exponentials(k, n):
                st = steps[k]
                r, part = st["unit"] % 2, st["part"]
                w = st["nb"] * P
                act.wait_ge(s["maxed"], n)
                act.activation(prob[:, k % 2, 0:w], scores[:, k % 2, 0:w], ACT.Exp,
                               bias=negmax[:, r, part:part + 1], accum_out=rowsum[:, r, part:part + 1])\
                    .then_inc(s["exped"], 1)

            def take_turned(pair, j, n):
                act.wait_ge(s["out_turned"], n)
                dst = out_T[:, pair, :].rearrange("p (t s) -> p t s", s=P)[:, j:NT - j:NT - 1 - 2 * j, :]
                copy(dst, shared[:, 0:2 * P].rearrange("p (t s) -> p t s", s=P)).then_inc(s["out_T_ok"], 1)

            for j in range(2):
                take_queries(j, j + 1)
                high_queries(j, j + 1)
            exponentials(0, 1)

            with act.Fori(0, PAIRS) as p:
                def take_sums(j):
                    act.wait_ge(s["summed"], p * UNITS + j + 1)
                    copy(raw_out[:, j % 2], latent[:, 0:6 * C].rearrange("p (a c) -> p a c", c=C))\
                        .then_inc(s["raw_ok"], 1)

                for k, st in enumerate(steps):
                    for g, b, nb in st["groups"]:
                        if k and k % 6 == 0 and g == st["groups"][-1][0]:
                            take_sums(st["unit"] - 1)
                        act.wait_ge(s["turned_p"], p * GROUPS + g + 1)
                        copy(probT_hi[:, g % 2, 0:nb * P], turned[:, g % 2, 0:nb * P])\
                            .then_inc(s["probT_hi_ok"], 1)
                    exponentials((k + 1) % STEPS, p * STEPS + k + 2)
                    for what, j in finish[k]:
                        if what != "weigh":
                            continue
                        r = j % 2
                        if j == UNITS - 1:
                            take_sums(j)
                        act.wait_ge(s["below_ok"], p * UNITS + j + 1)
                        act.activation(weight[:, r].rearrange("p a b -> p (a b)"),
                                       below[:, r].rearrange("p a b -> p (a b)"), ACT.Exp)\
                            .then_inc(s["weight_ok"], 1)
                    for what, j in side[k]:
                        if what == "project":
                            take_queries(j % 2, p * UNITS + j + 1)
                        elif what == "turn_query":
                            high_queries(j % 4, p * UNITS + j + 1)
                        elif what == "turn_wo":
                            act.wait_ge(s["wo_turned"], p + 1)
                            copy(wo_T[:, :, :].rearrange("p h n -> p (h n)"), shared[:, :]).then_inc(s["wo_T_ok"], 1)
                        elif what == "value_map":
                            act.wait_ge(s["gmapped"], p + 2)
                            copy(g_f[:, :], shared[:, 0:D], scale=wcol[:, 0:1]).then_inc(s["gmap_sb"], 1)
                        elif what == "turn_out":
                            pair = p if j >= 0 else (p + PAIRS - 1) % PAIRS
                            take_turned(pair, j % UNITS, p * UNITS + j + 2)

            def high_out(q, tokens, used):
                act.wait_ge(s["o_used"], used)
                copy(o_hi[:, q % 4], tokens).then_inc(s["o_hi_ok"], 1)

            def take_attended(c):
                act.wait_ge(s["o_used"], c * PAIRS + PAIRS + 1)
                copy(att_T[:, :, :].rearrange("p a s -> p (a s)"), scores[:, 0]).then_inc(s["att_sb"], 1)

            def high_tokens(c):
                act.wait_ge(s["z_psum"], c + 1)
                copy(zT_hi[:, :, :].rearrange("p a s -> p (a s)"), scores[:, 0]).then_inc(s["zT_hi_ok"], 1)

            def gate(c, t):
                rows = min(P, HID - t * P)
                bank = [turned[:, 0], latent[:, :]][t % 2]
                act.wait_ge(s["gate_psum"], c * HT + t + 1)
                act.activation(tanh_g[0:rows, t % 2], bank[0:rows, :], ACT.Tanh,
                               scale=sgate_half[0:rows, t:t + 1]).then_inc(s["tanh_ok"], 1)

            def high_hidden(c, t):
                rows = min(P, HID - t * P)
                act.wait_ge(s["h_ok"], c * HT + t + 2)
                copy(h_hi[0:rows, t], h_f[0:rows, t % 2]).then_inc(s["h_hi_ok"], 1)

            for q in range(PAIRS):
                high_out(q, out_T[:, q, 0:512], max(q - 2, 1))
            take_attended(0)
            take_turned(PAIRS - 1, UNITS - 1, PAIRS * UNITS + 1)
            n = 0
            for hi in (wg_hi, wu_hi):
                for t0 in (0, 2, 4):
                    w = min(2 * P, HID - t0 * P)
                    act.wait_ge(s["fw_psum"], n + 1)
                    copy(hi[:, :, t0 * P:t0 * P + w],
                         turned[:, n % 2].rearrange("p (k c) -> p k c", k=KT)[:, :, 0:w]).then_inc(s["fw_hi_ok"], 1)
                    n += 1
            high_tokens(0)
            for q in range(4):
                high_out(q, out_T[:, q, 512:1024], PAIRS + 1)
            for t0 in (0, 2, 4):
                act.wait_ge(s["fw_psum"], n + 1)
                for t, rows in ((t0, P), (t0 + 1, min(P, HID - (t0 + 1) * P))):
                    m = copy(wd_hi[0:rows, t], turned[0:rows, n % 2, (t - t0) * D:(t - t0 + 1) * D])
                m.then_inc(s["fw_hi_ok"], 1)
                n += 1
            with act.Fori(0, 3) as c:
                for q in range(4, PAIRS):
                    high_out(q, out_T[:, q, bass.ds(c * 512 + 512, 512)], c * PAIRS + PAIRS + q - 2)
                take_attended(c + 1)
                gate(c, 0)
                for t in range(HT):
                    if t + 1 < HT:
                        gate(c, t + 1)
                    high_hidden(c, t)
                high_tokens(c + 1)
                for q in range(4):
                    high_out(q, out_flat[:, bass.ds(c * 512 + (q * S + 1024), 512)], c * PAIRS + 2 * PAIRS + 1)
            gate(3, 0)
            for t in range(HT):
                if t + 1 < HT:
                    gate(3, t + 1)
                high_hidden(3, t)

        @block.vector
        def _(dve):
            for name in ("ffn_ok", "h_ok", "result_free"):
                dve.sem_inc(s[name], 1)
            dve.wait_ge(s["wkva_hi_ok"], 1)
            dve.tensor_tensor(wkva_lo[:, :, :].rearrange("p k c -> p (k c)"), shared[:, 0:2 * P],
                              wkva_hi[:, :, :].rearrange("p k c -> p (k c)").bitcast(F32), ALU.subtract)\
                .then_inc(s["wkva_lo_ok"], 1)
            dve.wait_ge(s["const_in"], 64)
            dve.wait_ge(s["ones_ok"], 3)
            dve.tensor_scalar(wscale[:, :], wscale[:, :], SCALE, None, ALU.mult).then_inc(s["wscale_ok"], 1)

            with dve.Fori(0, 4) as g:
                PER = 6
                count = [0]

                def link(ins):
                    count[0] += 1
                    ins.then_inc(s["dve_setup"], 1)
                    dve.wait_ge(s["dve_setup"], g * PER + count[0])

                dve.wait_ge(s["x_in_s"], g * 16 + 16)
                xs = out_T[:, PAIRS - 1, :].rearrange("p (t d) -> p t d", d=D)[:, bass.ds((g % 2) * 4, 4), :]
                for t in range(4):
                    m = dve.bn_stats(stats[:, t, :], xs[:, t, :])
                link(m)
                dve.memset(pause[:, :], 0.0)
                for t in range(4):
                    m = dve.bn_aggr(meanvar[:, t, :], stats[:, t, :])
                link(m)
                dve.tensor_scalar(vareps[:, :], meanvar[:, :, 1], EPS_LN, None, ALU.add).then_inc(s["var_ready"], 1)
                dve.wait_ge(s["rstd_ready"], g + 1)
                for t in range(4):
                    m = dve.tensor_scalar(xn[:, t, :], xs[:, t, :], meanvar[:, t, 0:1], rstd[:, t:t + 1],
                                          ALU.subtract, ALU.mult)
                m.then_inc(s["xn_ready"], 1)
                dve.wait_ge(s["xT_hi_ok"], g + 1)
                dve.tensor_tensor(xT_lo[:, :, bass.ds(g * 512, 512)],
                                  scores[:, 0].rearrange("p (k s) -> p k s", k=KT),
                                  xT_hi[:, :, bass.ds(g * 512, 512)].bitcast(F32), ALU.subtract)\
                    .then_inc(s["xT_lo_ok"], 1)
                dve.wait_ge(s["kv_sb"], g + 1)
                link(dve.tensor_tensor(square[:, :, :], kv_f[:, :, 0:C], kv_f[:, :, 0:C], ALU.mult))
                link(dve.tensor_reduce(vareps[:, :], square[:, :, :], AX.X, ALU.add))
                dve.tensor_scalar(vareps[:, :], vareps[:, :], 1.0 / C, EPS_RMS, ALU.mult, ALU.add)\
                    .then_inc(s["ms_ready"], 1)
                dve.tensor_copy(keys[:, :, C:P], kv_f[:, :, C:P]).then_inc(s["keys_ok"], 1)
                dve.wait_ge(s["rms_ready"], g + 1)
                link(dve.tensor_tensor(keys[:, :, 0:C], kv_f[:, :, 0:C],
                                       rstd[:, :, None].to_broadcast([P, 4, C]), ALU.mult))
                link(dve.tensor_copy(v_hi[:, bass.ds(g * 4, 4), :], keys[:, :, 0:C]))
                dve.tensor_tensor(v_lo[:, bass.ds(g * 4, 4), :], keys[:, :, 0:C],
                                  v_hi[:, bass.ds(g * 4, 4), :], ALU.subtract).then_inc(s["values_ok"], 1)
                dve.wait_ge(s["k_hi_ok"], g + 1)
                dve.tensor_tensor(kT_lo[:, bass.ds(g * 512, 512)], turned[:, 0],
                                  kT_hi[:, bass.ds(g * 512, 512)].bitcast(F32), ALU.subtract)\
                    .then_inc(s["k_lo_ok"], 1)
                assert count[0] == PER

            def take_absorbed(n):
                dve.wait_ge(s["absorbed"], n)
                dve.tensor_tensor(w_f[:, :, :, :].rearrange("p k t c -> p (k t) c"),
                                  shared[:, :].rearrange("p (a c) -> p a c", c=P),
                                  wscale[:, None, :].to_broadcast([P, 2 * KT, P]), ALU.mult)\
                    .then_inc(s["absorbed_sb"], 1)

            def low_queries(slot, n):
                dve.wait_ge(s["q_hi_ok"], n)
                dve.tensor_tensor(q_lo[:, slot], shared[:, :], q_hi[:, slot].bitcast(F32), ALU.subtract)\
                    .then_inc(s["q_lo_ok"], 1)

            def maxima(k, n):
                st = steps[k]
                dve.wait_ge(s["scored"], n)
                dve.tensor_reduce(negmax[:, st["unit"] % 2, st["part"]:st["part"] + 1],
                                  scores[:, k % 2, 0:st["nb"] * P], AX.X, ALU.max, negate=True)\
                    .then_inc(s["maxed"], 1)

            dve.wait_ge(s["wscale_ok"], 1)
            take_absorbed(1)
            for j in range(2):
                low_queries(j, j + 1)
            for k in range(2):
                maxima(k, k + 1)

            with dve.Fori(0, PAIRS) as p:
                for k, st in enumerate(steps):
                    for g, b, nb in st["groups"]:
                        dve.wait_ge(s["probT_hi_ok"], p * GROUPS + g + 1)
                        dve.tensor_tensor(probT_lo[:, g % 2, 0:nb * P], turned[:, g % 2, 0:nb * P],
                                          probT_hi[:, g % 2, 0:nb * P], ALU.subtract).then_inc(s["probT_lo_ok"], 1)
                    maxima((k + 2) % STEPS, p * STEPS + k + 3)
                    for what, j in finish[k]:
                        r = j % 2
                        if what == "least":
                            dve.wait_ge(s["maxed"], p * STEPS + 6 * j + 6)
                            both = negmax[:, r, 0:4].rearrange("p (a b) -> p a b", b=2)
                            dve.tensor_tensor(negall[:, r], both[:, :, 0], both[:, :, 1], ALU.min)\
                                .then_inc(s["least_ok"], 1)
                        elif what == "scale":
                            dve.wait_ge(s["exped"], p * STEPS + 6 * j + 6)
                            dve.reciprocal(inverse[:, r, 2:4], rowsum[:, r, 4:6])
                            dve.wait_ge(s["total_ok"], p * UNITS + j + 1)
                            dve.reciprocal(inverse[:, r, 0:2], total[:, r]).then_inc(s["inverse_ok"], 1)
                    for what, j in side[k]:
                        if what == "turn_query":
                            low_queries(j % 4, p * UNITS + j + 1)
                        elif what == "absorb":
                            take_absorbed(p + 2)

            def low_out(q, tokens, n, done):
                dve.wait_ge(s["o_hi_ok"], n)
                dve.tensor_tensor(o_lo[:, q % 4], tokens, o_hi[:, q % 4].bitcast(F32), ALU.subtract)\
                    .then_inc(s[done], 1)

            for q in range(PAIRS):
                low_out(q, out_T[:, q, 0:512], q + 1, "o_lo_front" if q < 4 else "o_lo_back")
            dve.wait_ge(s["scales_in"], 80)
            for half_, full in ((sgate_half, sgate), (sup_half, sup)):
                dve.tensor_scalar(half_[:, 0:HT - 1], full[:, 0:HT - 1], 0.5, None, ALU.mult)
                m = dve.tensor_scalar(half_[0:HTAIL, HT - 1:HT], full[0:HTAIL, HT - 1:HT], 0.5, None, ALU.mult)
            m.then_inc(s["scales_chain"], 1)
            dve.wait_ge(s["scales_chain"], 1)
            dve.tensor_tensor(sgu[:, 0:HT - 1], sgate[:, 0:HT - 1], sup_half[:, 0:HT - 1], ALU.mult)
            dve.tensor_tensor(sgu[0:HTAIL, HT - 1:HT], sgate[0:HTAIL, HT - 1:HT], sup_half[0:HTAIL, HT - 1:HT],
                              ALU.mult).then_inc(s["scales_chain"], 1)
            dve.wait_ge(s["scales_chain"], 2)

            def low_up_gate(n):
                w = min(2 * P, HID - (n % 3) * 2 * P)
                lo, hi = ((wg_lo, wg_hi), (wu_lo, wu_hi))[n // 3]
                c0 = (n % 3) * 2 * P
                dve.wait_ge(s["fw_hi_ok"], n + 1)
                dve.tensor_tensor(lo[:, :, c0:c0 + w],
                                  turned[:, n % 2].rearrange("p (k c) -> p k c", k=KT)[:, :, 0:w],
                                  hi[:, :, c0:c0 + w].bitcast(F32), ALU.subtract).then_inc(s["fw_lo_ok"], 1)

            def low_down(n):
                t0 = (n - 6) * 2
                dve.wait_ge(s["fw_hi_ok"], n + 1)
                for t in (t0, t0 + 1):
                    rows = min(P, HID - t * P)
                    m = dve.tensor_tensor(wd_lo[0:rows, t], turned[0:rows, n % 2, (t - t0) * D:(t - t0 + 1) * D],
                                          wd_hi[0:rows, t].bitcast(F32), ALU.subtract)
                m.then_inc(s["fw_lo_ok"], 1)

            def tiles_of(c, t0, n):
                if isinstance(c, int):
                    return y1[:, (c % 2) * 4 + t0:(c % 2) * 4 + t0 + n, :]
                return y1[:, bass.ds((c % 2) * 4 + t0, n), :]

            def variances(src, n, st, mv, var, done, link):
                for t in range(n):
                    m = dve.bn_stats(st[:, t, :], src[:, t, :])
                link(m)
                dve.memset(pause[:, :], 0.0)
                for t in range(n):
                    m = dve.bn_aggr(mv[:, t, :], st[:, t, :])
                link(m)
                dve.tensor_scalar(var, mv[:, :, 1], EPS_LN, None, ALU.add).then_inc(s[done], 1)

            def normalise(dst, src, n, mv, rstd_):
                for t in range(n):
                    m = dve.tensor_scalar(dst[:, t, :], src[:, t, :], mv[:, t, 0:1], rstd_[:, t:t + 1],
                                          ALU.subtract, ALU.mult)
                return m

            attended = scores[:, 1].rearrange("p (t d) -> p t d", d=D)

            def first_variances(c, link):
                dve.wait_ge(s["att_back"], c + 1)
                variances(attended, 4, lstats[:, :, :], lmv[:, :, :], lvar[:, :], "ln_var", link)

            def first_norm(c):
                dve.wait_ge(s["ln_rstd"], c * 2 + 1)
                normalise(z[:, :, :], attended, 4, lmv, lrstd).then_inc(s["z1_ok"], 1)

            def second_variances(c, link):
                dve.wait_ge(s["y1_ok"], c + 1)
                variances(tiles_of(c, 0, 4), 4, lstats[:, :, :], lmv[:, :, :], lvar[:, :], "ln_var", link)

            def second_norm(c):
                dve.wait_ge(s["ln_rstd"], c * 2 + 2)
                normalise(z[:, :, :], tiles_of(c, 0, 4), 4, lmv, lrstd).then_inc(s["z_ready"], 1)

            def low_tokens(c):
                dve.wait_ge(s["zT_hi_ok"], c + 1)
                dve.tensor_tensor(zT_lo[:, :, :].rearrange("p a s -> p (a s)"), scores[:, 0],
                                  zT_hi[:, :, :].rearrange("p a s -> p (a s)").bitcast(F32), ALU.subtract)\
                    .then_inc(s["zT_lo_ok"], 1)

            def hidden(c, t):
                rows = min(P, HID - t * P)
                gate_ps = [turned[:, 0], latent[:, :]][t % 2]
                up_ps = [turned[:, 1], shared[:, :]][t % 2]
                dve.wait_ge(s["tanh_ok"], c * HT + t + 1)
                dve.scalar_tensor_tensor(gated[0:rows, t % 2], tanh_g[0:rows, t % 2], 1.0, gate_ps[0:rows, :],
                                         ALU.add, ALU.mult).then_inc(s["gated_ok"], 1)
                dve.wait_ge(s["gated_ok"], c * HT + t + 1)
                if t >= 2:
                    dve.wait_ge(s["h_lo_ok"], c * HT + t - 1)
                dve.scalar_tensor_tensor(h_f[0:rows, t % 2], up_ps[0:rows, :], sgu[0:rows, t:t + 1],
                                         gated[0:rows, t % 2], ALU.mult, ALU.mult).then_inc(s["h_ok"], 1)

            def finish_chunk(c, link):
                dve.wait_ge(s["result_free"], c + 1)
                for half_ in range(2):
                    two = slice(2 * half_, 2 * half_ + 2)
                    dve.wait_ge(s["down_psum"], c * 2 + half_ + 1)
                    link(dve.tensor_tensor(result[:, two], attended[:, two],
                                           sdown[:, None, :].to_broadcast([P, 2, D]), ALU.mult))
                    if half_:
                        dve.sem_inc(s["ffn_ok"], 1)
                    variances(result[:, two], 2, fstats[:, two], fmv[:, two], fvar[:, two], "ffn_var", link)
                for half_ in range(2):
                    two = slice(2 * half_, 2 * half_ + 2)
                    dve.wait_ge(s["ffn_rstd"], c * 2 + half_ + 1)
                    link(normalise(result[:, two], result[:, two], 2, fmv[:, two], frstd[:, two]))
                    dve.tensor_tensor(result[:, two], result[:, two], tiles_of(c, 2 * half_, 2), ALU.add)\
                        .then_inc(s["result_ok"], 1)

            late_count = [0]

            def late_link(ins):
                late_count[0] += 1
                ins.then_inc(s["dve_late"], 1)
                dve.wait_ge(s["dve_late"], late_count[0])

            first_variances(0, late_link)
            low_up_gate(0)
            first_norm(0)
            low_up_gate(1)
            second_variances(0, late_link)
            low_up_gate(2)
            second_norm(0)
            for n in range(3, 6):
                low_up_gate(n)
            low_tokens(0)
            for q in range(4):
                low_out(q, out_T[:, q, 512:1024], PAIRS + q + 1, "o_lo_front")
            for n in range(6, 9):
                low_down(n)
            BEFORE = late_count[0]
            PER_LATE = 4 + 8
            with dve.Fori(0, 3) as c:
                count = [0]

                def link(ins):
                    count[0] += 1
                    ins.then_inc(s["dve_late"], 1)
                    dve.wait_ge(s["dve_late"], c * PER_LATE + BEFORE + count[0])

                first_variances(c + 1, link)
                hidden(c, 0)
                first_norm(c + 1)
                hidden(c, 1)
                hidden(c, 2)
                second_variances(c + 1, link)
                hidden(c, 3)
                second_norm(c + 1)
                hidden(c, 4)
                hidden(c, 5)
                low_tokens(c + 1)
                for q in range(4):
                    low_out(q, out_flat[:, bass.ds(c * 512 + (q * S + 1024), 512)], c * PAIRS + 2 * PAIRS + q + 1,
                            "o_lo_front")
                finish_chunk(c, link)
                assert count[0] == PER_LATE, count
            late_count[0] = BEFORE + 3 * PER_LATE
            for t in range(HT):
                hidden(3, t)
            finish_chunk(3, late_link)


_INS = ["L0_attn_x", "L0_attn_wq", "L0_attn_wkv_a", "L0_attn_wkv_b", "L0_attn_wo", "L0_attn_kv_norm_w",
        "L0_ffn_wq_gate", "L0_ffn_s_gate", "L0_ffn_wq_up", "L0_ffn_s_up", "L0_ffn_wq_down", "L0_ffn_s_down"]


def kernel(**inputs):
    import concourse.bacc as bacc
    from concourse.bass_utils import run_bass_kernel_spmd

    nc = bacc.Bacc("TRN2", target_bir_lowering=False, num_devices=1)
    arrays = {name: np.ascontiguousarray(inputs[name]) for name in _INS}
    freqs = 1.0 / THETA ** (np.arange(0, ROPE, 2, dtype=np.float32) / ROPE)
    angles = np.outer(np.arange(S, dtype=np.float32), freqs)
    arrays["cos_table"] = np.cos(angles).astype(np.float32)
    arrays["sin_table"] = np.sin(angles).astype(np.float32)
    args = [nc.dram_tensor(name, a.shape, mybir.dt.from_np(a.dtype), kind="ExternalInput").ap()
            for name, a in arrays.items()]
    out = nc.dram_tensor("out", (1, S, D), F32, kind="ExternalOutput").ap()
    build(nc, *args, out)
    r = run_bass_kernel_spmd(nc, [arrays], core_ids=[0])
    return r.results[0]["out"]
```

```python
from contextlib import ExitStack

import numpy as np

import concourse.bass as bass
from concourse import mybir


P = 128
F32 = mybir.dt.float32
F32R = mybir.dt.float32r
F16 = mybir.dt.float16
BF16 = mybir.dt.bfloat16
I32 = mybir.dt.int32
ALU = mybir.AluOpType
ACT = mybir.ActivationFunctionType
AX = mybir.AxisListType

S = 2048
D = 256
KT = D // P
H = 16
NOPE, ROPE, VD, C = 128, 64, 128, 64
QK = NOPE + ROPE
NT = S // P
PAIRS = H // 2
HID = 704
HT = -(-HID // P)
HTAIL = HID - (HT - 1) * P
SCALE = float(QK) ** -0.5
EPS_LN = 1e-5
EPS_RMS = 1e-6
MASKED = -1e30
ZERO_POINT = 128.0
THETA = 10000.0


UNITS = NT // 2
LAG = 2
SLOTS = LAG + 1


def plan_attention():
    steps, groups = [], 0
    for j in range(UNITS):
        small, big = j, NT - 1 - j
        n = big + 1
        for head in range(2):
            for part, tile, b0, b1 in ((2 * head, big, 0, -(-n // 2)), (4 + head, small, 0, small + 1),
                                       (2 * head + 1, big, -(-n // 2), n)):
                g = []
                for b in range(b0, b1, 4):
                    g.append((groups, b, min(4, b1 - b)))
                    groups += 1
                steps.append(dict(unit=j, head=head, tile=tile, part=part, b0=b0, nb=b1 - b0, groups=g,
                                  diagonal=b1 == tile + 1))
    side = [[] for _ in steps]
    for j in range(UNITS):
        side[6 * j].append(("project", j + 2))
        side[6 * j + 4].append(("turn_out", j - 1))
        side[6 * j + 5].append(("turn_query", j + 2))
    side[6 * 5 + 3].append(("absorb", 0))
    side[6 * 6 + 1].append(("turn_wo", 0))
    side[6 * 7 + 2].append(("value_map", 0))
    finish = [[] for _ in steps]
    for j in range(UNITS):
        for lag, what in ((0, "least"), (1, "weigh"), (3, "scale")):
            finish[min(6 * j + 5 + lag, len(steps) - 1)].append((what, j))
    return steps, groups, side, finish


def build(nc, x, wq, wkv_a, wkv_b, wo, kv_norm_w, wq_gate, s_gate, wq_up, s_up, wq_down, s_down,
          cos_table, sin_table, out):
    steps, GROUPS, side, finish = plan_attention()
    STEPS = len(steps)
    SPLIT = [st["nb"] > 4 for st in steps]
    SPLITS = sum(SPLIT)

    def splits(k):
        return sum(SPLIT[:k + 1])

    ctx = ExitStack()
    with ctx:
        def sem(name):
            return ctx.enter_context(nc.semaphore(name))

        def psum(name, shape):
            return ctx.enter_context(nc.psum_tensor(name, shape, F32))

        def kept(name, shape, dt):
            return ctx.enter_context(nc.sbuf_tensor(name, shape, dt))

        scores = psum("scores", [P, 2, 1024])
        turned = psum("turned", [P, 2, 512])
        latent = psum("latent", [P, 512])
        shared = psum("shared", [P, 512])

        ident = kept("ident", [P, P], F32)
        half = kept("half", [P, 1], F32)
        one = kept("one", [P, 1], F32)
        pause = kept("pause", [P, 1], F32)
        out_T = kept("out_T", [P, PAIRS, S], F32)
        gmap_hi = kept("gmap_hi", [P, PAIRS, D], F32R)
        gmap_lo = kept("gmap_lo", [P, PAIRS, D], F32R)

        early = ExitStack()

        def sb(name, shape, dt):
            return early.enter_context(nc.sbuf_tensor(name, shape, dt))

        ident16 = sb("ident16", [P, P], BF16)
        mask = sb("mask", [P, P], BF16)
        cos_sb = sb("cos_sb", [P, NT, ROPE // 2], F32)
        sin_sb = sb("sin_sb", [P, NT, ROPE // 2], F32)
        wscale = sb("wscale", [P, P], F32)
        wcol = sb("wcol", [P, 1], F32)
        xT_hi = sb("xT_hi", [P, KT, S], F32R)
        xT_lo = sb("xT_lo", [P, KT, S], F32R)
        kT_hi = sb("kT_hi", [P, S], F32R)
        kT_lo = sb("kT_lo", [P, S], F32R)
        v_hi = sb("v_hi", [P, NT, C], F16)
        v_lo = sb("v_lo", [P, NT, C], F16)
        wqn = sb("wqn", [P, 2, D], F32)
        wqr = sb("wqr", [P, D], F32)
        wkb = sb("wkb", [P, 2, C], F32)
        wvb = sb("wvb", [P, 2, P], F32)
        wo_sb = sb("wo_sb", [P, KT, 2, VD], F32)
        wo_T = sb("wo_T", [P, 2, D], F32)
        w_f = sb("w_f", [P, KT, 2, P], F32)
        w_hi = sb("w_hi", [P, KT, 2 * P], F32R)
        w_lo = sb("w_lo", [P, KT, 2 * P], F32R)
        g_f = sb("g_f", [P, D], F32)
        qn = sb("qn", [P, 2, 2, 2, P], F32)
        q_hi = sb("q_hi", [P, 4, 512], F32R)
        q_lo = sb("q_lo", [P, 4, 512], F32R)
        rope_t = sb("rope_t", [P, 4, 2, 2, ROPE // 2], F32)
        prob = sb("prob", [P, 2, 1024], F32)
        probT_hi = sb("probT_hi", [P, SLOTS, 512], F16)
        probT_lo = sb("probT_lo", [P, SLOTS, 512], F16)
        negmax = sb("negmax", [P, 2, 6], F32)
        halfmax = sb("halfmax", [P, 2, 2], F32)
        rowsum = sb("rowsum", [P, 2, 6], F32)
        negall = sb("negall", [P, 2, 2], F32)
        below = sb("below", [P, 2, 2, 2], F32)
        weight = sb("weight", [P, 2, 2, 2], F32)
        wsum = sb("wsum", [P, 2, 2, 2], F32)
        total = sb("total", [P, 2, 2], F32)
        inverse = sb("inverse", [P, 2, 4], F32)
        factor = sb("factor", [P, 2, 2, 2], F32)
        raw_out = sb("raw_out", [P, 2, 6, C], F32)
        part_out = sb("part_out", [P, 4, C], F32)
        norm_out = sb("norm_out", [P, 2, 2, 2, C], F32)
        stats = sb("stats", [P, 4, 6], F32)
        meanvar = sb("meanvar", [P, 4, 2], F32)
        vareps = sb("vareps", [P, 4], F32)
        rstd = sb("rstd", [P, 4], F32)
        latent_ms = sb("latent_ms", [P, 4], F32)
        latent_rms = sb("latent_rms", [P, 4], F32)
        wkva_f = sb("wkva_f", [P, D], F32)
        wkva_hi = sb("wkva_hi", [P, KT, P], F32R)
        wkva_lo = sb("wkva_lo", [P, KT, P], F32R)
        x_in = out_T[:, PAIRS - 2:PAIRS, :].rearrange("p a (g d) -> p (a g) d", d=D)
        kv_f = out_T[:, PAIRS - 3, 0:512].rearrange("p (t c) -> p t c", c=P)
        keys = out_T[:, PAIRS - 3, 512:1024].rearrange("p (t c) -> p t c", c=P)
        xn = prob[:, :, :].rearrange("p a (t d) -> p (a t) d", d=D)[:, 0:4, :]
        kvT = prob[:, 1, 0:512]
        square = raw_out[:, 0, 0:4]
        early.close()

        late = ExitStack()

        def sl(name, shape, dt):
            return late.enter_context(nc.sbuf_tensor(name, shape, dt))

        sdown = sl("sdown", [P, D], F32)
        sgate_half = sl("sgate_half", [P, HT], F32)
        sgate = sl("sgate", [P, HT], F32)
        sup_half = sl("sup_half", [P, HT], F32)
        sup = sl("sup", [P, HT], F32)
        sgu = sl("sgu", [P, HT], F32)
        lstats = sl("lstats", [P, 4, 6], F32)
        lmv = sl("lmv", [P, 4, 2], F32)
        lvar = sl("lvar", [P, 4], F32)
        lrstd = sl("lrstd", [P, 4], F32)
        fstats = sl("fstats", [P, 4, 6], F32)
        fmv = sl("fmv", [P, 4, 2], F32)
        fvar = sl("fvar", [P, 4], F32)
        frstd = sl("frstd", [P, 4], F32)
        o_hi = sl("o_hi", [P, 4, 512], F32R)
        o_lo = sl("o_lo", [P, 4, 512], F32R)
        x_res = sl("x_res", [P, 4, D], F32)
        att_T = sl("att_T", [P, KT, 512], F32)
        y1 = sl("y1", [P, 2 * 4, D], F32)
        z = sl("z", [P, 4, D], F32)
        wg_hi = sl("wg_hi", [P, KT, HID], F32R)
        wg_lo = sl("wg_lo", [P, KT, HID], F32R)
        wu_hi = sl("wu_hi", [P, KT, HID], F32R)
        wu_lo = sl("wu_lo", [P, KT, HID], F32R)
        wd_hi = sl("wd_hi", [P, HT, D], F32R)
        wd_lo = sl("wd_lo", [P, HT, D], F32R)
        zT_hi = sl("zT_hi", [P, KT, 512], F32R)
        zT_lo = sl("zT_lo", [P, KT, 512], F32R)
        with ExitStack() as passing:
            w_int = passing.enter_context(nc.sbuf_tensor("w_int", [P, 4, HID], I32))
            w_flt = passing.enter_context(nc.sbuf_tensor("w_flt", [P, 4, HID], F32))
        h_hi = sl("h_hi", [P, HT, 512], F32R)
        tanh_g = sl("tanh_g", [P, 2, 512], F32)
        gated = sl("gated", [P, 2, 512], F32)
        h_f = sl("h_f", [P, 2, 512], F32)
        h_lo = sl("h_lo", [P, HT, 512], F32R)
        result = sl("result", [P, 4, D], F32)
        late.close()

        x_v = x.rearrange("b (g t p) d -> (b g) p t d", t=4, p=P)
        out_v = out.rearrange("b (g t p) d -> (b g) p t d", t=4, p=P)
        wq_v = wq.rearrange("(g t e) d -> g e t d", t=2, e=QK)
        wkvb_v = wkv_b.rearrange("(g t e) c -> g e t c", t=2, e=NOPE + VD)
        wo_v = wo.rearrange("(a p) (g t v) -> g p a t v", p=P, t=2, v=VD)

        names = """wkva_in const_in table_in x_in_s ident_ok ones_ok pad_ok var_ready rstd_ready xn_ready
            xT_psum xT_hi_ok xT_lo_ok kvT_psum kvT_sb kv_psum kv_sb ms_ready rms_ready keys_ok
            k_psum k_hi_ok k_lo_ok values_ok wkva_psum wkva_hi_ok wkva_lo_ok wscale_ok dve_setup
            pool_setup head_w head_v absorbed absorbed_sb w_split wo_turned wo_T_ok gmapped gmap_sb
            gmap_ok projected qn_ok roped q_turned q_hi_ok q_lo_ok half_scored half_maxed scored
            maxed exped turned_p probT_hi_ok probT_lo_ok summed raw_ok least_ok below_ok weight_ok
            total_ok inverse_ok norm_ok out_turned out_T_ok pool_chain wint_in0 wint_in1 wint_in2
            wint_in3 wflt_ok fw_psum fw_hi_ok fw_lo_ok scales_in scales_chain xres_in o_hi_ok
            o_lo_ok h_tail_ok o_used att_sb att_back ln_var ln_rstd z1_ok dve_late z_ready z_psum
            zT_hi_ok zT_lo_ok y1_ok gate_psum tanh_ok gated_ok h_ok h_hi_ok h_lo_ok down_psum ffn_ok
            ffn_var ffn_rstd result_ok stored result_free""".split()
        s = {n: sem(n) for n in names}
        block = ctx.enter_context(nc.Block())

        @block.sync
        def _(sp):
            sp.dma_start(wkva_f[:, :], wkv_a).then_inc(s["wkva_in"], 16)
            sp.dma_start(x_in[:, 0:4], x_v[0]).then_inc(s["x_in_s"], 16)

            def load_key_weights(p):
                sp.dma_start(wqn[:, :, :], wq_v[p, 0:NOPE]).then_inc(s["head_w"], 16)
                sp.dma_start(wqr[0:ROPE, :], wq_v[p, NOPE:QK, 0]).then_inc(s["head_w"], 16)
                sp.dma_start(wqr[ROPE:P, :], wq_v[p, NOPE:QK, 1]).then_inc(s["head_w"], 16)
                sp.dma_start(wkb[:, :, :], wkvb_v[p, 0:NOPE]).then_inc(s["head_w"], 16)

            def load_value_weights(p):
                sp.dma_start(wvb[:, 0, 0:C], wkvb_v[p, NOPE:NOPE + VD, 0]).then_inc(s["head_v"], 16)
                sp.dma_start(wvb[:, 1, C:P], wkvb_v[p, NOPE:NOPE + VD, 1]).then_inc(s["head_v"], 16)
                for a in range(KT):
                    sp.dma_start(wo_sb[:, a], wo_v[p, :, a]).then_inc(s["head_v"], 16)

            load_key_weights(0)
            sp.dma_start(wscale[:, 0:C], kv_norm_w.partition_broadcast(P)).then_inc(s["const_in"], 16)
            for half_ in range(2):
                sp.dma_start(wcol[half_ * C:(half_ + 1) * C, :],
                             kv_norm_w.rearrange("(p a) -> p a", a=1)).then_inc(s["const_in"], 16)
            sp.dma_start(cos_sb[:, :, :], cos_table.rearrange("(t p) f -> p t f", p=P)).then_inc(s["table_in"], 16)
            sp.dma_start(sin_sb[:, :, :], sin_table.rearrange("(t p) f -> p t f", p=P)).then_inc(s["table_in"], 16)
            for g in range(1, 4):
                sp.wait_ge(s["x_in_s"], 16 * g)
                sp.dma_start(x_in[:, 4 * g:4 * g + 4], x_v[g]).then_inc(s["x_in_s"], 16)

            sp.wait_ge(s["pad_ok"], 1)
            with sp.Fori(0, PAIRS - 1) as p:
                sp.wait_ge(s["gmapped"], p + 1)
                load_value_weights(p)
                sp.wait_ge(s["absorbed"], p + 1)
                load_key_weights(p + 1)
            sp.wait_ge(s["gmapped"], PAIRS)
            load_value_weights(PAIRS - 1)
            sp.wait_ge(s["absorbed"], PAIRS)
            load_key_weights(PAIRS - 1)

            sp.wait_ge(s["exped"], PAIRS * STEPS + 1)
            sp.wait_ge(s["maxed"], PAIRS * STEPS + 2)
            sp.wait_ge(s["q_lo_ok"], PAIRS * UNITS + 2)
            sp.wait_ge(s["gmap_ok"], PAIRS)
            sp.wait_ge(s["w_split"], PAIRS + 1)
            n = 0
            for w in (wq_gate, wq_up):
                for t0 in (0, 2, 4):
                    for t in (t0, t0 + 1):
                        rows = min(P, HID - t * P)
                        if n == 8:
                            sp.dma_start(x_res[:, :, :], x_v[0]).then_inc(s["xres_in"], 16)
                            for scale, tile in ((s_gate, sgate), (s_up, sup)):
                                with nc.allow_non_contiguous_dma(reason="704 scales, once"):
                                    sp.dma_start(tile[:, 0:HT - 1],
                                                 scale[0:(HT - 1) * P].rearrange("(t p) -> p t", p=P))\
                                        .then_inc(s["scales_in"], 16)
                                sp.dma_start(tile[0:HTAIL, HT - 1:HT], scale[(HT - 1) * P:HID].rearrange("(p a) -> p a", a=1))\
                                    .then_inc(s["scales_in"], 16)
                            sp.dma_start(sdown[:, :], s_down.partition_broadcast(P)).then_inc(s["scales_in"], 16)
                        if n >= 8:
                            sp.wait_ge(s["wflt_ok"], n // 2 - 3)
                        sp.dma_start(w_int[0:rows, (n // 2) % 4, (t - t0) * D:(t - t0 + 1) * D],
                                     w[t * P:t * P + rows, :]).then_inc(s[f"wint_in{n // 2 % 4}"], 16)
                        n += 1
            for a in range(KT):
                sp.wait_ge(s["wflt_ok"], n // 2 - 3 + a)
                sp.dma_start(w_int[:, (n // 2 + a) % 4, 0:HID], wq_down[a * P:(a + 1) * P, :])\
                    .then_inc(s[f"wint_in{(n // 2 + a) % 4}"], 16)

            def store(c):
                for half_ in range(2):
                    sp.wait_ge(s["result_ok"], c * 2 + half_ + 1)
                    sp.dma_start(out_v[c][:, 2 * half_:2 * half_ + 2], result[:, 2 * half_:2 * half_ + 2, :])\
                        .then_inc(s["stored"], 16)
                sp.wait_ge(s["stored"], c * 32 + 32)
                sp.sem_inc(s["result_free"], 1)

            with sp.Fori(0, 3) as c:
                sp.wait_ge(s["y1_ok"], c + 1)
                sp.dma_start(x_res[:, :, :], x_v[c + 1]).then_inc(s["xres_in"], 16)
                store(c)
            store(3)

        @block.gpsimd
        def _(pool):
            pool.memset(half[:, :], -0.5).then_inc(s["ones_ok"], 1)
            pool.memset(one[:, :], 1.0).then_inc(s["ones_ok"], 1)
            pool.memset(wscale[:, C:P], 1.0).then_inc(s["ones_ok"], 1)
            pool.memset(wvb[:, :, :], 0.0).then_inc(s["pad_ok"], 1)
            pool.memset(norm_out[:, :, :, :, :], 0.0).then_inc(s["norm_ok"], 1)
            pool.memset(ident[:, :], 0.0).then_inc(s["ident_ok"], 1)
            pool.memset(ident16[:, :], 0.0).then_inc(s["ident_ok"], 1)
            pool.memset(mask[:, :], 0.0).then_inc(s["ident_ok"], 1)
            pool.wait_ge(s["ident_ok"], 3)
            for m in (ident, ident16):
                pool.affine_select(out=m[:, :], in_=m[:, :], compare_op=ALU.not_equal, fill=1.0, base=0,
                                   pattern=[[-1, P]], channel_multiplier=1).then_inc(s["ident_ok"], 1)
            pool.affine_select(out=mask[:, :], in_=mask[:, :], compare_op=ALU.is_ge, fill=MASKED, base=0,
                               pattern=[[-1, P]], channel_multiplier=1).then_inc(s["ident_ok"], 1)

            def power(dst, src):
                return pool.tensor_tensor(dst, src, half[:, 0:1].to_broadcast([P, 4]), ALU.pow)

            def rope(src, cos, sin, shape, link):
                even, odd = src[..., 0:ROPE:2], src[..., 1:ROPE:2]
                t = [rope_t[:, n] if len(shape) == 4 else rope_t[:, n].rearrange("p a b f -> p (a b) f")
                     for n in range(4)]
                pool.tensor_tensor(t[0], even, cos, ALU.mult)
                pool.tensor_tensor(t[1], odd, sin, ALU.mult)
                pool.tensor_tensor(t[2], even, sin, ALU.mult)
                link(pool.tensor_tensor(t[3], odd, cos, ALU.mult))
                pool.tensor_tensor(even, t[0], t[1], ALU.subtract)
                return pool.tensor_tensor(odd, t[2], t[3], ALU.add)

            pool.wait_ge(s["ones_ok"], 3)
            def token_roots(g):
                pool.wait_ge(s["var_ready"], g + 1)
                power(rstd[:, :], vareps[:, :]).then_inc(s["rstd_ready"], 1)

            def finish_keys(g):
                pool.wait_ge(s["ms_ready"], g + 1)
                power(latent_rms[:, :], latent_ms[:, :]).then_inc(s["rms_ready"], 1)

                def link(ins):
                    ins.then_inc(s["pool_setup"], 1)
                    pool.wait_ge(s["pool_setup"], g + 1)

                pool.wait_ge(s["keys_ok"], 2 * g + 1)
                four = slice(4 * g, 4 * g + 4) if isinstance(g, int) else bass.ds(g * 4, 4)
                rope(keys[:, :, C:P], cos_sb[:, four, :], sin_sb[:, four, :], [P, 4, 32], link)\
                    .then_inc(s["keys_ok"], 1)

            def split_w(n):
                pool.wait_ge(s["absorbed_sb"], n)
                flat = w_f[:, :, :, :].rearrange("p k t c -> p k (t c)")
                pool.tensor_tensor(w_hi[:, :, :], flat, one[:, 0:1, None].to_broadcast([P, KT, 2 * P]), ALU.mult)\
                    .then_inc(s["pool_chain"], 1)

            def split_w_low():
                flat = w_f[:, :, :, :].rearrange("p k t c -> p k (t c)")
                pool.tensor_tensor(w_lo[:, :, :], flat, w_hi[:, :, :].bitcast(F32), ALU.subtract)\
                    .then_inc(s["w_split"], 1)

            def rope_group(slot, j, n, link):
                pool.wait_ge(s["qn_ok"], n)
                two = slice(j, NT - j, NT - 1 - 2 * j)
                cos = cos_sb[:, two, None, :].to_broadcast([P, 2, 2, ROPE // 2])
                sin = sin_sb[:, two, None, :].to_broadcast([P, 2, 2, ROPE // 2])
                rope(qn[:, slot, :, :, C:P], cos, sin, [P, 2, 2, 32], link).then_inc(s["roped"], 1)

            LEAD = 1 + 2
            count = [0]

            def first_link(ins):
                count[0] += 1
                if ins is not None:
                    ins.then_inc(s["pool_chain"], 1)
                pool.wait_ge(s["pool_chain"], count[0])

            token_roots(0)
            split_w(1)
            first_link(None)
            split_w_low()
            pool.wait_ge(s["table_in"], 32)
            token_roots(1)
            with pool.Fori(0, 2) as g:
                finish_keys(g)
                token_roots(g + 2)
            finish_keys(2)
            rope_group(0, 0, 1, first_link)
            pool.wait_ge(s["roped"], 1)
            finish_keys(3)
            pool.wait_ge(s["keys_ok"], 8)
            rope_group(1, 1, 2, first_link)
            assert count[0] == LEAD

            with pool.Fori(0, PAIRS) as p:
                PER = 8 + 1 + 1 + 8 * 4
                count = [0]

                def link(ins):
                    count[0] += 1
                    if ins is not None:
                        ins.then_inc(s["pool_chain"], 1)
                    pool.wait_ge(s["pool_chain"], p * PER + LEAD + count[0])

                for k in range(STEPS):
                    for what, i in side[k]:
                        if what == "project":
                            rope_group(i % 2, i % UNITS, p * UNITS + i + 1, link)
                        elif what == "absorb":
                            split_w(p + 2)
                            link(None)
                            split_w_low()
                        elif what == "value_map":
                            pool.wait_ge(s["gmap_sb"], p + 1)
                            link(pool.tensor_tensor(gmap_hi[:, p, :], g_f[:, :], one[:, 0:1].to_broadcast([P, D]), ALU.mult))
                            pool.tensor_tensor(gmap_lo[:, p, :], g_f[:, :], gmap_hi[:, p, :].bitcast(F32),
                                               ALU.subtract).then_inc(s["gmap_ok"], 1)
                    for what, j in finish[k]:
                        r = j % 2
                        four = lambda a: a[:, r].rearrange("p a b -> p (a b)")
                        if what == "least":
                            pool.wait_ge(s["least_ok"], p * UNITS + j + 1)
                            pool.tensor_tensor(below[:, r], negall[:, r, :, None].to_broadcast([P, 2, 2]),
                                               negmax[:, r, 0:4].rearrange("p (a b) -> p a b", b=2),
                                               ALU.subtract).then_inc(s["below_ok"], 1)
                        elif what == "weigh":
                            pool.wait_ge(s["weight_ok"], p * UNITS + j + 1)
                            link(pool.tensor_tensor(four(wsum), four(weight), rowsum[:, r, 0:4], ALU.mult))
                            pool.tensor_tensor(total[:, r], wsum[:, r, :, 0], wsum[:, r, :, 1], ALU.add)\
                                .then_inc(s["total_ok"], 1)
                        elif what == "scale":
                            pool.wait_ge(s["inverse_ok"], p * UNITS + j + 1)
                            pool.wait_ge(s["raw_ok"], p * UNITS + j + 2)
                            pool.tensor_tensor(norm_out[:, r, 0], raw_out[:, r, 4:6],
                                               inverse[:, r, 2:4, None].to_broadcast([P, 2, C]), ALU.mult)
                            link(pool.tensor_tensor(factor[:, r], weight[:, r],
                                                    inverse[:, r, 0:2, None].to_broadcast([P, 2, 2]), ALU.mult))
                            link(pool.tensor_tensor(part_out[:, :, :], raw_out[:, r, 0:4],
                                                    four(factor)[:, :, None].to_broadcast([P, 4, C]), ALU.mult))
                            pair = part_out[:, :, :].rearrange("p (a b) c -> p a b c", b=2)
                            link(pool.tensor_tensor(norm_out[:, r, 1], pair[:, :, 0], pair[:, :, 1], ALU.add))
                            pool.sem_inc(s["norm_ok"], 1)
                assert count[0] == PER, count

            def power_of(dst, src, n):
                return pool.tensor_tensor(dst, src, half[:, 0:1].to_broadcast([P, n]), ALU.pow)

            def norm_root(n):
                pool.wait_ge(s["ln_var"], n + 1)
                power_of(lrstd[:, :], lvar[:, :], 4).then_inc(s["ln_rstd"], 1)

            def add_tokens(c):
                pool.wait_ge(s["z1_ok"], c + 1)
                pool.wait_ge(s["xres_in"], c * 16 + 16)
                slot = c % 2
                pool.tensor_tensor(y1[:, slot * 4:slot * 4 + 4, :] if isinstance(c, int) else
                                   y1[:, bass.ds(slot * 4, 4), :], z[:, :, :], x_res[:, :, :], ALU.add)\
                    .then_inc(s["y1_ok"], 1)

            def low_hidden(c, t):
                rows = min(P, HID - t * P)
                pool.wait_ge(s["h_hi_ok"], c * HT + t + 1)
                pool.tensor_tensor(h_lo[0:rows, t], h_f[0:rows, t % 2], h_hi[0:rows, t].bitcast(F32),
                                   ALU.subtract).then_inc(s["h_lo_ok"], 1)

            def ffn_roots(c):
                for half_ in range(2):
                    pool.wait_ge(s["ffn_var"], c * 2 + half_ + 1)
                    two = slice(2 * half_, 2 * half_ + 2)
                    power_of(frstd[:, two], fvar[:, two], 2).then_inc(s["ffn_rstd"], 1)

            def low_out(c, q):
                tokens = slice(c * 512, c * 512 + 512) if isinstance(c, int) else bass.ds(c * 512, 512)
                pool.wait_ge(s["o_hi_ok"], c * PAIRS + q + 1)
                pool.tensor_tensor(o_lo[:, q % 4], out_T[:, q, tokens], o_hi[:, q % 4].bitcast(F32), ALU.subtract)\
                    .then_inc(s["o_lo_ok"], 1)

            low_out(1, 0)
            norm_root(0)
            for q in range(1, 4):
                low_out(1, q)
            norm_root(1)
            for q in range(4, PAIRS):
                low_out(1, q)

            def chunk(c, more):
                norm_root(c * 2 + 2)
                low_hidden(c, 0)
                add_tokens(c + 1)
                low_hidden(c, 1)
                low_hidden(c, 2)
                norm_root(c * 2 + 3)
                for t in range(3, HT - 1):
                    low_hidden(c, t)
                for q in range(6 * more):
                    low_out(c + 2, q)
                ffn_roots(c)
                for q in range(6, PAIRS * more):
                    low_out(c + 2, q)

            with pool.Fori(0, 2) as c:
                chunk(c, True)
            chunk(2, False)
            for t in range(HT - 1):
                low_hidden(3, t)
            ffn_roots(3)

        @block.tensor
        def _(pe):
            def three(dst, w_h, w_l, x_h, x_l, start, stop):
                pe.matmul(dst, w_h, x_h, start=start, stop=False)
                pe.matmul(dst, w_h, x_l, start=False, stop=False)
                return pe.matmul(dst, w_l, x_h, start=False, stop=stop)

            pe.sem_inc(s["gmapped"], 1)
            pe.sem_inc(s["o_used"], 1)
            pe.wait_ge(s["ident_ok"], 6)
            pe.wait_ge(s["wkva_in"], 16)
            for k in range(KT):
                m = pe.transpose(shared[:, k * P:(k + 1) * P], wkva_f[:, k * P:(k + 1) * P], ident[:, :])
            m.then_inc(s["wkva_psum"], 1)
            pe.wait_ge(s["wkva_lo_ok"], 1)
            xT_ps = scores[:, 0]

            def turn_x(g):
                pe.wait_ge(s["xn_ready"], g + 1)
                for k in range(KT):
                    for t in range(4):
                        m = pe.transpose(xT_ps[:, k * 512 + t * P:k * 512 + (t + 1) * P],
                                         xn[:, t, k * P:(k + 1) * P], ident[:, :])
                m.then_inc(s["xT_psum"], 1)

            def latents(g):
                tokens = slice(0, 512) if isinstance(g, int) else bass.ds(g * 512, 512)
                for k in range(KT):
                    m = three(turned[:, 1], wkva_hi[:, k], wkva_lo[:, k], xT_hi[:, k, tokens], xT_lo[:, k, tokens],
                              k == 0, k == KT - 1)
                m.then_inc(s["kvT_psum"], 1)

            def turn_latents(g):
                pe.wait_ge(s["kvT_sb"], g + 1)
                for t in range(4):
                    m = pe.transpose(latent[:, t * P:(t + 1) * P], kvT[:, t * P:(t + 1) * P], ident[:, :])
                m.then_inc(s["kv_psum"], 1)

            def turn_keys(g):
                pe.wait_ge(s["values_ok"], g + 1)
                pe.wait_ge(s["keys_ok"], 2 * g + 2)
                for t in range(4):
                    m = pe.transpose(turned[:, 0, t * P:(t + 1) * P], keys[:, t, :], ident[:, :])
                m.then_inc(s["k_psum"], 1)

            def absorb():
                for k in range(KT):
                    for t in range(2):
                        pe.matmul(shared[:, (2 * k + t) * P:(2 * k + t) * P + C], wqn[:, t, k * P:(k + 1) * P],
                                  wkb[:, t, :], start=True, stop=True)
                    rot = shared[:, k * 2 * P:(k + 1) * 2 * P].rearrange("p (t c) -> p t c", t=2)[:, :, C:P]
                    m = pe.transpose(rot, wqr[:, k * P:(k + 1) * P], ident[:, :])
                m.then_inc(s["absorbed"], 1)

            def project(j):
                for t, tile in enumerate((j, NT - 1 - j)):
                    for k in range(KT):
                        cols = slice(tile * P, (tile + 1) * P)
                        m = three(shared[:, t * 256:(t + 1) * 256], xT_hi[:, k, cols], xT_lo[:, k, cols],
                                  w_hi[:, k], w_lo[:, k], k == 0, k == KT - 1)
                m.then_inc(s["projected"], 1)

            def turn_query(slot):
                for t in range(2):
                    for h in range(2):
                        m = pe.transpose(shared[:, (2 * t + h) * P:(2 * t + h + 1) * P], qn[:, slot, t, h, :],
                                         ident[:, :])
                m.then_inc(s["q_turned"], 1)

            def score(k, half_, done):
                st = steps[k]
                q0 = ((0 if st["part"] >= 4 else 2) + st["head"]) * P
                qh = q_hi[:, st["unit"] % 4, q0:q0 + P]
                ql = q_lo[:, st["unit"] % 4, q0:q0 + P]
                nb = min(4, st["nb"] - half_)
                wide = max(nb, 2)
                c0 = (st["b0"] + half_) * P
                dst = scores[:, k % 2, half_ * P:(half_ + wide) * P]
                kh, kl = kT_hi[:, c0:c0 + wide * P], kT_lo[:, c0:c0 + wide * P]
                pe.matmul(dst, qh, kh, start=True, stop=False)
                if st["diagonal"] and half_ + nb == st["nb"]:
                    d0 = (half_ + nb - 1) * P
                    pe.matmul(scores[:, k % 2, d0:d0 + P], ident16[:, :], mask[:, :], start=False, stop=False)
                pe.matmul(dst, qh, kl, start=False, stop=False)
                m = pe.matmul(dst, ql, kh, start=False, stop=True)
                if done:
                    m.then_inc(s["scored"], 1)
                elif half_ == 0:
                    m.then_inc(s["half_scored"], 1)

            def turn_out(j, n):
                pe.wait_ge(s["norm_ok"], n)
                for t in range(2):
                    m = pe.transpose(shared[:, t * P:(t + 1) * P],
                                     norm_out[:, j % 2, t].rearrange("p a c -> p (a c)"), ident[:, :])
                m.then_inc(s["out_turned"], 1)

            pe.wait_ge(s["head_w"], 64)
            absorb()
            turn_x(0)
            pe.wait_ge(s["xT_lo_ok"], 1)
            latents(0)
            with pe.Fori(0, 3) as g:
                turn_latents(g)
                turn_x(g + 1)
                pe.wait_ge(s["xT_lo_ok"], g + 2)
                latents(g + 1)
                turn_keys(g)
            pe.wait_ge(s["w_split"], 1)
            project(0)
            turn_latents(3)
            pe.wait_ge(s["roped"], 1)
            turn_query(0)
            pe.wait_ge(s["q_lo_ok"], 1)
            project(1)
            for half_ in range(0, steps[0]["nb"], 4):
                score(0, half_, half_ + 4 >= steps[0]["nb"])
            for half_ in range(0, steps[1]["nb"], 4):
                score(1, half_, half_ + 4 >= steps[1]["nb"])
            turn_keys(3)
            pe.wait_ge(s["roped"], 2)
            turn_query(1)
            pe.wait_ge(s["k_lo_ok"], 4)

            with pe.Fori(0, PAIRS) as p:
                reader = [("q_lo_ok", p * UNITS + 2)]

                def turn(k, group):
                    g, b, nb = group
                    b -= steps[k]["b0"]
                    if g >= 2:
                        pe.wait_ge(s["probT_lo_ok"], p * GROUPS + g - 1)
                    for n in range(nb):
                        m = pe.transpose(turned[:, g % 2, n * P:(n + 1) * P], prob[:, k % 2, (b + n) * P:(b + n + 1) * P],
                                         ident[:, :])
                    m.then_inc(s["turned_p"], 1)

                def add_values(k, group):
                    st = steps[k]
                    g, b, nb = group
                    if k % 6 == 0 and group is st["groups"][0]:
                        pe.wait_ge(s["raw_ok"], p * UNITS + st["unit"] + 1)
                    pe.wait_ge(s["probT_lo_ok"], p * GROUPS + g + 1)
                    dst = latent[:, st["part"] * C:(st["part"] + 1) * C]
                    for n in range(nb):
                        cols = slice(n * P, (n + 1) * P)
                        m = three(dst, probT_hi[:, g % SLOTS, cols], probT_lo[:, g % SLOTS, cols], v_hi[:, b + n, :],
                                  v_lo[:, b + n, :], b + n == st["b0"], b + n == st["b0"] + st["nb"] - 1)
                    if k % 6 == 5 and group is st["groups"][-1]:
                        m.then_inc(s["summed"], 1)

                by_number = [(k, group) for k, st in enumerate(steps) for group in st["groups"]]
                for k, st in enumerate(steps):
                    pe.wait_ge(s["exped"], p * STEPS + k + 1)
                    nk = (k + 2) % STEPS
                    if nk % 6 == 0:
                        ahead = k + 2 == STEPS
                        new_unit = p * UNITS + steps[nk]["unit"] + 1 + UNITS * ahead
                    halves = list(range(0, steps[nk]["nb"], 4))
                    for n, group in enumerate(st["groups"]):
                        turn(k, group)
                        last_group = n == len(st["groups"]) - 1
                        now = halves if last_group else halves[:-1][:1]
                        halves = halves[len(now):]
                        for half_ in now:
                            if nk % 6 == 0 and half_ == 0:
                                pe.wait_ge(s["q_lo_ok"], new_unit)
                            score(nk, half_, half_ + 4 >= steps[nk]["nb"])
                        if group[0] >= LAG:
                            add_values(*by_number[group[0] - LAG])
                    if k == STEPS - 1:
                        for g in range(GROUPS - LAG, GROUPS):
                            add_values(*by_number[g])
                    for what, j in side[k]:
                        for name, value in reader:
                            pe.wait_ge(s[name], value)
                        if what == "project":
                            if j == UNITS:
                                pe.wait_ge(s["w_split"], p + 2)
                            project(j % UNITS)
                            reader = [("qn_ok", p * UNITS + j + 1)]
                        elif what == "turn_query":
                            pe.wait_ge(s["roped"], p * UNITS + j + 1)
                            turn_query(j % 2)
                            reader = [("q_lo_ok", p * UNITS + j + 1)]
                        elif what == "absorb":
                            pe.wait_ge(s["head_w"], p * 64 + 128)
                            absorb()
                            reader = [("absorbed_sb", p + 2)]
                        elif what == "turn_wo":
                            pe.wait_ge(s["head_v"], p * 64 + 64)
                            for h in range(2):
                                for a in range(KT):
                                    m = pe.transpose(shared[:, h * D + a * P:h * D + (a + 1) * P],
                                                     wo_sb[:, a, h, :], ident[:, :])
                            m.then_inc(s["wo_turned"], 1)
                            reader = [("wo_T_ok", p + 1)]
                        elif what == "value_map":
                            for h in range(2):
                                m = pe.matmul(shared[:, 0:D], wvb[:, h, :], wo_T[:, h, :], start=h == 0, stop=h == 1)
                            m.then_inc(s["gmapped"], 1)
                            reader = [("gmap_sb", p + 1)]
                        elif what == "turn_out":
                            turn_out(j, p * UNITS + j + 2)
                            reader = [("out_T_ok", p * UNITS + j + 2)]
                assert reader[0][0] == "q_lo_ok"

            wide0, wide1 = scores[:, 0], scores[:, 1]
            gate_bank = [turned[:, 0], latent[:, :]]
            up_bank = [turned[:, 1], shared[:, :]]

            def attend(c, between=None):
                for q in range(PAIRS):
                    pe.wait_ge(s["o_lo_ok"], c * PAIRS + q + 1)
                    for a in range(KT):
                        m = three(wide0[:, a * 512:(a + 1) * 512], gmap_hi[:, q, a * P:(a + 1) * P],
                                  gmap_lo[:, q, a * P:(a + 1) * P], o_hi[:, q % 4], o_lo[:, q % 4],
                                  q == 0, q == PAIRS - 1)
                    m.then_inc(s["o_used"], 1)
                    if between:
                        between(q)

            def turn_attended(c):
                pe.wait_ge(s["att_sb"], c + 1)
                for t in range(4):
                    for a in range(KT):
                        m = pe.transpose(wide1[:, t * D + a * P:t * D + (a + 1) * P],
                                         att_T[:, a, t * P:(t + 1) * P], ident[:, :])
                m.then_inc(s["att_back"], 1)

            def turn_tokens(c):
                pe.wait_ge(s["z_ready"], c + 1)
                for k in range(KT):
                    for t in range(4):
                        m = pe.transpose(turned[:, k, t * P:(t + 1) * P],
                                         z[:, t, k * P:(k + 1) * P], ident[:, :])
                m.then_inc(s["z_psum"], 1)

            def gates(c, first, last):
                for t in range(first, last):
                    rows = min(P, HID - t * P)
                    pe.wait_ge(s["h_ok"], c * HT + max(t, 1))
                    for bank, whi, wlo in ((gate_bank, wg_hi, wg_lo), (up_bank, wu_hi, wu_lo)):
                        for k in range(KT):
                            m = three(bank[t % 2][0:rows, :], whi[:, k, t * P:t * P + rows],
                                      wlo[:, k, t * P:t * P + rows], zT_hi[:, k], zT_lo[:, k],
                                      k == 0, k == KT - 1)
                    m.then_inc(s["gate_psum"], 1)

            def down(c, between=None):
                def part(t, units):
                    for u in units:
                        rows = min(P, HID - u * P)
                        cols = slice(t * P, (t + 1) * P)
                        if t == 0:
                            if u < HT - 1:
                                pe.wait_ge(s["h_lo_ok"], c * (HT - 1) + u + 1)
                            else:
                                pe.wait_ge(s["h_tail_ok"], c + 1)
                        m = three(wide1[:, t * D:(t + 1) * D], h_hi[0:rows, u, cols], h_lo[0:rows, u, cols],
                                  wd_hi[0:rows, u], wd_lo[0:rows, u], u == 0, u == HT - 1)
                    return m

                part(0, range(HT - 2))
                part(2, range(HT - 2))
                part(0, range(HT - 2, HT))
                part(2, range(HT - 2, HT))
                part(1, range(HT)).then_inc(s["down_psum"], 1)
                if between:
                    between()
                part(3, range(HT)).then_inc(s["down_psum"], 1)

            pe.wait_ge(s["exped"], PAIRS * STEPS + 1)
            pe.wait_ge(s["maxed"], PAIRS * STEPS + 2)

            def turn_gate_up(n):
                pe.wait_ge(s["wflt_ok"], n + 1)
                if n >= 2:
                    pe.wait_ge(s["fw_lo_ok"], n - 1)
                t0 = n % 3 * 2
                for t in range(2):
                    rows = min(P, HID - (t0 + t) * P)
                    for k in range(KT):
                        m = pe.transpose(turned[:, n % 2, k * 256 + t * P:k * 256 + t * P + rows],
                                         w_flt[0:rows, n % 4, t * D + k * P:t * D + (k + 1) * P],
                                         ident[0:rows, 0:rows])
                m.then_inc(s["fw_psum"], 1)

            def turn_down(n):
                pe.wait_ge(s["wflt_ok"], 8)
                pe.wait_ge(s["fw_lo_ok"], n - 1)
                t0 = (n - 6) * 2
                for t in range(2):
                    cols = min(P, HID - (t0 + t) * P)
                    for a in range(KT):
                        m = pe.transpose(turned[0:cols, n % 2, t * D + a * P:t * D + (a + 1) * P],
                                         w_flt[:, 2 + a, (t0 + t) * P:(t0 + t) * P + cols], ident[:, :])
                m.then_inc(s["fw_psum"], 1)

            attend(0, lambda q: turn_gate_up(q - 1) if 1 <= q <= 6 else None)
            pe.wait_ge(s["q_lo_ok"], PAIRS * UNITS + 2)
            turn_out(UNITS - 1, PAIRS * UNITS + 1)
            turn_attended(0)
            for n in range(6, 9):
                turn_down(n)
            def first_tokens(q):
                if q == 5:
                    pe.wait_ge(s["fw_lo_ok"], 9)
                    turn_tokens(0)

            attend(1, first_tokens)
            pe.wait_ge(s["out_T_ok"], PAIRS * UNITS + 1)

            def chunk(c, more):
                pe.wait_ge(s["zT_lo_ok"], c + 1)
                gates(c, 0, 1)
                pe.wait_ge(s["ffn_ok"], c + 1)
                turn_attended(c + 1)
                gates(c, 1, HT)
                down(c, lambda: turn_tokens(c + 1))
                if more:
                    attend(c + 2)

            with pe.Fori(0, 2) as c:
                chunk(c, True)
            chunk(2, False)
            pe.wait_ge(s["zT_lo_ok"], 4)
            gates(3, 0, HT)
            pe.wait_ge(s["ffn_ok"], 4)
            down(3)

        @block.scalar
        def _(act):
            def copy(dst, src, **kw):
                return act.activation(dst, src, ACT.Copy, **kw)

            act.sem_inc(s["raw_ok"], 1)
            act.wait_ge(s["wkva_psum"], 1)
            copy(wkva_hi[:, :, :].rearrange("p k c -> p (k c)"), shared[:, 0:2 * P]).then_inc(s["wkva_hi_ok"], 1)

            def group(g):
                return slice(g * 512, g * 512 + 512) if isinstance(g, int) else bass.ds(g * 512, 512)

            def high_x(g):
                act.wait_ge(s["xT_psum"], g + 1)
                copy(xT_hi[:, :, group(g)], scores[:, 0].rearrange("p (k s) -> p k s", k=KT))\
                    .then_inc(s["xT_hi_ok"], 1)

            def take_turned_latents(g):
                act.wait_ge(s["kvT_psum"], g + 1)
                copy(kvT, turned[:, 1]).then_inc(s["kvT_sb"], 1)

            def take_latents(g):
                act.wait_ge(s["kv_psum"], g + 1)
                copy(kv_f, latent[:, :].rearrange("p (t c) -> p t c", t=4)).then_inc(s["kv_sb"], 1)

            def high_keys(g):
                act.wait_ge(s["k_psum"], g + 1)
                copy(kT_hi[:, group(g)], turned[:, 0]).then_inc(s["k_hi_ok"], 1)

            high_x(0)
            take_turned_latents(0)
            with act.Fori(0, 3) as g:
                take_latents(g)
                high_x(g + 1)
                take_turned_latents(g + 1)
                high_keys(g)

            def take_queries(slot, n):
                act.wait_ge(s["projected"], n)
                copy(qn[:, slot].rearrange("p a b c -> p (a b c)"), shared[:, :]).then_inc(s["qn_ok"], 1)

            def high_queries(slot, n):
                act.wait_ge(s["q_turned"], n)
                copy(q_hi[:, slot], shared[:, :]).then_inc(s["q_hi_ok"], 1)

            def exponentials(k, n):
                st = steps[k]
                r, part = st["unit"] % 2, st["part"]
                w = st["nb"] * P
                act.wait_ge(s["maxed"], n)
                act.activation(prob[:, k % 2, 0:w], scores[:, k % 2, 0:w], ACT.Exp,
                               bias=negmax[:, r, part:part + 1], accum_out=rowsum[:, r, part:part + 1])\
                    .then_inc(s["exped"], 1)

            def take_turned(pair, j, n):
                act.wait_ge(s["out_turned"], n)
                dst = out_T[:, pair, :].rearrange("p (t s) -> p t s", s=P)[:, j:NT - j:NT - 1 - 2 * j, :]
                copy(dst, shared[:, 0:2 * P].rearrange("p (t s) -> p t s", s=P)).then_inc(s["out_T_ok"], 1)

            take_queries(0, 1)
            take_latents(3)
            high_queries(0, 1)
            take_queries(1, 2)
            exponentials(0, 1)
            high_keys(3)
            high_queries(1, 2)

            with act.Fori(0, PAIRS) as p:
                def take_sums(j):
                    act.wait_ge(s["summed"], p * UNITS + j + 1)
                    copy(raw_out[:, j % 2], latent[:, 0:6 * C].rearrange("p (a c) -> p a c", c=C))\
                        .then_inc(s["raw_ok"], 1)

                for k, st in enumerate(steps):
                    exp_first = len(st["groups"]) > 1
                    for g, b, nb in st["groups"]:
                        if exp_first and g == st["groups"][-1][0]:
                            exponentials((k + 1) % STEPS, p * STEPS + k + 2)
                        act.wait_ge(s["turned_p"], p * GROUPS + g + 1)
                        copy(probT_hi[:, g % SLOTS, 0:nb * P], turned[:, g % 2, 0:nb * P])\
                            .then_inc(s["probT_hi_ok"], 1)
                    if not exp_first:
                        exponentials((k + 1) % STEPS, p * STEPS + k + 2)
                    for what, j in finish[k]:
                        if what != "weigh":
                            continue
                        r = j % 2
                        take_sums(j)
                        act.wait_ge(s["below_ok"], p * UNITS + j + 1)
                        act.activation(weight[:, r].rearrange("p a b -> p (a b)"),
                                       below[:, r].rearrange("p a b -> p (a b)"), ACT.Exp)\
                            .then_inc(s["weight_ok"], 1)
                    for what, j in side[k]:
                        if what == "project":
                            take_queries(j % 2, p * UNITS + j + 1)
                        elif what == "turn_query":
                            high_queries(j % 4, p * UNITS + j + 1)
                        elif what == "turn_wo":
                            act.wait_ge(s["wo_turned"], p + 1)
                            copy(wo_T[:, :, :].rearrange("p h n -> p (h n)"), shared[:, :]).then_inc(s["wo_T_ok"], 1)
                        elif what == "value_map":
                            act.wait_ge(s["gmapped"], p + 2)
                            copy(g_f[:, :], shared[:, 0:D], scale=wcol[:, 0:1]).then_inc(s["gmap_sb"], 1)
                        elif what == "turn_out":
                            pair = p if j >= 0 else (p + PAIRS - 1) % PAIRS
                            take_turned(pair, j % UNITS, p * UNITS + j + 2)

            def high_out(q, tokens, used):
                act.wait_ge(s["o_used"], used)
                copy(o_hi[:, q % 4], tokens).then_inc(s["o_hi_ok"], 1)

            def take_attended(c):
                act.wait_ge(s["o_used"], c * PAIRS + PAIRS + 1)
                copy(att_T[:, :, :].rearrange("p a s -> p (a s)"), scores[:, 0]).then_inc(s["att_sb"], 1)

            def high_tokens(c):
                act.wait_ge(s["z_psum"], c + 1)
                copy(zT_hi[:, :, :], turned[:, :, :]).then_inc(s["zT_hi_ok"], 1)

            def gate(c, t):
                rows = min(P, HID - t * P)
                bank = [turned[:, 0], latent[:, :]][t % 2]
                act.wait_ge(s["gate_psum"], c * HT + t + 1)
                act.activation(tanh_g[0:rows, t % 2], bank[0:rows, :], ACT.Tanh,
                               scale=sgate_half[0:rows, t:t + 1]).then_inc(s["tanh_ok"], 1)

            def high_hidden(c, t):
                rows = min(P, HID - t * P)
                act.wait_ge(s["h_ok"], c * HT + t + 2)
                copy(h_hi[0:rows, t], h_f[0:rows, t % 2]).then_inc(s["h_hi_ok"], 1)

            def high_gate_up(n):
                hi, t0 = (wg_hi, wu_hi)[n // 3], n % 3 * 2
                w = min(2 * P, HID - t0 * P)
                act.wait_ge(s["fw_psum"], n + 1)
                copy(hi[:, :, t0 * P:t0 * P + w],
                     turned[:, n % 2].rearrange("p (k c) -> p k c", k=KT)[:, :, 0:w]).then_inc(s["fw_hi_ok"], 1)

            def high_down(n):
                t0 = (n - 6) * 2
                act.wait_ge(s["fw_psum"], n + 1)
                for t, rows in ((t0, P), (t0 + 1, min(P, HID - (t0 + 1) * P))):
                    m = copy(wd_hi[0:rows, t], turned[0:rows, n % 2, (t - t0) * D:(t - t0 + 1) * D])
                m.then_inc(s["fw_hi_ok"], 1)

            for q in range(PAIRS):
                high_out(q, out_T[:, q, 0:512], max(q - 2, 1))
                if q >= 4:
                    high_gate_up(q - 4)
            for n in range(4, 6):
                high_gate_up(n)
            take_attended(0)
            take_turned(PAIRS - 1, UNITS - 1, PAIRS * UNITS + 1)

            def high_outs(c, pairs):
                tokens = slice(c * 512, c * 512 + 512) if isinstance(c, int) else bass.ds(c * 512, 512)
                for q in pairs:
                    high_out(q, out_T[:, q, tokens], c * PAIRS + q - 2)

            high_outs(1, range(2))
            for n in range(6, 9):
                high_down(n)
            high_outs(1, range(2, PAIRS))
            high_tokens(0)
            take_attended(1)

            def chunk(c, more):
                gate(c, 0)
                for t in range(HT):
                    if t + 1 < HT:
                        gate(c, t + 1)
                    high_hidden(c, t)
                high_outs(c + 2, range(4 * more))
                high_tokens(c + 1)
                if more:
                    high_outs(c + 2, range(4, PAIRS))
                    take_attended(c + 2)

            with act.Fori(0, 2) as c:
                chunk(c, True)
            chunk(2, False)
            gate(3, 0)
            for t in range(HT):
                if t + 1 < HT:
                    gate(3, t + 1)
                high_hidden(3, t)

        @block.vector
        def _(dve):
            for name in ("ffn_ok", "h_ok", "result_free"):
                dve.sem_inc(s[name], 1)
            x_all = out_T[:, PAIRS - 2:PAIRS, :].rearrange("p a (g d) -> p (a g) d", d=D)

            def setup_link(n):
                def link(ins):
                    link.count += 1
                    ins.then_inc(s["dve_setup"], 1)
                    dve.wait_ge(s["dve_setup"], n + link.count)
                link.count = 0
                return link

            def four_tiles(g):
                return slice(4 * g, 4 * g + 4) if isinstance(g, int) else bass.ds(g * 4, 4)

            def group(g):
                return slice(g * 512, g * 512 + 512) if isinstance(g, int) else bass.ds(g * 512, 512)

            def token_variances(g, link):
                dve.wait_ge(s["x_in_s"], g * 16 + 16)
                xs = x_all[:, four_tiles(g), :]
                for t in range(4):
                    m = dve.bn_stats(stats[:, t, :], xs[:, t, :])
                link(m)
                dve.memset(pause[:, :], 0.0)
                for t in range(4):
                    m = dve.bn_aggr(meanvar[:, t, :], stats[:, t, :])
                link(m)
                dve.tensor_scalar(vareps[:, :], meanvar[:, :, 1], EPS_LN, None, ALU.add).then_inc(s["var_ready"], 1)

            def normalise_tokens(g):
                dve.wait_ge(s["rstd_ready"], g + 1)
                xs = x_all[:, four_tiles(g), :]
                for t in range(4):
                    m = dve.tensor_scalar(xn[:, t, :], xs[:, t, :], meanvar[:, t, 0:1], rstd[:, t:t + 1],
                                          ALU.subtract, ALU.mult)
                m.then_inc(s["xn_ready"], 1)

            def low_x(g):
                dve.wait_ge(s["xT_hi_ok"], g + 1)
                dve.tensor_tensor(xT_lo[:, :, group(g)], scores[:, 0].rearrange("p (k s) -> p k s", k=KT),
                                  xT_hi[:, :, group(g)].bitcast(F32), ALU.subtract).then_inc(s["xT_lo_ok"], 1)

            def latent_squares(g, link):
                dve.wait_ge(s["kv_sb"], g + 1)
                dve.tensor_copy(keys[:, :, C:P], kv_f[:, :, C:P]).then_inc(s["keys_ok"], 1)
                link(dve.tensor_tensor(square[:, :, :], kv_f[:, :, 0:C], kv_f[:, :, 0:C], ALU.mult))
                link(dve.tensor_reduce(latent_ms[:, :], square[:, :, :], AX.X, ALU.add))
                dve.tensor_scalar(latent_ms[:, :], latent_ms[:, :], 1.0 / C, EPS_RMS, ALU.mult, ALU.add)\
                    .then_inc(s["ms_ready"], 1)

            def values(g, link):
                dve.wait_ge(s["rms_ready"], g + 1)
                link(dve.tensor_tensor(keys[:, :, 0:C], kv_f[:, :, 0:C],
                                       latent_rms[:, :, None].to_broadcast([P, 4, C]), ALU.mult))
                link(dve.tensor_copy(v_hi[:, four_tiles(g), :], keys[:, :, 0:C]))
                dve.tensor_tensor(v_lo[:, four_tiles(g), :], keys[:, :, 0:C],
                                  v_hi[:, four_tiles(g), :], ALU.subtract).then_inc(s["values_ok"], 1)

            def low_keys(g):
                dve.wait_ge(s["k_hi_ok"], g + 1)
                dve.tensor_tensor(kT_lo[:, group(g)], turned[:, 0], kT_hi[:, group(g)].bitcast(F32), ALU.subtract)\
                    .then_inc(s["k_lo_ok"], 1)

            def take_absorbed(n):
                dve.wait_ge(s["absorbed"], n)
                dve.tensor_tensor(w_f[:, :, :, :].rearrange("p k t c -> p (k t) c"),
                                  shared[:, :].rearrange("p (a c) -> p a c", c=P),
                                  wscale[:, None, :].to_broadcast([P, 2 * KT, P]), ALU.mult)\
                    .then_inc(s["absorbed_sb"], 1)

            token_variances(0, setup_link(0))
            dve.wait_ge(s["wkva_hi_ok"], 1)
            dve.tensor_tensor(wkva_lo[:, :, :].rearrange("p k c -> p (k c)"), shared[:, 0:2 * P],
                              wkva_hi[:, :, :].rearrange("p k c -> p (k c)").bitcast(F32), ALU.subtract)\
                .then_inc(s["wkva_lo_ok"], 1)
            dve.wait_ge(s["const_in"], 48)
            dve.wait_ge(s["ones_ok"], 3)
            dve.tensor_scalar(wscale[:, :], wscale[:, :], SCALE, None, ALU.mult).then_inc(s["wscale_ok"], 1)
            normalise_tokens(0)
            low_x(0)
            dve.wait_ge(s["wscale_ok"], 1)
            take_absorbed(1)
            token_variances(1, setup_link(2))
            normalise_tokens(1)
            with dve.Fori(0, 2) as g:
                link = setup_link(g * 6 + 4)
                latent_squares(g, link)
                low_x(g + 1)
                values(g, link)
                token_variances(g + 2, link)
                normalise_tokens(g + 2)
                low_keys(g)
                assert link.count == 6
            link = setup_link(16)
            latent_squares(2, link)
            low_x(3)
            values(2, link)
            low_keys(2)
            latent_squares(3, link)

            def low_queries(slot, n):
                dve.wait_ge(s["q_hi_ok"], n)
                dve.tensor_tensor(q_lo[:, slot], shared[:, :], q_hi[:, slot].bitcast(F32), ALU.subtract)\
                    .then_inc(s["q_lo_ok"], 1)

            def first_maxima(k, pair):
                if SPLIT[k]:
                    dve.wait_ge(s["half_scored"], pair * SPLITS + splits(k))
                    dve.tensor_reduce(halfmax[:, k % 2, 0:1], scores[:, k % 2, 0:512], AX.X, ALU.max, negate=True)

            def maxima(k, pair):
                st = steps[k]
                dst = negmax[:, st["unit"] % 2, st["part"]:st["part"] + 1]
                dve.wait_ge(s["scored"], pair * STEPS + k + 1)
                if SPLIT[k]:
                    dve.tensor_reduce(halfmax[:, k % 2, 1:2], scores[:, k % 2, 512:st["nb"] * P], AX.X, ALU.max,
                                      negate=True).then_inc(s["half_maxed"], 1)
                    dve.wait_ge(s["half_maxed"], pair * SPLITS + splits(k))
                    dve.tensor_tensor(dst, halfmax[:, k % 2, 0:1], halfmax[:, k % 2, 1:2], ALU.min)\
                        .then_inc(s["maxed"], 1)
                else:
                    dve.tensor_reduce(dst, scores[:, k % 2, 0:st["nb"] * P], AX.X, ALU.max, negate=True)\
                        .then_inc(s["maxed"], 1)

            low_queries(0, 1)
            values(3, link)
            first_maxima(0, 0)
            maxima(0, 0)
            maxima(1, 0)
            low_keys(3)
            low_queries(1, 2)

            with dve.Fori(0, PAIRS) as p:
                for k, st in enumerate(steps):
                    nk, pair = (k + 2) % STEPS, p + (k + 2) // STEPS
                    many = len(st["groups"]) > 1
                    for g, b, nb in st["groups"]:
                        last = g == st["groups"][-1][0]
                        if last and many:
                            first_maxima(nk, pair)
                        if last and k % 3 == 0:
                            maxima(nk, pair)
                        dve.wait_ge(s["probT_hi_ok"], p * GROUPS + g + 1)
                        dve.tensor_tensor(probT_lo[:, g % SLOTS, 0:nb * P], turned[:, g % 2, 0:nb * P],
                                          probT_hi[:, g % SLOTS, 0:nb * P], ALU.subtract).then_inc(s["probT_lo_ok"], 1)
                    if not many:
                        first_maxima(nk, pair)
                    if k % 3:
                        maxima(nk, pair)
                    for what, j in finish[k]:
                        r = j % 2
                        if what == "least":
                            dve.wait_ge(s["maxed"], p * STEPS + 6 * j + 6)
                            both = negmax[:, r, 0:4].rearrange("p (a b) -> p a b", b=2)
                            dve.tensor_tensor(negall[:, r], both[:, :, 0], both[:, :, 1], ALU.min)\
                                .then_inc(s["least_ok"], 1)
                        elif what == "scale":
                            dve.wait_ge(s["exped"], p * STEPS + 6 * j + 6)
                            dve.reciprocal(inverse[:, r, 2:4], rowsum[:, r, 4:6])
                            dve.wait_ge(s["total_ok"], p * UNITS + j + 1)
                            dve.reciprocal(inverse[:, r, 0:2], total[:, r]).then_inc(s["inverse_ok"], 1)
                    for what, j in side[k]:
                        if what == "turn_query":
                            low_queries(j % 4, p * UNITS + j + 1)
                        elif what == "absorb":
                            take_absorbed(p + 2)

            def to_float(n):
                dve.wait_ge(s[f"wint_in{n % 4}"], 32 if n < 4 else 64 if n < 6 else 48)
                if n >= 4:
                    dve.wait_ge(s["fw_psum"], n - 3)
                parts = [(P, 0, HID)] if n >= 6 else [(P, 0, D), (HTAIL, D, 2 * D)] if n % 3 == 2 else [(P, 0, 2 * D)]
                for rows, c0, c1 in parts:
                    m = dve.tensor_scalar(w_flt[0:rows, n % 4, c0:c1], w_int[0:rows, n % 4, c0:c1],
                                          -ZERO_POINT, None, ALU.add)
                m.then_inc(s["wflt_ok"], 1)

            def low_up_gate(n):
                w = min(2 * P, HID - (n % 3) * 2 * P)
                lo, hi = ((wg_lo, wg_hi), (wu_lo, wu_hi))[n // 3]
                c0 = (n % 3) * 2 * P
                dve.wait_ge(s["fw_hi_ok"], n + 1)
                dve.tensor_tensor(lo[:, :, c0:c0 + w],
                                  turned[:, n % 2].rearrange("p (k c) -> p k c", k=KT)[:, :, 0:w],
                                  hi[:, :, c0:c0 + w].bitcast(F32), ALU.subtract).then_inc(s["fw_lo_ok"], 1)

            def low_down(n):
                t0 = (n - 6) * 2
                dve.wait_ge(s["fw_hi_ok"], n + 1)
                for t in (t0, t0 + 1):
                    rows = min(P, HID - t * P)
                    m = dve.tensor_tensor(wd_lo[0:rows, t], turned[0:rows, n % 2, (t - t0) * D:(t - t0 + 1) * D],
                                          wd_hi[0:rows, t].bitcast(F32), ALU.subtract)
                m.then_inc(s["fw_lo_ok"], 1)

            def tiles_of(c, t0, n):
                if isinstance(c, int):
                    return y1[:, (c % 2) * 4 + t0:(c % 2) * 4 + t0 + n, :]
                return y1[:, bass.ds((c % 2) * 4 + t0, n), :]

            def variances(src, n, st, mv, var, done, link):
                for t in range(n):
                    m = dve.bn_stats(st[:, t, :], src[:, t, :])
                link(m)
                dve.memset(pause[:, :], 0.0)
                for t in range(n):
                    m = dve.bn_aggr(mv[:, t, :], st[:, t, :])
                link(m)
                dve.tensor_scalar(var, mv[:, :, 1], EPS_LN, None, ALU.add).then_inc(s[done], 1)

            def normalise(dst, src, n, mv, rstd_):
                for t in range(n):
                    m = dve.tensor_scalar(dst[:, t, :], src[:, t, :], mv[:, t, 0:1], rstd_[:, t:t + 1],
                                          ALU.subtract, ALU.mult)
                return m

            attended = scores[:, 1].rearrange("p (t d) -> p t d", d=D)

            def first_variances(c, link):
                dve.wait_ge(s["att_back"], c + 1)
                variances(attended, 4, lstats[:, :, :], lmv[:, :, :], lvar[:, :], "ln_var", link)

            def first_norm(c):
                dve.wait_ge(s["ln_rstd"], c * 2 + 1)
                normalise(z[:, :, :], attended, 4, lmv, lrstd).then_inc(s["z1_ok"], 1)

            def second_variances(c, link):
                dve.wait_ge(s["y1_ok"], c + 1)
                variances(tiles_of(c, 0, 4), 4, lstats[:, :, :], lmv[:, :, :], lvar[:, :], "ln_var", link)

            def second_norm(c):
                dve.wait_ge(s["ln_rstd"], c * 2 + 2)
                normalise(z[:, :, :], tiles_of(c, 0, 4), 4, lmv, lrstd).then_inc(s["z_ready"], 1)

            def low_tokens(c):
                dve.wait_ge(s["zT_hi_ok"], c + 1)
                dve.tensor_tensor(zT_lo[:, :, :], turned[:, :, :], zT_hi[:, :, :].bitcast(F32), ALU.subtract)\
                    .then_inc(s["zT_lo_ok"], 1)

            def hidden(c, t):
                rows = min(P, HID - t * P)
                gate_ps = [turned[:, 0], latent[:, :]][t % 2]
                up_ps = [turned[:, 1], shared[:, :]][t % 2]
                dve.wait_ge(s["tanh_ok"], c * HT + t + 1)
                dve.scalar_tensor_tensor(gated[0:rows, t % 2], tanh_g[0:rows, t % 2], 1.0, gate_ps[0:rows, :],
                                         ALU.add, ALU.mult).then_inc(s["gated_ok"], 1)
                dve.wait_ge(s["gated_ok"], c * HT + t + 1)
                if t >= 2:
                    dve.wait_ge(s["h_lo_ok"], c * (HT - 1) + t - 1)
                dve.scalar_tensor_tensor(h_f[0:rows, t % 2], up_ps[0:rows, :], sgu[0:rows, t:t + 1],
                                         gated[0:rows, t % 2], ALU.mult, ALU.mult).then_inc(s["h_ok"], 1)

            def low_tail(c):
                dve.wait_ge(s["h_hi_ok"], c * HT + HT)
                dve.tensor_tensor(h_lo[0:HTAIL, HT - 1], h_f[0:HTAIL, (HT - 1) % 2],
                                  h_hi[0:HTAIL, HT - 1].bitcast(F32), ALU.subtract).then_inc(s["h_tail_ok"], 1)

            def finish_chunk(c, link, between=None):
                dve.wait_ge(s["result_free"], c + 1)
                for half_ in range(2):
                    two = slice(2 * half_, 2 * half_ + 2)
                    dve.wait_ge(s["down_psum"], c * 2 + half_ + 1)
                    link(dve.tensor_tensor(result[:, two], attended[:, two],
                                           sdown[:, None, :].to_broadcast([P, 2, D]), ALU.mult))
                    if half_:
                        dve.sem_inc(s["ffn_ok"], 1)
                    variances(result[:, two], 2, fstats[:, two], fmv[:, two], fvar[:, two], "ffn_var", link)
                if between:
                    between()
                for half_ in range(2):
                    two = slice(2 * half_, 2 * half_ + 2)
                    dve.wait_ge(s["ffn_rstd"], c * 2 + half_ + 1)
                    link(normalise(result[:, two], result[:, two], 2, fmv[:, two], frstd[:, two]))
                    dve.tensor_tensor(result[:, two], result[:, two], tiles_of(c, 2 * half_, 2), ALU.add)\
                        .then_inc(s["result_ok"], 1)

            late_count = [0]

            def late_link(ins):
                late_count[0] += 1
                ins.then_inc(s["dve_late"], 1)
                dve.wait_ge(s["dve_late"], late_count[0])

            for q in range(PAIRS):
                dve.wait_ge(s["o_hi_ok"], q + 1)
                dve.tensor_tensor(o_lo[:, q % 4], out_T[:, q, 0:512], o_hi[:, q % 4].bitcast(F32), ALU.subtract)\
                    .then_inc(s["o_lo_ok"], 1)
                if q >= 3:
                    to_float(q - 3)
                if q >= 4:
                    low_up_gate(q - 4)
            to_float(5)
            for n in range(4, 6):
                low_up_gate(n)
                to_float(n + 2)
            dve.wait_ge(s["scales_in"], 80)
            for half_, full in ((sgate_half, sgate), (sup_half, sup)):
                dve.tensor_scalar(half_[:, 0:HT - 1], full[:, 0:HT - 1], 0.5, None, ALU.mult)
                m = dve.tensor_scalar(half_[0:HTAIL, HT - 1:HT], full[0:HTAIL, HT - 1:HT], 0.5, None, ALU.mult)
            m.then_inc(s["scales_chain"], 1)
            dve.wait_ge(s["scales_chain"], 1)
            dve.tensor_tensor(sgu[:, 0:HT - 1], sgate[:, 0:HT - 1], sup_half[:, 0:HT - 1], ALU.mult)
            dve.tensor_tensor(sgu[0:HTAIL, HT - 1:HT], sgate[0:HTAIL, HT - 1:HT], sup_half[0:HTAIL, HT - 1:HT],
                              ALU.mult).then_inc(s["scales_chain"], 1)
            dve.wait_ge(s["scales_chain"], 2)
            first_variances(0, late_link)
            low_down(6)
            low_down(7)
            first_norm(0)
            dve.wait_ge(s["z1_ok"], 1)
            dve.wait_ge(s["xres_in"], 16)
            dve.tensor_tensor(y1[:, 0:4, :], z[:, :, :], x_res[:, :, :], ALU.add).then_inc(s["y1_ok"], 1)
            second_variances(0, late_link)
            low_down(8)
            second_norm(0)
            low_tokens(0)
            BEFORE = late_count[0]
            PER_LATE = 4 + 8

            def chunk(c, between=None):
                count = [0]

                def link(ins):
                    count[0] += 1
                    ins.then_inc(s["dve_late"], 1)
                    dve.wait_ge(s["dve_late"], c * PER_LATE + BEFORE + count[0])

                hidden(c, 0)
                first_variances(c + 1, link)
                hidden(c, 1)
                first_norm(c + 1)
                hidden(c, 2)
                hidden(c, 3)
                second_variances(c + 1, link)
                hidden(c, 4)
                hidden(c, 5)
                low_tail(c)
                second_norm(c + 1)
                low_tokens(c + 1)
                finish_chunk(c, link, between)
                assert count[0] == PER_LATE, count

            with dve.Fori(0, 2) as c:
                chunk(c)
            chunk(2, lambda: hidden(3, 0))
            late_count[0] = BEFORE + 3 * PER_LATE
            for t in range(1, HT):
                hidden(3, t)
            low_tail(3)
            finish_chunk(3, late_link)


_INS = ["L0_attn_x", "L0_attn_wq", "L0_attn_wkv_a", "L0_attn_wkv_b", "L0_attn_wo", "L0_attn_kv_norm_w",
        "L0_ffn_wq_gate", "L0_ffn_s_gate", "L0_ffn_wq_up", "L0_ffn_s_up", "L0_ffn_wq_down", "L0_ffn_s_down"]


def kernel(**inputs):
    import concourse.bacc as bacc
    from concourse.bass_utils import run_bass_kernel_spmd

    nc = bacc.Bacc("TRN2", target_bir_lowering=False, num_devices=1)
    arrays = {name: np.ascontiguousarray(inputs[name]) for name in _INS}
    freqs = 1.0 / THETA ** (np.arange(0, ROPE, 2, dtype=np.float32) / ROPE)
    angles = np.outer(np.arange(S, dtype=np.float32), freqs)
    arrays["cos_table"] = np.cos(angles).astype(np.float32)
    arrays["sin_table"] = np.sin(angles).astype(np.float32)
    args = [nc.dram_tensor(name, a.shape, mybir.dt.from_np(a.dtype), kind="ExternalInput").ap()
            for name, a in arrays.items()]
    out = nc.dram_tensor("out", (1, S, D), F32, kind="ExternalOutput").ap()
    build(nc, *args, out)
    r = run_bass_kernel_spmd(nc, [arrays], core_ids=[0])
    return r.results[0]["out"]
```
